# Optimizing a Trainium2 kernel written in Bass

```python
import numpy as np
import jax
import jax.numpy as jnp

def _softmax(x, axis=-1):
    return jax.nn.softmax(x, axis=axis)

def _gelu(x):
    return jax.nn.gelu(x, approximate=True)

def _silu(x):
    return jax.nn.silu(x)

def _sigmoid(x):
    return jax.nn.sigmoid(x)

def _layernorm(x, axis=-1, eps=1e-05):
    m = jnp.mean(x, axis=axis, keepdims=True)
    v = jnp.var(x, axis=axis, keepdims=True)
    return (x - m) / jnp.sqrt(v + eps)

def _scatter_add(tgt, idx, src, axis=0):
    return tgt.at[idx].add(src)

def _segment_sum(src, seg, n):
    return jax.ops.segment_sum(src, seg, n)
kernel_name = 'mk_adj_resnorm_d2_adj_r2_be4c98'

def setup_inputs(seed: int=0):
    np.random.seed(seed)
    _w = jnp.asarray

    def _rec_inputs():
        import jax
        import jax.numpy as jnp
        _gk = jax.random.key(seed)
        x = 7.22e-05 + 1 * jax.random.normal(jax.random.fold_in(_gk, 1), (64, 128, 512), jnp.float32)
        _w = (1.0 + jnp.arange(128, dtype=jnp.float32)) ** (-0.5)
        _w = _w / _w.mean()
        _pij = jnp.clip(0.03125 * _w[:, None] * _w[None, :], 0.0, 1.0)
        _a = jax.random.uniform(jax.random.fold_in(_gk, 2), (128, 128)) < _pij
        _a = jnp.logical_or(_a, jnp.swapaxes(_a, -1, -2))
        _a = jnp.logical_or(_a, jnp.eye(128, dtype=bool))
        _af = _a.astype(jnp.float32)
        _af = _af * jax.random.uniform(jax.random.fold_in(_gk, 3), (128, 128), jnp.float32, 0.05, 0.108252)
        adj = _af
        return (x, adj)
    x, adj = _rec_inputs()

    def _L0_gnn_setup():
        import jax, jax.numpy as jnp
        import numpy as np

        def _ada_gcn(xn, weight, bias):
            N, B, L = xn.shape
            x_norm = xn / jnp.maximum(jnp.linalg.norm(xn, axis=-1, keepdims=True), 1e-12)
            mean_sim = jnp.einsum('nbl,mbl->nm', x_norm, x_norm) / B
            k = max(int(N * 0.3), 1)
            _, idx = jax.lax.top_k(mean_sim, k + 1)
            rows = jnp.arange(N)[:, None]
            non_self = idx != rows
            order = jnp.cumsum(non_self.astype(jnp.int32), axis=1) - 1
            keep = non_self & (order < k)
            mask = jnp.zeros((N, N), dtype=bool).at[jnp.broadcast_to(rows, idx.shape), idx].set(keep)
            A = jnp.where(mask, mean_sim, jnp.zeros((), mean_sim.dtype))
            deg = A.sum(axis=0)
            dinv = jnp.where(deg > 0, jax.lax.rsqrt(deg), jnp.zeros((), deg.dtype))
            An = dinv[:, None] * A * dinv[None, :]
            xw = jnp.einsum('nbl,lo->nbo', xn, weight)
            out = jnp.einsum('sd,sbl->dbl', An, xw) + bias
            return out
        key = jax.random.key(seed)
        k1, k2 = jax.random.split(key)
        B, L, N = (32, 128, 512)
        x = jax.random.normal(k1, (B, L, N), dtype=jnp.float32)
        limit = float(np.sqrt(6.0 / (L + L)))
        weight = jax.random.uniform(k2, (L, L), dtype=jnp.float32, minval=-limit, maxval=limit)
        bias = jnp.zeros((L,), dtype=jnp.float32)
        return {'x': x, 'weight': weight, 'bias': bias}
    _L0_gnn_all = _L0_gnn_setup()
    _L0_gnn_in = {k: v for k, v in _L0_gnn_all.items() if k in ('bias',)}
    del _L0_gnn_all

    def _L1_gnn_setup():
        import jax, jax.numpy as jnp
        import numpy as np
        EPS = 1e-08

        def _row_stochastic_causal(A, causal_mask):
            A = A * causal_mask
            deg = jnp.maximum(A.sum(axis=-1, keepdims=True), EPS)
            return A / deg
        key = jax.random.key(seed)
        k = jax.random.split(key, 5)
        B, N, D = (4, 1024, 512)
        s = 1.0 / np.sqrt(D)
        h = jax.random.normal(k[0], (B, N, D), dtype=jnp.float32)
        W_lang = jax.random.normal(k[1], (D, D), dtype=jnp.float32) * s
        W_grav = jax.random.normal(k[2], (D, D), dtype=jnp.float32) * s
        W_V = jax.random.normal(k[3], (D, D), dtype=jnp.float32) * s
        W_O = jax.random.normal(k[4], (D, D), dtype=jnp.float32) * s
        causal_mask = jnp.tril(jnp.ones((N, N), dtype=jnp.float32))
        gate_logit = jnp.zeros((), jnp.float32)
        log_sigma = jnp.zeros((), jnp.float32)
        return {'h': h, 'causal_mask': causal_mask, 'W_lang': W_lang, 'W_grav': W_grav, 'W_V': W_V, 'W_O': W_O, 'gate_logit': gate_logit, 'log_sigma': log_sigma}
    _L1_gnn_all = _L1_gnn_setup()
    _L1_gnn_in = {k: v for k, v in _L1_gnn_all.items() if k in ('W_lang', 'W_grav', 'W_V', 'W_O', 'gate_logit', 'log_sigma')}
    del _L1_gnn_all
    return {'x': x, 'adj': adj, 'L0_gnn_bias': _L0_gnn_in['bias'], 'L1_gnn_W_lang': _L1_gnn_in['W_lang'], 'L1_gnn_W_grav': _L1_gnn_in['W_grav'], 'L1_gnn_W_V': _L1_gnn_in['W_V'], 'L1_gnn_W_O': _L1_gnn_in['W_O'], 'L1_gnn_gate_logit': _L1_gnn_in['gate_logit'], 'L1_gnn_log_sigma': _L1_gnn_in['log_sigma']}

def reference(x, adj, L0_gnn_bias, L1_gnn_W_lang, L1_gnn_W_grav, L1_gnn_W_V, L1_gnn_W_O, L1_gnn_gate_logit, L1_gnn_log_sigma):
    import jax
    import jax.numpy as jnp

    def _L0_gnn_ref(x, weight, bias):
        import jax, jax.numpy as jnp
        import numpy as np

        def _ada_gcn(xn, weight, bias):
            N, B, L = xn.shape
            x_norm = xn / jnp.maximum(jnp.linalg.norm(xn, axis=-1, keepdims=True), 1e-12)
            mean_sim = jnp.einsum('nbl,mbl->nm', x_norm, x_norm) / B
            k = max(int(N * 0.3), 1)
            _, idx = jax.lax.top_k(mean_sim, k + 1)
            rows = jnp.arange(N)[:, None]
            non_self = idx != rows
            order = jnp.cumsum(non_self.astype(jnp.int32), axis=1) - 1
            keep = non_self & (order < k)
            mask = jnp.zeros((N, N), dtype=bool).at[jnp.broadcast_to(rows, idx.shape), idx].set(keep)
            A = jnp.where(mask, mean_sim, jnp.zeros((), mean_sim.dtype))
            deg = A.sum(axis=0)
            dinv = jnp.where(deg > 0, jax.lax.rsqrt(deg), jnp.zeros((), deg.dtype))
            An = dinv[:, None] * A * dinv[None, :]
            xw = jnp.einsum('nbl,lo->nbo', xn, weight)
            out = jnp.einsum('sd,sbl->dbl', An, xw) + bias
            return out
        xn = jnp.transpose(x, (2, 0, 1))
        num_levels = 1
        for _ in range(num_levels):
            xn = _ada_gcn(xn, weight, bias)
        return jnp.transpose(xn, (1, 2, 0))

    def _L1_gnn_ref(h, causal_mask, W_lang, W_grav, W_V, W_O, gate_logit, log_sigma):
        import jax, jax.numpy as jnp
        import numpy as np
        EPS = 1e-08

        def _row_stochastic_causal(A, causal_mask):
            A = A * causal_mask
            deg = jnp.maximum(A.sum(axis=-1, keepdims=True), EPS)
            return A / deg
        z_l = jnp.einsum('bnd,ed->bne', h, W_lang)
        z_g = jnp.einsum('bnd,ed->bne', h, W_grav)
        v = jnp.einsum('bnd,ed->bne', h, W_V)
        N = h.shape[-2]
        not_eye = 1.0 - jnp.eye(N, dtype=h.dtype)
        zn = z_l / jnp.maximum(jnp.linalg.norm(z_l, axis=-1, keepdims=True), EPS)
        A_l = jnp.maximum(jnp.einsum('bnd,bmd->bnm', zn, zn), 0.0) * not_eye
        sq = jnp.sum(z_g * z_g, axis=-1, keepdims=True)
        d2 = jnp.maximum(sq + jnp.swapaxes(sq, -1, -2) - 2.0 * jnp.einsum('bnd,bmd->bnm', z_g, z_g), 0.0)
        sigma = jnp.exp(log_sigma)
        A_g = jnp.exp(-d2 / (2.0 * sigma * sigma)) * not_eye
        K_l = _row_stochastic_causal(A_l, causal_mask)
        K_g = _row_stochastic_causal(A_g, causal_mask)
        w_l = jax.nn.sigmoid(gate_logit)
        K = w_l * K_l + (1.0 - w_l) * K_g
        out = jnp.einsum('bnm,bmd->bnd', K, v)
        return jnp.einsum('bnd,ed->bne', out, W_O)
    x = _layernorm(x + _L0_gnn_ref(x, adj, L0_gnn_bias), axis=-1)
    x = _layernorm(x + _L1_gnn_ref(x, adj, L1_gnn_W_lang, L1_gnn_W_grav, L1_gnn_W_V, L1_gnn_W_O, L1_gnn_gate_logit, L1_gnn_log_sigma), axis=-1)
    return x

_drawn_inputs = setup_inputs


def setup_inputs(seed=0):
    import zlib

    import numpy as np

    out = dict(_drawn_inputs(seed))
    spreads = {'L0_gnn_bias': (0.0, 0.1)}
    factors = {}
    for name, (base, spread) in spreads.items():
        noise = np.random.default_rng([zlib.crc32(name.encode()), seed]).standard_normal(out[name].shape)
        drawn = base * np.exp(spread * noise) if base else spread * noise
        out[name] = jnp.asarray(drawn.astype(out[name].dtype))
    for name, factor in factors.items():
        out[name] = (out[name] * factor).astype(out[name].dtype)
    return out
```

```python
from contextlib import ExitStack

import concourse.bass as bass
from concourse import mybir

F32 = mybir.dt.float32
F16 = mybir.dt.float16
I32 = mybir.dt.int32
ALU = mybir.AluOpType
ACT = mybir.ActivationFunctionType
AX = mybir.AxisListType
ABSMAX = bass.bass_isa.ReduceOp.absmax

P = 128
EXPONENT = 0x7F800000


def wait(eng, sem, value):
    if not isinstance(value, int) or value > 0:
        eng.wait_ge(sem, value)


def build(nc, x, adj, bias, wlT, wgT, wv, woT, gate, log_sigma, out):
    B, L, NODES = x.shape
    assert L == P and NODES % P == 0
    KB = NODES // P
    GB = 4
    NG = B // GB
    K_NEAR = max(int(NODES * 0.3), 1)
    ROUNDS = K_NEAR // 8
    LAST = K_NEAR % 8
    CB = 8
    NC = B // CB
    LG = P // CB
    CL = L // LG
    assert NG % 2 == 0 and NG >= 4 and NC >= 3 and NC % 2 == 0 and LAST > 0
    N4 = GB * P

    X_HAT = 2.0 ** 12
    S_SCALE = 1.0 / (X_HAT * X_HAT * B)
    X_UP, W_UP, A_UP, H_UP, K_UP = 2.0 ** 13, 2.0 ** 10, 2.0 ** 12, 2.0 ** 8, 2.0 ** 14
    XW_DOWN, Z_DOWN, VO_DOWN, V_DOWN = 2.0 ** -14, 2.0 ** -13, 2.0 ** -16, 2.0 ** -17
    ALPHA = 1.0 / (X_UP * W_UP * XW_DOWN * A_UP)
    Z_UNIT = 1.0 / (H_UP * W_UP * Z_DOWN)
    BETA = 1.0 / (H_UP * W_UP * W_UP * VO_DOWN * V_DOWN * K_UP)
    TAKEN, SELF, PAD = -1e30, -2e30, -3e30
    NORM_EPS, LN_EPS, ROW_EPS = 1e-12, 1e-5, 1e-8

    x_chunk = x.rearrange("(c b) (g l) n -> c (b g) l n", b=CB, g=LG)
    x_group = x.rearrange("(g b) l n -> g l b n", b=GB)
    out_group = out.rearrange("(g b) l n -> g l b n", b=GB)

    with ExitStack() as ctx:
        def sb(name, shape, dt=F32):
            return ctx.enter_context(nc.sbuf_tensor(name, shape, dt))

        def sem(name):
            return ctx.enter_context(nc.semaphore(name))

        bank = [ctx.enter_context(nc.psum_tensor(f"bank{i}", [P, 512], F32)) for i in range(8)]

        ident = sb("ident", [P, P])
        ones = sb("ones", [P, P])
        minus_half = sb("minus_half", [P, P])
        same_item = sb("same_item", [P, P])
        self_mark = sb("self_mark", [P, P])
        mask = sb("mask", [P, P])
        adj_sb = sb("adj_sb", [P, P])
        adj_h = sb("adj_h", [P, P], F16)
        adj_l = sb("adj_l", [P, P], F16)
        bias_c = sb("bias_c", [P, 1])
        gate_c = sb("gate_c", [P, 1])
        ls_c = sb("ls_c", [P, 1])
        chunk_max = sb("chunk_max", [P, NC])
        magn = sb("magn", [P, 8])
        magn_all = sb("magn_all", [P, 8])
        pw = sb("pw", [P, 8])
        ipw = sb("ipw", [P, 8])
        up = sb("up", [P, 8])
        col = sb("col", [P, 16])
        D_MAX, D_POW, D_INV, ALPHA_C, CAP_C, KAPPA, W_L, W_G, BETA_C, T0, T1, HK = range(12)
        c1 = lambda i: col[:, i:i + 1]
        dinv_col = sb("dinv_col", [P, KB])
        top8 = sb("top8", [P, KB, 8])
        stats = sb("stats", [P, GB, 6])
        stats2 = sb("stats2", [P, GB, 6])
        mv = sb("mv", [P, GB, 2])
        mv2 = sb("mv2", [P, GB, 2])
        ln1 = sb("ln1", [P, 5, GB])
        ln2 = sb("ln2", [P, 5, GB])
        nl = sb("nl", [P, 6, GB])
        cf = sb("cf", [P, 8, GB])

        KIB = 1024
        arena = sb("arena", [P, 198 * KIB // 4])

        def at(start, free, dt=F32):
            size = (2 if dt == F16 else 4)
            n = 1
            for d in free:
                n *= d
            flat = arena[:, start // 4:(start + n * size) // 4]
            if dt == F16:
                flat = flat.bitcast(F16)
            if len(free) == 1:
                return flat
            names = "abcd"[:len(free)]
            spec = f"p ({' '.join(names)}) -> p {' '.join(names)}"
            return flat.rearrange(spec, **dict(zip(names, free)))

        TILES = B * L // P
        xn_h = at(0, [TILES, NODES], F16)
        xn_l = at(64 * KIB, [TILES, NODES], F16)
        xc = [at((128 + 16 * s) * KIB, [CL, NODES]) for s in range(2)]
        sq = at(160 * KIB, [CL, NODES])
        S = at(176 * KIB, [KB, NODES])
        work = at(184 * KIB, [KB, NODES + 8])
        row = [at((193 + 2 * i) * KIB - KIB // 2, [NODES]) for i in range(2)]
        ssum, nrm = row
        rinv = sb("rinv", [P, NODES])
        wT_h = [at((128 + 8 * i) * KIB, [KB, NODES], F16) for i in range(3)]
        wT_l = [at((132 + 8 * i) * KIB, [KB, NODES], F16) for i in range(3)]
        an_h = at(152 * KIB, [KB, NODES], F16)
        an_l = at(156 * KIB, [KB, NODES], F16)
        w_raw = [at(160 * KIB, [KB, NODES]), at(168 * KIB, [KB, NODES]),
                 at(88 * KIB, [KB, NODES]), at(96 * KIB, [KB, NODES])]
        A = at(160 * KIB, [KB, NODES])
        vo_h = [at(104 * KIB, [KB, NODES], F16), at(112 * KIB, [KB, NODES], F16)]
        vo_l = [at(108 * KIB, [KB, NODES], F16), at(116 * KIB, [KB, NODES], F16)]
        vo_raw = at(120 * KIB, [KB, NODES])
        deg_m = at(168 * KIB, [NODES])
        deg_t = at(170 * KIB, [NODES])
        deg_u = at(172 * KIB, [NODES])
        dinv = at(174 * KIB, [NODES])
        xg = at(0, [GB, NODES])
        x_h = at(8 * KIB, [GB, NODES], F16)
        x_l = at(12 * KIB, [GB, NODES], F16)
        xw_h = at(16 * KIB, [GB, KB, P], F16)
        xw_l = at(20 * KIB, [GB, KB, P], F16)
        y = at(24 * KIB, [GB, NODES])
        h = [at(32 * KIB, [GB, NODES]), at(40 * KIB, [GB, NODES])]
        hT_h = at(48 * KIB, [KB, GB, P], F16)
        hT_l = at(52 * KIB, [KB, GB, P], F16)
        z_h = [at(56 * KIB, [KB, GB, P], F16), at(64 * KIB, [KB, GB, P], F16)]
        z_l = [at(60 * KIB, [KB, GB, P], F16), at(68 * KIB, [KB, GB, P], F16)]
        v_h = at(72 * KIB, [GB, NODES], F16)
        v_l = at(76 * KIB, [GB, NODES], F16)
        y2 = at(80 * KIB, [GB, NODES])
        tile_at = iter(range(88 * KIB, 110 * KIB, 2 * KIB))
        diag_l, diag_g, diag_r, t_l, a_l, e_g, a_g, k_g, k_mix = (
            at(next(tile_at), [GB, P]) for _ in range(9))
        kT_h = at(108 * KIB, [GB, P], F16)
        kT_l = at(109 * KIB, [GB, P], F16)

        names = """consts_made const_steps small_in bias_in
            sq_ready ssum_ready nrm_ps nrm_in nrm_ready rinv_ready xn_ready xn_h_ready xn_l_ready gram_ps
            S_ready S_turned work_ready pick_steps A_ready stream_done
            w_in0 w_in1 w_in2 w_in3 magn_ready magn_all_ready scale_steps scale_ready
            adj_h_ready adj_l_ready w_scaled w_h_ready w_l_ready vo_ps vo_scaled
            deg_ps deg_steps deg_in deg_root d_ready an_h_ready an_l_ready an_f
            col_exp col_steps col_ready
            x_in x_h_ready x_l_ready xw_ps xw_h_ready xw_l_ready mix_ps mixed y_ready stats_ready
            ln1_var ln1_log ln1_exp ln1_steps h_ready hT_ps hT_h_ready hT_l_ready
            zl_ps zl_h_ready zl_l_ready zg_ps zg_h_ready zg_l_ready
            gl_ps gg_ps nl_in nl_log nl_exp nl_steps r_ready dr_ready dg_ready
            sq_ps rm_ps hk_ready e_ready graph_steps cf_steps cf_ready k_ready kg_ready cl_ready
            v_ps v_h_ready v_l_ready kT_ps kT_h_ready kT_l_ready out_ps y2_ready
            ln2_var ln2_log ln2_exp ln2_steps o_ready stored stats2_ready nl_steps2 stat1_steps stat2_steps""".split()
        s = {n: sem(n) for n in names}
        x_loaded = [sem("x_loaded0"), sem("x_loaded1")]

        def three(pe, dst, ah, al, bh, bl, start, stop):
            pe.matmul(dst, ah, bh, start=start, stop=False)
            pe.matmul(dst, ah, bl, start=False, stop=False)
            return pe.matmul(dst, al, bh, start=False, stop=stop)

        def per_item(c):
            return c.unsqueeze(2).broadcast_to([P, GB, P])

        def for_items(m):
            return m.unsqueeze(1).broadcast_to([P, GB, P])

        block = ctx.enter_context(nc.Block())

        @block.sync
        def _(sp):
            for c in range(2):
                sp.dma_start(xc[c], x_chunk[c]).then_inc(x_loaded[c], 16)
            sp.dma_start(adj_sb[:], adj).then_inc(s["small_in"], 16)
            sp.dma_start(bias_c[:], bias).then_inc(s["small_in"], 16)
            sp.dma_start(gate_c[:], gate.broadcast_to([P, 1])).then_inc(s["small_in"], 16)
            sp.dma_start(ls_c[:], log_sigma.broadcast_to([P, 1])).then_inc(s["small_in"], 16)
            with sp.Fori(0, NC // 2 - 1) as j:
                for c in range(2):
                    sp.wait_ge(s["xn_l_ready"], j * 2 + (c + 1))
                    sp.dma_start(xc[c], x_chunk[j * 2 + (c + 2)]).then_inc(x_loaded[c], 16)
            sp.wait_ge(s["ssum_ready"], NC)
            sp.dma_start(w_raw[0], wlT.rearrange("(k p) e -> p k e", p=P)).then_inc(s["w_in0"], 16)
            sp.dma_start(w_raw[1], wgT.rearrange("(k p) e -> p k e", p=P)).then_inc(s["w_in1"], 16)
            sp.wait_ge(s["gram_ps"], 4)
            sp.dma_start(w_raw[2], wv.rearrange("(k p) e -> p k e", p=P)).then_inc(s["w_in2"], 16)
            sp.dma_start(w_raw[3], woT.rearrange("(k p) e -> p k e", p=P)).then_inc(s["w_in3"], 16)
            sp.dma_start(xg, x_group[0]).then_inc(s["x_in"], 16)

            def load_x(g):
                sp.wait_ge(s["y_ready"], g * GB)
                sp.wait_ge(s["x_h_ready"], g)
                sp.wait_ge(s["x_l_ready"], g)
                sp.dma_start(xg, x_group[g]).then_inc(s["x_in"], 16)

            def store(g):
                sp.wait_ge(s["o_ready"], g * GB + GB)
                sp.dma_start(out_group[g], y2).then_inc(s["stored"], 16)

            load_x(1)
            load_x(2)
            with sp.Fori(0, NG - 3) as g:
                load_x(g + 3)
                store(g)
            for g in range(NG - 3, NG):
                store(g)
            sp.wait_ge(s["stored"], 16 * NG)

        @block.gpsimd
        def _(pool):
            cs = s["const_steps"]
            pool.memset(ident[:], 0.0).then_inc(cs, 1)
            pool.memset(same_item[:], 1.0).then_inc(cs, 1)
            pool.memset(ones[:], 1.0).then_inc(cs, 1)
            pool.memset(minus_half[:], -0.5).then_inc(cs, 1)
            pool.memset(self_mark[:], 0.0).then_inc(cs, 1)
            pool.memset(magn[:], 1.0).then_inc(cs, 1)
            pool.wait_ge(cs, 6)
            pool.affine_select(out=ident[:], in_=ident[:], compare_op=ALU.not_equal, fill=1.0, base=0,
                               pattern=[[-1, P]], channel_multiplier=1).then_inc(s["consts_made"], 1)
            pool.affine_select(out=self_mark[:], in_=self_mark[:], compare_op=ALU.not_equal, fill=SELF, base=0,
                               pattern=[[-1, P]], channel_multiplier=1).then_inc(s["consts_made"], 1)
            si = same_item[:].rearrange("p (b g) -> p b g", g=LG)
            pool.affine_select(out=si, in_=si, compare_op=ALU.is_ge, fill=0.0, base=0,
                               pattern=[[-LG, CB], [0, LG]], channel_multiplier=1).then_inc(cs, 1)
            pool.wait_ge(cs, 7)
            pool.affine_select(out=si, in_=si, compare_op=ALU.is_ge, fill=0.0, base=LG - 1,
                               pattern=[[LG, CB], [0, LG]], channel_multiplier=-1).then_inc(s["consts_made"], 1)
            pool.wait_ge(s["small_in"], 64)
            pool.affine_select(out=mask[:], in_=adj_sb[:], compare_op=ALU.not_equal, fill=0.0, base=0,
                               pattern=[[-1, P]], channel_multiplier=1).then_inc(s["consts_made"], 1)

            with pool.Fori(0, NC // 2) as j:
                for c in range(2):
                    pool.wait_ge(s["xn_h_ready"], j * 2 + (c + 1))
                    pool.tensor_tensor(xn_l[:, bass.ds(j * (2 * CL) + c * CL, CL), :], xc[c],
                                       xn_h[:, bass.ds(j * (2 * CL) + c * CL, CL), :],
                                       ALU.subtract).then_inc(s["xn_l_ready"], 1)

            pool.wait_ge(s["magn_ready"], 6)
            pool.partition_all_reduce(magn_all[:], magn[:], P, ABSMAX).then_inc(s["magn_all_ready"], 1)
            pool.wait_ge(s["adj_h_ready"], 2)
            pool.tensor_tensor(adj_l[:], adj_sb[:], adj_h[:], ALU.subtract).then_inc(s["adj_l_ready"], 1)
            for i, (raw, hi, lo) in enumerate([(w_raw[0], wT_h[0], wT_l[0]), (w_raw[1], wT_h[1], wT_l[1]),
                                               (w_raw[2], vo_h[0], vo_l[0]), (w_raw[3], vo_h[1], vo_l[1]),
                                               (vo_raw, wT_h[2], wT_l[2])]):
                pool.wait_ge(s["w_h_ready"], i + 1)
                pool.tensor_tensor(lo, raw, hi, ALU.subtract).then_inc(s["w_l_ready"], 1)

            def graphs(g):
                pool.wait_ge(s["r_ready"], g + 1)
                wait(pool, s["rm_ps"], g)
                pool.tensor_tensor(diag_r, for_items(ident[:]), per_item(nl[:, 5, :]),
                                   ALU.mult).then_inc(s["dr_ready"], 1)
                pool.wait_ge(s["cf_ready"], g + 1)
                wait(pool, s["k_ready"], g)
                pool.tensor_tensor(k_g, a_g, per_item(cf[:, 7, :]), ALU.mult).then_inc(s["kg_ready"], 1)

            graphs(0)
            with pool.Fori(1, NG) as g:
                graphs(g)

        @block.tensor
        def _(pe):
            pe.wait_ge(s["consts_made"], 3)

            def item_sums(c):
                pe.wait_ge(s["ssum_ready"], c + 1)
                wait(pe, s["nrm_in"], c)
                pe.matmul(bank[7][:], same_item[:], ssum, start=True, stop=True).then_inc(s["nrm_ps"], 1)

            def gram(c, rows, first, last):
                for t in range(CL):
                    for r in rows:
                        o = bass.ds(c * CL + t, 1) if not isinstance(c, int) else slice(c * CL + t, c * CL + t + 1)
                        xh = xn_h[:, o, :].rearrange("p a n -> p (a n)")
                        xl = xn_l[:, o, :].rearrange("p a n -> p (a n)")
                        mm = three(pe, bank[r][:, 0:NODES - r * P],
                                   xh[:, r * P:(r + 1) * P], xl[:, r * P:(r + 1) * P],
                                   xh[:, r * P:], xl[:, r * P:],
                                   start=(first and t == 0), stop=(last and t == CL - 1))
                        if last and t == CL - 1:
                            mm.then_inc(s["gram_ps"], 1)

            def turn(dst, i, j):
                return pe.transpose(dst, S[:, i, j * P:(j + 1) * P], ident[:])

            item_sums(0)
            item_sums(1)
            pe.wait_ge(s["xn_l_ready"], 1)
            gram(0, (0, 1), True, False)
            with pe.Fori(1, NC - 1) as c:
                item_sums(c + 1)
                pe.wait_ge(s["xn_l_ready"], c + 1)
                gram(c, (0, 1), False, False)
            pe.wait_ge(s["xn_l_ready"], NC)
            gram(NC - 1, (0, 1), False, True)
            pe.wait_ge(s["S_ready"], 2)
            turn(bank[4][:, 0:P], 0, 1).then_inc(s["S_turned"], 1)
            turn(bank[5][:, 0:P], 0, 2)
            turn(bank[5][:, P:2 * P], 1, 2).then_inc(s["S_turned"], 1)
            turn(bank[6][:, 0:P], 0, 3)
            turn(bank[6][:, P:2 * P], 1, 3).then_inc(s["S_turned"], 1)
            for r in range(2, KB):
                gram(0, (r,), True, False)
                with pe.Fori(1, NC - 1) as c:
                    gram(c, (r,), False, False)
                gram(NC - 1, (r,), False, True)
            pe.wait_ge(s["S_ready"], 6)
            turn(bank[7][:, 0:P], 2, 3).then_inc(s["S_turned"], 1)

            pe.wait_ge(s["w_l_ready"], 4)
            for d in range(KB):
                for f in range(KB):
                    mm = three(pe, bank[d][:], vo_h[0][:, f, d * P:(d + 1) * P], vo_l[0][:, f, d * P:(d + 1) * P],
                               vo_h[1][:, f, :], vo_l[1][:, f, :], start=(f == 0), stop=(f == KB - 1))
                mm.then_inc(s["vo_ps"], 1)

            def project_x(g):
                pe.wait_ge(s["x_l_ready"], g + 1)
                for b in range(GB):
                    wait(pe, s["zl_l_ready"], g * GB - GB + (b + 1) if not isinstance(g, int) or g > 0 else 0)
                    for k in range(KB):
                        mm = three(pe, bank[b][:, k * P:(k + 1) * P],
                                   x_h[:, b, k * P:(k + 1) * P], x_l[:, b, k * P:(k + 1) * P],
                                   adj_h[:], adj_l[:], start=True, stop=True)
                    mm.then_inc(s["xw_ps"], 1)

            def mix_nodes(g):
                for b in range(GB):
                    pe.wait_ge(s["xw_l_ready"], g * GB + (b + 1))
                    wait(pe, s["zg_l_ready"], g * GB - GB + (b + 1) if not isinstance(g, int) or g > 0 else 0)
                    for k in range(KB):
                        mm = three(pe, bank[b][:], xw_h[:, b, k, :], xw_l[:, b, k, :],
                                   an_h[:, k, :], an_l[:, k, :], start=(k == 0), stop=(k == KB - 1))
                    mm.then_inc(s["mix_ps"], 1)

            h_bank = [bank[4], bank[5], bank[7], bank[4]]

            def turn_h(g, slot, b):
                pe.wait_ge(s["h_ready"], g * GB + (b + 1))
                if b == 3:
                    pe.wait_ge(s["hT_l_ready"], g * GB + 1)
                for k in range(KB):
                    mm = pe.transpose(h_bank[b][:, k * P:(k + 1) * P], h[slot][:, b, k * P:(k + 1) * P], ident[:])
                mm.then_inc(s["hT_ps"], 1)

            def project_z(g, i, freed, done):
                for e in range(KB):
                    wait(pe, freed[0], freed[1] + (e + 1))
                    for k in range(KB):
                        mm = three(pe, bank[e][:], wT_h[i][:, k, e * P:(e + 1) * P], wT_l[i][:, k, e * P:(e + 1) * P],
                                   hT_h[:, k, :, :], hT_l[:, k, :, :], start=(k == 0), stop=(k == KB - 1))
                    mm.then_inc(done, 1)

            def inner_products(g, i, done):
                for b in range(GB):
                    for e in range(KB):
                        mm = three(pe, bank[4 + i][:, b * P:(b + 1) * P], z_h[i][:, e, b, :], z_l[i][:, e, b, :],
                                   z_h[i][:, e, b, :], z_l[i][:, e, b, :],
                                   start=(b == 0 and e == 0), stop=(b == GB - 1 and e == KB - 1))
                mm.then_inc(done, 1)

            def values(g, b, last_group):
                if last_group:
                    pe.wait_ge(s["zg_l_ready"], g * GB + (b + 1))
                else:
                    pe.wait_ge(s["mixed"], g * GB + GB + (b + 1))
                for k in range(KB):
                    mm = three(pe, bank[b][:], hT_h[:, k, b, :], hT_l[:, k, b, :],
                               wT_h[2][:, k, :], wT_l[2][:, k, :], start=(k == 0), stop=(k == KB - 1))
                mm.then_inc(s["v_ps"], 1)

            def weighted(g, b):
                pe.wait_ge(s["v_l_ready"], g * GB + (b + 1))
                three(pe, bank[b][:], kT_h[:, b, :], kT_l[:, b, :], v_h[:, b, :], v_l[:, b, :],
                      start=True, stop=True).then_inc(s["out_ps"], 1)

            def body(g, slot, has_next):
                pe.wait_ge(s["hT_l_ready"], g * GB + GB)
                if isinstance(g, int) and g == 0:
                    project_z(g, 0, (s["mixed"], 0), s["zl_ps"])
                else:
                    project_z(g, 0, (s["y2_ready"], g * GB - GB), s["zl_ps"])
                if has_next:
                    project_x(g + 1)
                    project_z(g, 1, (s["xw_l_ready"], g * GB + GB), s["zg_ps"])
                    mix_nodes(g + 1)
                else:
                    project_z(g, 1, (s["zl_l_ready"], g * GB), s["zg_ps"])
                pe.wait_ge(s["zg_l_ready"], g * GB + GB)
                inner_products(g, 1, s["gg_ps"])
                inner_products(g, 0, s["gl_ps"])
                values(g, 0, not has_next)
                pe.wait_ge(s["dg_ready"], g * 2 + 2)
                pe.matmul(bank[5][:], minus_half[:], diag_g, start=False, stop=True,
                          skip_group_check=True).then_inc(s["sq_ps"], 1)
                values(g, 1, not has_next)
                pe.wait_ge(s["dr_ready"], g + 1)
                pe.matmul(bank[7][:], ones[:], diag_r, start=True, stop=True).then_inc(s["rm_ps"], 1)
                values(g, 2, not has_next)
                values(g, 3, not has_next)
                pe.wait_ge(s["k_ready"], g + 1)
                wait(pe, s["kT_l_ready"], g)
                for b in range(GB):
                    mm = pe.transpose(bank[6][:, b * P:(b + 1) * P], k_mix[:, b, :], ident[:])
                mm.then_inc(s["kT_ps"], 1)
                if has_next:
                    for b in range(3):
                        turn_h(g + 1, 1 - slot, b)
                pe.wait_ge(s["kT_l_ready"], g + 1)
                weighted(g, 0)
                weighted(g, 1)
                if has_next:
                    turn_h(g + 1, 1 - slot, 3)
                weighted(g, 2)
                weighted(g, 3)

            pe.wait_ge(s["vo_scaled"], KB)
            pe.wait_ge(s["adj_l_ready"], 1)
            project_x(0)
            for i in range(KB):
                pe.wait_ge(s["A_ready"], i + 1)
                mm = pe.matmul(bank[7][:], ones[:], A[:, i, :], start=(i == 0), stop=(i == KB - 1))
            mm.then_inc(s["deg_ps"], 1)
            pe.wait_ge(s["an_l_ready"], KB)
            mix_nodes(0)
            pe.wait_ge(s["w_l_ready"], 5)
            for b in range(GB):
                turn_h(0, 0, b)
            body(0, 0, True)
            with pe.Fori(0, NG // 2 - 1) as j:
                for t in (1, 2):
                    body(j * 2 + t, t % 2, True)
            body(NG - 1, (NG - 1) % 2, False)

        @block.scalar
        def _(act):
            def square(c, slot, turn_):
                act.wait_ge(x_loaded[slot], turn_ * 16 + 16)
                wait(act, s["ssum_ready"], c)
                act.activation(sq, xc[slot], ACT.Square).then_inc(s["sq_ready"], 1)

            def root(c):
                act.wait_ge(s["nrm_in"], c + 1)
                act.activation(nrm, nrm, ACT.Sqrt).then_inc(s["nrm_ready"], 1)

            def high(c, slot):
                act.wait_ge(s["xn_ready"], c + 1)
                o = bass.ds(c * CL, CL) if not isinstance(c, int) else slice(c * CL, (c + 1) * CL)
                act.activation(xn_h[:, o, :], xc[slot], ACT.Copy).then_inc(s["xn_h_ready"], 1)

            def chunk_pair(j):
                root(j * 2)
                square(j * 2 + 1, 1, j)
                high(j * 2, 0)
                root(j * 2 + 1)
                square(j * 2 + 2, 0, j + 1)
                high(j * 2 + 1, 1)

            square(0, 0, 0)
            chunk_pair(0)
            with act.Fori(1, NC // 2 - 1) as j:
                chunk_pair(j)
            root(NC - 2)
            square(NC - 1, 1, NC // 2 - 1)
            high(NC - 2, 0)
            root(NC - 1)
            high(NC - 1, 1)

            def s_out(dst, src):
                act.activation(dst, src, ACT.Copy, scale=S_SCALE).then_inc(s["S_ready"], 1)

            act.wait_ge(s["gram_ps"], 2)
            s_out(S[:, 0, :], bank[0][:])
            s_out(S[:, 1, P:], bank[1][:, 0:NODES - P])
            act.wait_ge(s["S_turned"], 3)
            for dst, src in ((S[:, 1, 0:P], bank[4][:, 0:P]), (S[:, 2, 0:2 * P], bank[5][:, 0:2 * P]),
                             (S[:, 3, 0:2 * P], bank[6][:, 0:2 * P])):
                act.activation(dst, src, ACT.Copy).then_inc(s["S_ready"], 1)
            act.wait_ge(s["gram_ps"], 3)
            s_out(S[:, 2, 2 * P:], bank[2][:, 0:2 * P])
            act.wait_ge(s["gram_ps"], 4)
            s_out(S[:, 3, 3 * P:], bank[3][:, 0:P])
            act.wait_ge(s["S_turned"], 4)
            act.activation(S[:, 3, 2 * P:3 * P], bank[7][:, 0:P], ACT.Copy).then_inc(s["S_ready"], 1)

            act.wait_ge(s["scale_ready"], 1)
            act.wait_ge(s["consts_made"], 4)
            act.activation(adj_sb[:], adj_sb[:], ACT.Copy, scale=up[:, 4:5]).then_inc(s["adj_h_ready"], 1)
            act.wait_ge(s["adj_h_ready"], 1)
            act.activation(adj_h[:], adj_sb[:], ACT.Copy).then_inc(s["adj_h_ready"], 1)
            act.wait_ge(s["xn_l_ready"], NC)
            act.wait_ge(s["gram_ps"], 4)
            for i, hi in enumerate([wT_h[0], wT_h[1], vo_h[0], vo_h[1]]):
                act.activation(w_raw[i], w_raw[i], ACT.Copy, scale=up[:, i:i + 1]).then_inc(s["w_scaled"], 1)
                act.wait_ge(s["w_scaled"], i + 1)
                act.activation(hi, w_raw[i], ACT.Copy).then_inc(s["w_h_ready"], 1)

            def x_high(g):
                act.wait_ge(s["x_in"], g * 16 + 16)
                wait(act, s["xw_ps"], g * GB)
                act.activation(x_h, xg, ACT.Copy, scale=up[:, 5:6]).then_inc(s["x_h_ready"], 1)

            def xw_high(g):
                for b in range(GB):
                    act.wait_ge(s["xw_ps"], g * GB + (b + 1))
                    act.activation(xw_h[:, b, :, :], bank[b][:], ACT.Copy, scale=XW_DOWN).then_inc(s["xw_h_ready"], 1)

            def add_bias(g):
                for b in range(GB):
                    act.wait_ge(s["mix_ps"], g * GB + (b + 1))
                    wait(act, s["h_ready"], g * GB - GB + (b + 1) if not isinstance(g, int) or g > 0 else 0)
                    act.activation(y[:, b, :], bank[b][:], ACT.Identity, scale=c1(ALPHA_C),
                                   bias=bias_c[:]).then_inc(s["mixed"], 1)

            def log_exp(g, t, ready, logged, done):
                act.wait_ge(ready, g + 1)
                act.activation(t[:, 1, :], t[:, 0, :], ACT.Ln).then_inc(logged, 1)
                act.wait_ge(logged, g + 1)
                act.activation(t[:, 2, :], t[:, 1, :], ACT.Exp, scale=-0.5).then_inc(done, 1)

            x_high(0)
            for d in range(KB):
                act.wait_ge(s["vo_ps"], d + 1)
                act.activation(vo_raw[:, d, :], bank[d][:], ACT.Copy, scale=VO_DOWN).then_inc(s["vo_scaled"], 1)
            act.wait_ge(s["vo_scaled"], KB)
            act.activation(wT_h[2], vo_raw, ACT.Copy).then_inc(s["w_h_ready"], 1)
            xw_high(0)
            act.wait_ge(s["deg_in"], 1)
            act.activation(deg_t, deg_m, ACT.Sqrt).then_inc(s["deg_root"], 1)
            for i in range(KB):
                act.wait_ge(s["an_f"], i + 1)
                act.activation(an_h[:, i, :], A[:, i, :], ACT.Copy).then_inc(s["an_h_ready"], 1)
            act.preload_act_table_set("natural_log_exp_and_others")
            act.wait_ge(s["small_in"], 64)
            act.activation(c1(T0), gate_c[:], ACT.Exp, scale=-1.0).then_inc(s["col_exp"], 1)
            act.activation(c1(T1), ls_c[:], ACT.Exp, scale=-2.0).then_inc(s["col_exp"], 1)
            act.wait_ge(s["d_ready"], 1)
            add_bias(0)
            log_exp(0, ln1, s["ln1_var"], s["ln1_log"], s["ln1_exp"])

            def hT_high(g, b):
                act.wait_ge(s["hT_ps"], g * GB + (b + 1))
                act.activation(hT_h[:, :, b, :], bank[(4, 5, 7, 4)[b]][:].rearrange("p (k n) -> p k n", k=KB),
                               ACT.Copy, scale=H_UP).then_inc(s["hT_h_ready"], 1)

            def body(g, slot, has_next, has_second, has_previous):
                def z_high(i, ps, done, e):
                    act.wait_ge(ps, g * GB + (e + 1))
                    act.activation(z_h[i][:, e, :, :], bank[e][:].rearrange("p (b n) -> p b n", b=GB), ACT.Copy,
                                   scale=Z_DOWN).then_inc(done, 1)

                for e in range(KB):
                    z_high(0, s["zl_ps"], s["zl_h_ready"], e)
                    if e == 1 and has_previous:
                        log_exp(g - 1, ln2, s["ln2_var"], s["ln2_log"], s["ln2_exp"])
                if has_next:
                    xw_high(g + 1)
                for e in range(KB):
                    z_high(1, s["zg_ps"], s["zg_h_ready"], e)
                if has_next:
                    add_bias(g + 1)
                    log_exp(g + 1, ln1, s["ln1_var"], s["ln1_log"], s["ln1_exp"])
                log_exp(g, nl, s["nl_in"], s["nl_log"], s["nl_exp"])

                def v_high(b):
                    act.wait_ge(s["v_ps"], g * GB + (b + 1))
                    act.activation(v_h[:, b, :], bank[b][:], ACT.Copy, scale=V_DOWN).then_inc(s["v_h_ready"], 1)

                v_high(0)
                act.wait_ge(s["sq_ps"], g + 1)
                act.wait_ge(s["hk_ready"], g + 1)
                wait(act, s["graph_steps"], g * 4)
                for b in range(GB):
                    ex = act.activation(e_g[:, b, :], bank[5][:, b * P:(b + 1) * P], ACT.Exp,
                                        scale=c1(KAPPA), bias=cf[:, 0, b:b + 1])
                ex.then_inc(s["e_ready"], 1)
                for b in range(1, GB):
                    v_high(b)
                act.wait_ge(s["kT_ps"], g + 1)
                act.activation(kT_h, bank[6][:].rearrange("p (b n) -> p b n", b=GB), ACT.Copy,
                               scale=K_UP).then_inc(s["kT_h_ready"], 1)
                if has_next:
                    for b in range(GB):
                        hT_high(g + 1, b)
                if has_second:
                    x_high(g + 2)

            for b in range(GB):
                hT_high(0, b)
            x_high(1)
            body(0, 0, True, True, False)
            with act.Fori(0, NG // 2 - 2) as j:
                for t in (1, 2):
                    body(j * 2 + t, t % 2, True, True, True)
            body(NG - 3, (NG - 3) % 2, True, True, True)
            body(NG - 2, (NG - 2) % 2, True, False, True)
            body(NG - 1, (NG - 1) % 2, False, False, True)
            log_exp(NG - 1, ln2, s["ln2_var"], s["ln2_log"], s["ln2_exp"])

        @block.vector
        def _(dve):
            def sum_squares(c):
                dve.wait_ge(s["sq_ready"], c + 1)
                wait(dve, s["nrm_ps"], c)
                dve.tensor_reduce(ssum, sq.rearrange("p l n -> p n l"), AX.X, ALU.add).then_inc(s["ssum_ready"], 1)

            def normalise(c, slot):
                dve.wait_ge(s["nrm_ps"], c + 1)
                wait(dve, s["xn_ready"], c)
                dve.tensor_scalar(nrm, bank[7][:], NORM_EPS * NORM_EPS, None, ALU.max).then_inc(s["nrm_in"], 1)
                dve.wait_ge(s["nrm_ready"], c + 1)
                o = bass.ds(c, 1) if not isinstance(c, int) else slice(c, c + 1)
                dve.tensor_reduce(chunk_max[:, o], nrm, AX.X, ALU.max)
                dve.reciprocal(rinv[:], nrm).then_inc(s["rinv_ready"], 1)
                dve.wait_ge(s["rinv_ready"], c + 1)
                dve.wait_ge(s["sq_ready"], c + 1)
                dve.scalar_tensor_tensor(xc[slot], xc[slot], X_HAT, rinv[:].unsqueeze(1).broadcast_to([P, CL, NODES]),
                                         ALU.mult, ALU.mult).then_inc(s["xn_ready"], 1)

            dve.memset(work[:, :, NODES:], PAD).then_inc(s["work_ready"], 1)
            sum_squares(0)
            for c in range(2):
                normalise(c, c)
                sum_squares(c + 1)
            with dve.Fori(1, NC // 2 - 1) as j:
                for t in range(2):
                    normalise(j * 2 + t, t)
                    sum_squares(j * 2 + (t + 1))
            normalise(NC - 2, 0)
            sum_squares(NC - 1)
            normalise(NC - 1, 1)

            def fill_work(r, done):
                dve.wait_ge(s["S_ready"], done)
                dve.tensor_copy(work[:, r, 0:NODES], S[:, r, :]).then_inc(s["work_ready"], 1)
                dve.wait_ge(s["work_ready"], 1 + 2 * r + 1)
                dve.tensor_tensor(work[:, r, r * P:(r + 1) * P], work[:, r, r * P:(r + 1) * P], self_mark[:],
                                  ALU.add).then_inc(s["work_ready"], 1)

            PICKS = 4 * (ROUNDS + 1) + 2

            def pick(pair):
                r0 = 2 * pair
                base = pair * PICKS
                ps = s["pick_steps"]
                dve.wait_ge(s["work_ready"], 1 + 2 * (r0 + 2))
                for i in range(ROUNDS + 1):
                    n = base + 4 * i
                    for t in range(2):
                        wait(dve, ps, n - 1 + t if i > 0 else 0)
                        dve.max(top8[:, r0 + t, :], work[:, r0 + t, :]).then_inc(ps, 1)
                    n += 2
                    if i == ROUNDS:
                        for t in range(2):
                            dve.wait_ge(ps, n - 1 + t)
                            dve.memset(top8[:, r0 + t, LAST:], PAD).then_inc(ps, 1)
                        n += 2
                    for t in range(2):
                        dve.wait_ge(ps, n - 1 + t)
                        dve.match_replace(work[:, r0 + t, :], top8[:, r0 + t, :], work[:, r0 + t, :],
                                          TAKEN).then_inc(ps, 1)
                return base + PICKS

            def keep(pair, picked):
                for t in range(2):
                    r = 2 * pair + t
                    dve.wait_ge(s["pick_steps"], picked)
                    dve.wait_ge(s["w_l_ready"], 2)
                    dve.scalar_tensor_tensor(A[:, r, :], work[:, r, 0:NODES], TAKEN, S[:, r, :],
                                             ALU.is_equal, ALU.mult).then_inc(s["A_ready"], 1)

            dve.wait_ge(s["consts_made"], 4)
            fill_work(0, 2)
            fill_work(1, 3)
            picked = pick(0)
            mg = s["magn_ready"]
            for i in range(4):
                dve.wait_ge(s[f"w_in{i}"], 16)
                dve.tensor_reduce(magn[:, i:i + 1], w_raw[i].rearrange("p k e -> p (k e)"), AX.X,
                                  ALU.max, apply_absolute_value=True).then_inc(mg, 1)
            dve.wait_ge(s["small_in"], 64)
            dve.tensor_reduce(magn[:, 4:5], adj_sb[:], AX.X, ALU.max, apply_absolute_value=True).then_inc(mg, 1)
            dve.wait_ge(s["xn_ready"], NC)
            dve.tensor_reduce(magn[:, 5:6], chunk_max[:], AX.X, ALU.max).then_inc(mg, 1)
            dve.wait_ge(s["magn_all_ready"], 1)
            ss = s["scale_steps"]
            dve.tensor_scalar(magn_all[:], magn_all[:], 1e-30, None, ALU.max).then_inc(ss, 1)
            dve.wait_ge(ss, 1)
            dve.tensor_scalar(pw[:].bitcast(I32), magn_all[:].bitcast(I32), EXPONENT, None,
                              ALU.bitwise_and).then_inc(ss, 1)
            dve.wait_ge(ss, 2)
            dve.reciprocal(ipw[:], pw[:]).then_inc(ss, 1)
            dve.wait_ge(ss, 3)
            dve.tensor_scalar(up[:, 0:5], ipw[:, 0:5], W_UP, None, ALU.mult).then_inc(ss, 1)
            dve.tensor_scalar(up[:, 5:6], ipw[:, 5:6], X_UP, None, ALU.mult).then_inc(ss, 1)
            dve.wait_ge(ss, 5)
            dve.tensor_scalar(magn_all[:], magn_all[:], 1.0, None, ALU.mult).then_inc(s["scale_ready"], 1)

            fill_work(2, 6)
            fill_work(3, 8)
            picked2 = pick(1)
            keep(0, picked)
            keep(1, picked2)

            def x_low(g):
                dve.wait_ge(s["x_h_ready"], g + 1)
                dve.scalar_tensor_tensor(x_l, xg, up[:, 5:6], x_h, ALU.mult,
                                         ALU.subtract).then_inc(s["x_l_ready"], 1)

            def xw_low(g):
                for b in range(GB):
                    dve.wait_ge(s["xw_h_ready"], g * GB + (b + 1))
                    dve.scalar_tensor_tensor(xw_l[:, b, :, :], bank[b][:].rearrange("p (k n) -> p k n", k=KB),
                                             XW_DOWN, xw_h[:, b, :, :], ALU.mult,
                                             ALU.subtract).then_inc(s["xw_l_ready"], 1)

            x_low(0)
            xw_low(0)
            ds_ = s["deg_steps"]
            dve.wait_ge(s["deg_ps"], 1)
            dve.tensor_scalar(deg_m, bank[7][:], 1e-34, None, ALU.max).then_inc(s["deg_in"], 1)
            dve.tensor_scalar(dinv, bank[7][:], 0.0, None, ALU.is_gt).then_inc(ds_, 1)
            dve.wait_ge(s["deg_root"], 1)
            dve.reciprocal(deg_t, deg_t).then_inc(ds_, 1)
            dve.wait_ge(ds_, 2)
            dve.tensor_tensor(deg_u, deg_m, deg_t, ALU.mult).then_inc(ds_, 1)
            dve.wait_ge(ds_, 3)
            dve.scalar_tensor_tensor(deg_u, deg_u, -0.5, deg_t, ALU.mult, ALU.mult).then_inc(ds_, 1)
            dve.wait_ge(ds_, 4)
            dve.scalar_tensor_tensor(deg_t, deg_u, 1.5, deg_t, ALU.add, ALU.mult).then_inc(ds_, 1)
            dve.wait_ge(ds_, 5)
            dve.tensor_tensor(dinv, dinv, deg_t, ALU.mult).then_inc(ds_, 1)
            dve.wait_ge(ds_, 6)
            dve.tensor_reduce(c1(D_MAX), dinv, AX.X, ALU.max).then_inc(ds_, 1)
            dve.tensor_tensor(deg_u.rearrange("p (k n) -> p k n", k=KB), dinv.rearrange("p (k n) -> p k n", k=KB),
                              ident[:].unsqueeze(1).broadcast_to([P, KB, P]), ALU.mult).then_inc(ds_, 1)
            dve.wait_ge(ds_, 8)
            dve.tensor_reduce(dinv_col[:], deg_u.rearrange("p (k n) -> p k n", k=KB), AX.X,
                              ALU.add).then_inc(ds_, 1)
            dve.tensor_scalar(c1(D_MAX), c1(D_MAX), 1e-30, None, ALU.max).then_inc(ds_, 1)
            dve.wait_ge(ds_, 10)
            dve.tensor_scalar(c1(D_POW).bitcast(I32), c1(D_MAX).bitcast(I32), EXPONENT, None,
                              ALU.bitwise_and).then_inc(ds_, 1)
            dve.wait_ge(ds_, 11)
            dve.reciprocal(c1(D_INV), c1(D_POW)).then_inc(ds_, 1)
            dve.wait_ge(ds_, 12)
            dve.tensor_scalar(dinv, dinv, c1(D_INV), None, ALU.mult).then_inc(ds_, 1)
            dve.tensor_scalar(dinv_col[:], dinv_col[:], c1(D_INV), A_UP, ALU.mult, ALU.mult).then_inc(ds_, 1)
            dve.wait_ge(ds_, 14)
            for i in range(KB):
                dve.scalar_tensor_tensor(A[:, i, :], A[:, i, :], dinv_col[:, i:i + 1], dinv, ALU.mult,
                                         ALU.mult).then_inc(s["an_f"], 1)
            for i in range(KB):
                dve.wait_ge(s["an_h_ready"], i + 1)
                dve.tensor_tensor(an_l[:, i, :], A[:, i, :], an_h[:, i, :], ALU.subtract).then_inc(s["an_l_ready"], 1)
            cs = s["col_steps"]
            dve.scalar_tensor_tensor(c1(ALPHA_C), c1(D_POW), ALPHA, c1(D_POW), ALU.mult, ALU.mult).then_inc(cs, 1)
            dve.wait_ge(cs, 1)
            dve.scalar_tensor_tensor(c1(ALPHA_C), c1(ALPHA_C), pw[:, 4:5], pw[:, 5:6], ALU.mult,
                                     ALU.mult).then_inc(s["d_ready"], 1)
            dve.tensor_scalar(c1(CAP_C), pw[:, 0:1], Z_UNIT / ROW_EPS, None, ALU.mult).then_inc(cs, 1)
            dve.scalar_tensor_tensor(c1(BETA_C), pw[:, 2:3], BETA, pw[:, 3:4], ALU.mult, ALU.mult).then_inc(cs, 1)
            dve.scalar_tensor_tensor(c1(KAPPA), pw[:, 1:2], Z_UNIT * Z_UNIT, pw[:, 1:2], ALU.mult,
                                     ALU.mult).then_inc(cs, 1)
            dve.wait_ge(cs, 4)
            dve.wait_ge(s["col_exp"], 2)
            dve.tensor_tensor(c1(KAPPA), c1(KAPPA), c1(T1), ALU.mult).then_inc(cs, 1)
            dve.tensor_scalar(c1(W_G), c1(T0), 1.0, None, ALU.add).then_inc(cs, 1)
            dve.wait_ge(cs, 6)
            dve.tensor_scalar(c1(HK), c1(KAPPA), -0.5, None, ALU.mult).then_inc(cs, 1)
            dve.reciprocal(c1(W_L), c1(W_G)).then_inc(cs, 1)
            dve.wait_ge(cs, 8)
            dve.tensor_scalar(c1(W_G), c1(W_L), -1.0, 1.0, ALU.mult, ALU.add).then_inc(cs, 1)
            dve.wait_ge(cs, 9)

            def newton(g, t, exped, steps, dst, per):
                dve.wait_ge(exped, g + 1)
                dve.scalar_tensor_tensor(t[:, 3, :], t[:, 0, :], -0.5, t[:, 2, :], ALU.mult, ALU.mult).then_inc(steps, 1)
                dve.wait_ge(steps, g * per + 1)
                dve.tensor_tensor(t[:, 4, :], t[:, 3, :], t[:, 2, :], ALU.mult).then_inc(steps, 1)
                dve.wait_ge(steps, g * per + 2)
                return dve.scalar_tensor_tensor(dst, t[:, 4, :], 1.5, t[:, 2, :], ALU.add, ALU.mult)

            def moments(g, st, m, var, ready, ln):
                dve.wait_ge(s["consts_made"], 4)
                dve.wait_ge(ready, g * GB + GB)
                for b in range(GB):
                    ag = dve.bn_aggr(m[:, b, :], st[:, b, :])
                ag.then_inc(s["stats_ready"] if m is mv else s["stats2_ready"], 1)
                dve.wait_ge(s["stats_ready"] if m is mv else s["stats2_ready"], g + 1)
                dve.tensor_scalar(ln[:, 0, :], m[:, :, 1], LN_EPS, None, ALU.add).then_inc(var, 1)

            def norm_rows(g, src, dst, m, ln, exped, steps, per, done):
                newton(g, ln, exped, steps, ln[:, 3, :], per).then_inc(steps, 1)
                dve.wait_ge(steps, g * per + 3)
                for b in range(GB):
                    dve.tensor_scalar(dst[:, b, :], src[:, b, :], m[:, b, 0:1], ln[:, 3, b:b + 1], ALU.subtract,
                                      ALU.mult).then_inc(done, 1)

            def residual(g):
                for b in range(GB):
                    dve.wait_ge(s["mixed"], g * GB + (b + 1))
                    dve.tensor_tensor(y[:, b, :], y[:, b, :], xg[:, b, :], ALU.add).then_inc(s["y_ready"], 1)
                    if b:
                        dve.wait_ge(s["y_ready"], g * GB + b)
                        dve.bn_stats(stats[:, b - 1, :], y[:, b - 1, :]).then_inc(s["stat1_steps"], 1)
                dve.wait_ge(s["y_ready"], g * GB + GB)
                dve.bn_stats(stats[:, GB - 1, :], y[:, GB - 1, :]).then_inc(s["stat1_steps"], 1)
                moments(g, stats, mv, s["ln1_var"], s["stat1_steps"], ln1)

            def first_norm(g, slot):
                norm_rows(g, y, h[slot], mv, ln1, s["ln1_exp"], s["ln1_steps"], 3, s["h_ready"])

            def second_norm(g):
                norm_rows(g, y2, y2, mv2, ln2, s["ln2_exp"], s["ln2_steps"], 3, s["o_ready"])

            def second_residual(g, slot, has_previous):
                if has_previous:
                    dve.wait_ge(s["stored"], g * 16)
                for b in range(GB):
                    dve.wait_ge(s["out_ps"], g * GB + (b + 1))
                    dve.scalar_tensor_tensor(y2[:, b, :], bank[b][:], c1(BETA_C), h[slot][:, b, :], ALU.mult,
                                             ALU.add).then_inc(s["y2_ready"], 1)
                    if b:
                        dve.wait_ge(s["y2_ready"], g * GB + b)
                        dve.bn_stats(stats2[:, b - 1, :], y2[:, b - 1, :]).then_inc(s["stat2_steps"], 1)
                dve.wait_ge(s["y2_ready"], g * GB + GB)
                dve.bn_stats(stats2[:, GB - 1, :], y2[:, GB - 1, :]).then_inc(s["stat2_steps"], 1)
                moments(g, stats2, mv2, s["ln2_var"], s["stat2_steps"], ln2)

            def hT_low(g, b):
                dve.wait_ge(s["hT_h_ready"], g * GB + (b + 1))
                dve.scalar_tensor_tensor(hT_l[:, :, b, :], bank[(4, 5, 7, 4)[b]][:].rearrange("p (k n) -> p k n", k=KB),
                                         H_UP, hT_h[:, :, b, :], ALU.mult,
                                         ALU.subtract).then_inc(s["hT_l_ready"], 1)

            def body(g, slot, has_next, has_second, has_previous):
                def z_low(i, hi, done, e):
                    dve.wait_ge(hi, g * GB + (e + 1))
                    dve.scalar_tensor_tensor(z_l[i][:, e, :, :], bank[e][:].rearrange("p (b n) -> p b n", b=GB),
                                             Z_DOWN, z_h[i][:, e, :, :], ALU.mult,
                                             ALU.subtract).then_inc(done, 1)

                for e in range(KB):
                    z_low(0, s["zl_h_ready"], s["zl_l_ready"], e)
                    if e == 1 and has_previous:
                        second_norm(g - 1)
                if has_next:
                    xw_low(g + 1)
                for e in range(KB):
                    z_low(1, s["zg_h_ready"], s["zg_l_ready"], e)
                if has_next:
                    residual(g + 1)

                gl = bank[4][:].rearrange("p (b n) -> p b n", b=GB)
                gg = bank[5][:].rearrange("p (b n) -> p b n", b=GB)
                gs = s["graph_steps"]
                dve.wait_ge(s["gg_ps"], g + 1)
                dve.tensor_tensor(diag_g, gg, for_items(ident[:]), ALU.mult).then_inc(s["dg_ready"], 1)
                dve.wait_ge(s["dg_ready"], g * 2 + 1)
                dve.tensor_reduce(cf[:, 1, :], diag_g, AX.X, ALU.add).then_inc(s["dg_ready"], 1)
                dve.wait_ge(s["dg_ready"], g * 2 + 2)
                dve.tensor_scalar(cf[:, 0, :], cf[:, 1, :], c1(HK), None, ALU.mult).then_inc(s["hk_ready"], 1)
                if has_next:
                    first_norm(g + 1, 1 - slot)
                dve.wait_ge(s["gl_ps"], g + 1)
                dve.tensor_tensor(diag_l, gl, for_items(ident[:]), ALU.mult).then_inc(s["nl_steps"], 1)
                dve.wait_ge(s["nl_steps"], g * 2 + 1)
                dve.tensor_reduce(nl[:, 5, :], diag_l, AX.X, ALU.add).then_inc(s["nl_steps"], 1)
                dve.wait_ge(s["nl_steps"], g * 2 + 2)
                dve.tensor_scalar(nl[:, 0, :], nl[:, 5, :], 1e-18, None, ALU.max).then_inc(s["nl_in"], 1)
                dve.scalar_tensor_tensor(t_l, gl, 0.0, for_items(mask[:]), ALU.max, ALU.mult).then_inc(gs, 1)
                newton(g, nl, s["nl_exp"], s["nl_steps2"], nl[:, 3, :], 3).then_inc(s["nl_steps2"], 1)
                dve.wait_ge(s["nl_steps2"], g * 3 + 3)
                dve.tensor_scalar(nl[:, 5, :], nl[:, 3, :], c1(CAP_C), None, ALU.min).then_inc(s["r_ready"], 1)

                def v_low(b):
                    dve.wait_ge(s["v_h_ready"], g * GB + (b + 1))
                    dve.scalar_tensor_tensor(v_l[:, b, :], bank[b][:], V_DOWN, v_h[:, b, :], ALU.mult,
                                             ALU.subtract).then_inc(s["v_l_ready"], 1)

                v_low(0)
                fs = s["cf_steps"]
                dve.wait_ge(s["e_ready"], g + 1)
                dve.scalar_tensor_tensor(a_g, e_g, 1.0, for_items(mask[:]), ALU.min, ALU.mult).then_inc(gs, 1)
                dve.wait_ge(gs, g * 4 + 2)
                dve.tensor_reduce(cf[:, 6, :], a_g, AX.X, ALU.add).then_inc(gs, 1)
                dve.wait_ge(gs, g * 4 + 3)
                dve.tensor_scalar(cf[:, 6, :], cf[:, 6, :], ROW_EPS, None, ALU.max).then_inc(fs, 1)
                dve.wait_ge(fs, g * 6 + 1)
                dve.reciprocal(cf[:, 6, :], cf[:, 6, :]).then_inc(fs, 1)
                dve.wait_ge(fs, g * 6 + 2)
                dve.tensor_scalar(cf[:, 7, :], cf[:, 6, :], c1(W_G), None, ALU.mult).then_inc(s["cf_ready"], 1)
                v_low(1)
                dve.wait_ge(s["rm_ps"], g + 1)
                dve.tensor_tensor(a_l, t_l, bank[7][:].rearrange("p (b n) -> p b n", b=GB), ALU.mult).then_inc(gs, 1)
                dve.wait_ge(gs, g * 4 + 4)
                dve.tensor_reduce(cf[:, 2, :], a_l, AX.X, ALU.add).then_inc(fs, 1)
                dve.wait_ge(fs, g * 6 + 3)
                dve.tensor_tensor(cf[:, 4, :], cf[:, 2, :], nl[:, 5, :], ALU.mult).then_inc(fs, 1)
                dve.wait_ge(fs, g * 6 + 4)
                dve.tensor_scalar(cf[:, 4, :], cf[:, 4, :], ROW_EPS, None, ALU.max).then_inc(fs, 1)
                dve.wait_ge(fs, g * 6 + 5)
                dve.reciprocal(cf[:, 5, :], cf[:, 4, :]).then_inc(fs, 1)
                dve.wait_ge(fs, g * 6 + 6)
                dve.scalar_tensor_tensor(cf[:, 3, :], cf[:, 5, :], c1(W_L), nl[:, 5, :], ALU.mult,
                                         ALU.mult).then_inc(s["cl_ready"], 1)
                dve.wait_ge(s["cl_ready"], g + 1)
                dve.wait_ge(s["kg_ready"], g + 1)
                for b in range(GB):
                    last = dve.scalar_tensor_tensor(k_mix[:, b, :], a_l[:, b, :], cf[:, 3, b:b + 1], k_g[:, b, :],
                                                    ALU.mult, ALU.add)
                last.then_inc(s["k_ready"], 1)
                v_low(2)
                v_low(3)
                dve.wait_ge(s["kT_h_ready"], g + 1)
                dve.scalar_tensor_tensor(kT_l, bank[6][:].rearrange("p (b n) -> p b n", b=GB), K_UP, kT_h, ALU.mult,
                                         ALU.subtract).then_inc(s["kT_l_ready"], 1)
                if has_next:
                    for b in range(GB):
                        hT_low(g + 1, b)
                second_residual(g, slot, has_previous)
                if has_second:
                    x_low(g + 2)

            residual(0)
            first_norm(0, 0)
            for b in range(GB):
                hT_low(0, b)
            x_low(1)
            body(0, 0, True, True, False)
            with dve.Fori(0, NG // 2 - 2) as j:
                for t in (1, 2):
                    body(j * 2 + t, t % 2, True, True, True)
            body(NG - 3, (NG - 3) % 2, True, True, True)
            body(NG - 2, (NG - 2) % 2, True, False, True)
            body(NG - 1, (NG - 1) % 2, False, False, True)
            second_norm(NG - 1)


def kernel(**inputs):
    import numpy as np
    import concourse.bacc as bacc
    from concourse.bass_utils import run_bass_kernel_spmd as run

    f = {n: np.asarray(a) for n, a in inputs.items()}
    arrays = {
        "x": np.ascontiguousarray(f["x"]),
        "adj": np.ascontiguousarray(f["adj"]),
        "bias": np.ascontiguousarray(f["L0_gnn_bias"].reshape(-1, 1)),
        "w_lang_t": np.ascontiguousarray(f["L1_gnn_W_lang"].T),
        "w_grav_t": np.ascontiguousarray(f["L1_gnn_W_grav"].T),
        "w_v": np.ascontiguousarray(f["L1_gnn_W_V"]),
        "w_o_t": np.ascontiguousarray(f["L1_gnn_W_O"].T),
        "gate_logit": np.ascontiguousarray(f["L1_gnn_gate_logit"].reshape(1, 1)),
        "log_sigma": np.ascontiguousarray(f["L1_gnn_log_sigma"].reshape(1, 1)),
    }
    nc = bacc.Bacc("TRN2", target_bir_lowering=False, num_devices=1)
    args = [nc.dram_tensor(f"in_{n}", a.shape, mybir.dt.from_np(a.dtype), kind="ExternalInput").ap()
            for n, a in arrays.items()]
    res = nc.dram_tensor("out_dram", arrays["x"].shape, F32, kind="ExternalOutput").ap()
    build(nc, *args, res)
    r = run(nc, [{f"in_{n}": a for n, a in arrays.items()}], core_ids=[0])
    return r.results[0]["out_dram"]
```

```python
from contextlib import ExitStack

import concourse.bass as bass
from concourse import mybir

F32 = mybir.dt.float32
F16 = mybir.dt.float16
I32 = mybir.dt.int32
ALU = mybir.AluOpType
ACT = mybir.ActivationFunctionType
AX = mybir.AxisListType
ABSMAX = bass.bass_isa.ReduceOp.absmax

P = 128
EXPONENT = 0x7F800000


def wait(eng, sem, value):
    if not isinstance(value, int) or value > 0:
        eng.wait_ge(sem, value)


def build(nc, x, adj, bias, wlT, wgT, wv, woT, gate, log_sigma, out):
    B, L, NODES = x.shape
    assert L == P and NODES % P == 0
    KB = NODES // P
    GB = 4
    NG = B // GB
    K_NEAR = max(int(NODES * 0.3), 1)
    ROUNDS = K_NEAR // 8
    LAST = K_NEAR % 8
    CB = 8
    NC = B // CB
    LG = P // CB
    CL = L // LG
    HALF = CL // 2
    SLOTS = 3
    assert NG % 2 == 0 and NG >= 4 and NC > SLOTS and CL % 4 == 0 and LAST > 0
    N4 = GB * P

    X_HAT = 2.0 ** 12
    S_SCALE = 1.0 / (X_HAT * X_HAT * B)
    X_UP, W_UP, A_UP, H_UP, K_UP = 2.0 ** 13, 2.0 ** 14, 2.0 ** 12, 2.0 ** 8, 2.0 ** 14
    XW_DOWN, Z_DOWN, VO_DOWN, V_DOWN = 2.0 ** -17, 2.0 ** -16, 2.0 ** -22, 2.0 ** -16
    ALPHA = 1.0 / (X_UP * W_UP * XW_DOWN * A_UP)
    Z_UNIT = 1.0 / (H_UP * W_UP * Z_DOWN)
    BETA = 1.0 / (H_UP * W_UP * W_UP * VO_DOWN * W_UP * V_DOWN * K_UP)
    TAKEN, SELF, PAD = -1e30, -2e30, -3e30
    NORM_EPS, LN_EPS, ROW_EPS = 1e-12, 1e-5, 1e-8

    x_chunk = x.rearrange("(c b) (g l) n -> c (b g) l n", b=CB, g=LG)
    x_group = x.rearrange("(g b) l n -> g l b n", b=GB)
    out_group = out.rearrange("(g b) l n -> g l b n", b=GB)

    with ExitStack() as ctx:
        def sb(name, shape, dt=F32):
            return ctx.enter_context(nc.sbuf_tensor(name, shape, dt))

        def sem(name):
            return ctx.enter_context(nc.semaphore(name))

        bank = [ctx.enter_context(nc.psum_tensor(f"bank{i}", [P, 512], F32)) for i in range(8)]

        ident = sb("ident", [P, P])
        ones = sb("ones", [P, P])
        minus_half = sb("minus_half", [P, P])
        same_item = sb("same_item", [P, P])
        self_mark = sb("self_mark", [P, P])
        mask = sb("mask", [P, P])
        adj_sb = sb("adj_sb", [P, P])
        adj_h = sb("adj_h", [P, P], F16)
        adj_l = sb("adj_l", [P, P], F16)
        bias_c = sb("bias_c", [P, 1])
        gate_c = sb("gate_c", [P, 1])
        ls_c = sb("ls_c", [P, 1])
        chunk_max = sb("chunk_max", [P, NC])
        magn = sb("magn", [P, 8])
        magn_all = sb("magn_all", [P, 8])
        pw = sb("pw", [P, 8])
        ipw = sb("ipw", [P, 8])
        vo_scale = sb("vo_scale", [P, 4])
        vo_magn = sb("vo_magn", [P, 2])
        up = sb("up", [P, 8])
        col = sb("col", [P, 16])
        D_MAX, D_POW, D_INV, ALPHA_C, CAP_C, KAPPA, W_L, W_G, BETA_C, T0, T1, HK = range(12)
        c1 = lambda i: col[:, i:i + 1]
        dinv_col = sb("dinv_col", [P, KB])
        top8 = sb("top8", [P, KB, 8])
        stats = sb("stats", [P, GB, 6])
        stats2 = sb("stats2", [P, GB, 6])
        mv = sb("mv", [P, GB, 2])
        mv2 = sb("mv2", [P, GB, 2])
        ln1 = sb("ln1", [P, 5, GB])
        ln2 = sb("ln2", [P, 5, GB])
        nl = sb("nl", [P, 6, GB])
        cf = sb("cf", [P, 8, GB])

        KIB = 1024
        arena = sb("arena", [P, 198 * KIB // 4])

        def at(start, free, dt=F32):
            size = (2 if dt == F16 else 4)
            n = 1
            for d in free:
                n *= d
            flat = arena[:, start // 4:(start + n * size) // 4]
            if dt == F16:
                flat = flat.bitcast(F16)
            if len(free) == 1:
                return flat
            names = "abcd"[:len(free)]
            spec = f"p ({' '.join(names)}) -> p {' '.join(names)}"
            return flat.rearrange(spec, **dict(zip(names, free)))

        TILES = B * L // P
        xn_h = at(0, [TILES, NODES], F16)
        xn_l = at(64 * KIB, [TILES, NODES], F16)
        xc = [at(k * KIB, [CL, NODES]) for k in (128, 144, 176)]
        sq = at(160 * KIB, [CL, NODES])
        S = at(176 * KIB, [KB, NODES])
        work = at(184 * KIB, [KB, NODES + 8])
        row = [at((193 + 2 * i) * KIB - KIB // 2, [NODES]) for i in range(2)]
        ssum, nrm = row
        rinv = sb("rinv", [P, NODES])
        wT_h = [at((128 + 8 * i) * KIB, [KB, NODES], F16) for i in range(3)]
        wT_l = [at((132 + 8 * i) * KIB, [KB, NODES], F16) for i in range(3)]
        an_h = at(152 * KIB, [KB, NODES], F16)
        an_l = at(156 * KIB, [KB, NODES], F16)
        w_raw = [at(160 * KIB, [KB, NODES]), at(168 * KIB, [KB, NODES]),
                 at(88 * KIB, [KB, NODES]), at(96 * KIB, [KB, NODES])]
        A = work[:, :, 0:NODES]
        squares = at(120 * KIB, [KB, NODES])
        vo_h = [at(104 * KIB, [KB, NODES], F16), at(112 * KIB, [KB, NODES], F16)]
        vo_l = [at(108 * KIB, [KB, NODES], F16), at(116 * KIB, [KB, NODES], F16)]
        vo_raw = at(120 * KIB, [KB, NODES])
        vo_squares = at(80 * KIB, [KB, NODES])
        deg_m = at(168 * KIB, [NODES])
        deg_t = at(170 * KIB, [NODES])
        deg_u = at(172 * KIB, [NODES])
        dinv = at(174 * KIB, [NODES])
        xg = at(0, [GB, NODES])
        x_h = at(8 * KIB, [GB, NODES], F16)
        x_l = at(12 * KIB, [GB, NODES], F16)
        xw_h = at(16 * KIB, [GB, KB, P], F16)
        xw_l = at(20 * KIB, [GB, KB, P], F16)
        y = at(24 * KIB, [GB, NODES])
        h = [at(32 * KIB, [GB, NODES]), at(40 * KIB, [GB, NODES])]
        hT_h = at(48 * KIB, [KB, GB, P], F16)
        hT_l = at(52 * KIB, [KB, GB, P], F16)
        z_h = [at(56 * KIB, [KB, GB, P], F16), at(64 * KIB, [KB, GB, P], F16)]
        z_l = [at(60 * KIB, [KB, GB, P], F16), at(68 * KIB, [KB, GB, P], F16)]
        v_h = at(72 * KIB, [GB, NODES], F16)
        v_l = at(76 * KIB, [GB, NODES], F16)
        y2 = at(80 * KIB, [GB, NODES])
        tile_at = iter(range(88 * KIB, 110 * KIB, 2 * KIB))
        diag_l, diag_g, diag_r, t_l, a_l, e_g, a_g, k_g, k_mix = (
            at(next(tile_at), [GB, P]) for _ in range(9))
        kT_h = at(108 * KIB, [GB, P], F16)
        kT_l = at(109 * KIB, [GB, P], F16)

        names = """consts_made const_steps small_in bias_in
            sq_ready ssum_ready nrm_ps nrm_in nrm_ready rinv_ready xn_ready xn_h_ready xn_l_ready gram_ps
            S_ready S_turned work_ready pick_steps A_ready stream_done
            w_in0 w_in1 w_in2 w_in3 magn_ready magn_x magn_all_ready magn_guarded magn_root scale_steps scale_ready
            adj_h_ready adj_l_ready w_scaled vo_out vo_magn_ready vo_magn_all vo_guarded vo_root vo_steps vo_up w_h_ready w_l_ready vo_ps vo_scaled
            deg_ps deg_steps deg_in deg_root d_ready an_h_ready an_l_ready an_f
            col_exp col_steps col_ready
            x_in x_h_ready x_l_ready xw_ps xw_h_ready xw_l_ready mix_ps mixed y_ready stats_ready
            ln1_var ln1_log ln1_exp ln1_steps h_ready hT_ps hT_h_ready hT_l_ready
            zl_ps zl_h_ready zl_l_ready zg_ps zg_h_ready zg_l_ready
            gl_ps gg_ps nl_in nl_log nl_exp nl_steps r_ready dr_ready dg_ready
            sq_ps rm_ps hk_ready e_ready graph_steps cf_steps cf_ready k_ready kg_ready cl_ready
            v_ps v_h_ready v_l_ready kT_ps kT_h_ready kT_l_ready out_ps y2_ready
            ln2_var ln2_log ln2_exp ln2_steps o_ready stored stats2_ready nl_steps2 stat1_steps stat2_steps""".split()
        s = {n: sem(n) for n in names}
        x_loaded = [sem(f"x_loaded{i}") for i in range(SLOTS)]

        def three(pe, dst, ah, al, bh, bl, start, stop):
            pe.matmul(dst, ah, bh, start=start, stop=False)
            pe.matmul(dst, ah, bl, start=False, stop=False)
            return pe.matmul(dst, al, bh, start=False, stop=stop)

        def per_item(c):
            return c.unsqueeze(2).broadcast_to([P, GB, P])

        def for_items(m):
            return m.unsqueeze(1).broadcast_to([P, GB, P])

        block = ctx.enter_context(nc.Block())

        @block.sync
        def _(sp):
            for c in range(SLOTS):
                sp.dma_start(xc[c], x_chunk[c]).then_inc(x_loaded[c], 16)
            sp.dma_start(adj_sb[:], adj).then_inc(s["small_in"], 16)
            sp.dma_start(bias_c[:], bias).then_inc(s["small_in"], 16)
            sp.dma_start(gate_c[:], gate.broadcast_to([P, 1])).then_inc(s["small_in"], 16)
            sp.dma_start(ls_c[:], log_sigma.broadcast_to([P, 1])).then_inc(s["small_in"], 16)
            for c in range(SLOTS, NC):
                sp.wait_ge(s["xn_l_ready"], 2 * (c - SLOTS + 1))
                sp.dma_start(xc[c % SLOTS], x_chunk[c]).then_inc(x_loaded[c % SLOTS], 16)
            sp.wait_ge(s["ssum_ready"], NC)
            sp.dma_start(w_raw[0], wlT.rearrange("(k p) e -> p k e", p=P)).then_inc(s["w_in0"], 16)
            sp.dma_start(w_raw[1], wgT.rearrange("(k p) e -> p k e", p=P)).then_inc(s["w_in1"], 16)
            sp.wait_ge(s["gram_ps"], 4)
            sp.dma_start(w_raw[2], wv.rearrange("(k p) e -> p k e", p=P)).then_inc(s["w_in2"], 16)
            sp.dma_start(w_raw[3], woT.rearrange("(k p) e -> p k e", p=P)).then_inc(s["w_in3"], 16)
            sp.dma_start(xg, x_group[0]).then_inc(s["x_in"], 16)

            def load_x(g):
                sp.wait_ge(s["y_ready"], g * GB)
                sp.wait_ge(s["x_h_ready"], g)
                sp.wait_ge(s["x_l_ready"], g)
                sp.dma_start(xg, x_group[g]).then_inc(s["x_in"], 16)

            def store(g):
                sp.wait_ge(s["o_ready"], g * GB + GB)
                sp.dma_start(out_group[g], y2).then_inc(s["stored"], 16)

            load_x(1)
            load_x(2)
            with sp.Fori(0, NG - 3) as g:
                load_x(g + 3)
                store(g)
            for g in range(NG - 3, NG):
                store(g)
            sp.wait_ge(s["stored"], 16 * NG)

        @block.gpsimd
        def _(pool):
            cs = s["const_steps"]
            pool.memset(ident[:], 0.0).then_inc(cs, 1)
            pool.memset(same_item[:], 1.0).then_inc(cs, 1)
            pool.memset(ones[:], 1.0).then_inc(cs, 1)
            pool.memset(minus_half[:], -0.5).then_inc(cs, 1)
            pool.memset(self_mark[:], 0.0).then_inc(cs, 1)
            pool.memset(magn[:], 1.0).then_inc(cs, 1)
            pool.wait_ge(cs, 6)
            pool.affine_select(out=ident[:], in_=ident[:], compare_op=ALU.not_equal, fill=1.0, base=0,
                               pattern=[[-1, P]], channel_multiplier=1).then_inc(s["consts_made"], 1)
            pool.affine_select(out=self_mark[:], in_=self_mark[:], compare_op=ALU.not_equal, fill=SELF, base=0,
                               pattern=[[-1, P]], channel_multiplier=1).then_inc(s["consts_made"], 1)
            si = same_item[:].rearrange("p (b g) -> p b g", g=LG)
            pool.affine_select(out=si, in_=si, compare_op=ALU.is_ge, fill=0.0, base=0,
                               pattern=[[-LG, CB], [0, LG]], channel_multiplier=1).then_inc(cs, 1)
            pool.wait_ge(cs, 7)
            pool.affine_select(out=si, in_=si, compare_op=ALU.is_ge, fill=0.0, base=LG - 1,
                               pattern=[[LG, CB], [0, LG]], channel_multiplier=-1).then_inc(s["consts_made"], 1)
            pool.wait_ge(s["small_in"], 64)
            pool.affine_select(out=mask[:], in_=adj_sb[:], compare_op=ALU.not_equal, fill=0.0, base=0,
                               pattern=[[-1, P]], channel_multiplier=1).then_inc(s["consts_made"], 1)

            for c in range(NC):
                for half in range(2):
                    t = slice(half * HALF, (half + 1) * HALF)
                    o = slice(c * CL + half * HALF, c * CL + (half + 1) * HALF)
                    pool.wait_ge(s["xn_h_ready"], 2 * c + half + 1)
                    pool.tensor_tensor(xn_l[:, o, :], xc[c % SLOTS][:, t, :], xn_h[:, o, :],
                                       ALU.subtract).then_inc(s["xn_l_ready"], 1)

            pool.wait_ge(s["magn_ready"], 5)
            pool.wait_ge(s["magn_x"], 1)
            pool.partition_all_reduce(magn_all[:], magn[:], P, ABSMAX).then_inc(s["magn_all_ready"], 1)
            pool.wait_ge(s["adj_h_ready"], 2)
            pool.tensor_tensor(adj_l[:], adj_sb[:], adj_h[:], ALU.subtract).then_inc(s["adj_l_ready"], 1)
            for i, (raw, hi, lo) in enumerate([(w_raw[0], wT_h[0], wT_l[0]), (w_raw[1], wT_h[1], wT_l[1]),
                                               (w_raw[2], vo_h[0], vo_l[0]), (w_raw[3], vo_h[1], vo_l[1])]):
                pool.wait_ge(s["w_h_ready"], i + 1)
                pool.tensor_tensor(lo, raw, hi, ALU.subtract).then_inc(s["w_l_ready"], 1)
            pool.wait_ge(s["vo_magn_ready"], 1)
            pool.partition_all_reduce(vo_magn[:, 1:2], vo_magn[:, 0:1], P, ABSMAX).then_inc(s["vo_magn_all"], 1)
            pool.wait_ge(s["vo_magn_all"], 1)
            pool.tensor_scalar(vo_magn[:, 1:2], vo_magn[:, 1:2], 1e-30, None, ALU.max).then_inc(s["vo_guarded"], 1)
            pool.wait_ge(s["w_h_ready"], 5)
            pool.tensor_tensor(wT_l[2], vo_raw, wT_h[2], ALU.subtract).then_inc(s["w_l_ready"], 1)

            def graphs(g):
                pool.wait_ge(s["r_ready"], g + 1)
                wait(pool, s["rm_ps"], g)
                pool.tensor_tensor(diag_r, for_items(ident[:]), per_item(nl[:, 5, :]),
                                   ALU.mult).then_inc(s["dr_ready"], 1)
                pool.wait_ge(s["cf_ready"], g + 1)
                wait(pool, s["k_ready"], g)
                pool.tensor_tensor(k_g, a_g, per_item(cf[:, 7, :]), ALU.mult).then_inc(s["kg_ready"], 1)

            graphs(0)
            with pool.Fori(1, NG) as g:
                graphs(g)

        @block.tensor
        def _(pe):
            pe.wait_ge(s["consts_made"], 3)

            def item_sums(c):
                pe.wait_ge(s["ssum_ready"], c + 1)
                wait(pe, s["nrm_in"], c)
                pe.matmul(bank[7][:], same_item[:], ssum, start=True, stop=True).then_inc(s["nrm_ps"], 1)

            def gram(c, half, rows, first=False, last=False):
                for t in range(half * HALF, (half + 1) * HALF):
                    for r in rows:
                        o = bass.ds(c * CL + t, 1) if not isinstance(c, int) else slice(c * CL + t, c * CL + t + 1)
                        xh = xn_h[:, o, :].rearrange("p a n -> p (a n)")
                        xl = xn_l[:, o, :].rearrange("p a n -> p (a n)")
                        begin = first and t == 0
                        end = last and t == CL - 1
                        mm = three(pe, bank[r][:, 0:NODES - r * P],
                                   xh[:, r * P:(r + 1) * P], xl[:, r * P:(r + 1) * P],
                                   xh[:, r * P:], xl[:, r * P:], start=begin, stop=end)
                        if end:
                            mm.then_inc(s["gram_ps"], 1)

            def turn(dst, i, j):
                return pe.transpose(dst, S[:, i, j * P:(j + 1) * P], ident[:])

            def rows_01(c, half, first=False, last=False):
                pe.wait_ge(s["xn_l_ready"], c * 2 + (half + 1))
                gram(c, half, (0, 1), first, last)

            item_sums(0)
            item_sums(1)
            rows_01(0, 0, first=True)
            with pe.Fori(1, NC - 1) as c:
                item_sums(c + 1)
                rows_01(c - 1, 1)
                rows_01(c, 0)
            rows_01(NC - 2, 1)
            rows_01(NC - 1, 0)
            rows_01(NC - 1, 1, last=True)
            pe.wait_ge(s["S_ready"], 2)
            turn(bank[4][:, 0:P], 0, 1).then_inc(s["S_turned"], 1)
            turn(bank[5][:, 0:P], 0, 2)
            turn(bank[5][:, P:2 * P], 1, 2).then_inc(s["S_turned"], 1)
            turn(bank[6][:, 0:P], 0, 3)
            turn(bank[6][:, P:2 * P], 1, 3).then_inc(s["S_turned"], 1)
            for r in range(2, KB):
                for half in range(2):
                    gram(0, half, (r,), first=True)
                with pe.Fori(1, NC - 1) as c:
                    for half in range(2):
                        gram(c, half, (r,))
                for half in range(2):
                    gram(NC - 1, half, (r,), last=True)
            pe.wait_ge(s["S_ready"], 6)
            turn(bank[7][:, 0:P], 2, 3).then_inc(s["S_turned"], 1)

            pe.wait_ge(s["w_l_ready"], 4)
            for d in range(KB):
                for f in range(KB):
                    mm = three(pe, bank[d][:], vo_h[0][:, f, d * P:(d + 1) * P], vo_l[0][:, f, d * P:(d + 1) * P],
                               vo_h[1][:, f, :], vo_l[1][:, f, :], start=(f == 0), stop=(f == KB - 1))
                mm.then_inc(s["vo_ps"], 1)

            def project_x(g):
                pe.wait_ge(s["x_l_ready"], g + 1)
                for b in range(GB):
                    wait(pe, s["zl_l_ready"], g * GB - GB + (b + 1) if not isinstance(g, int) or g > 0 else 0)
                    for k in range(KB):
                        mm = three(pe, bank[b][:, k * P:(k + 1) * P],
                                   x_h[:, b, k * P:(k + 1) * P], x_l[:, b, k * P:(k + 1) * P],
                                   adj_h[:], adj_l[:], start=True, stop=True)
                    mm.then_inc(s["xw_ps"], 1)

            def mix_nodes(g):
                for b in range(GB):
                    pe.wait_ge(s["xw_l_ready"], g * GB + (b + 1))
                    wait(pe, s["zg_l_ready"], g * GB - GB + (b + 1) if not isinstance(g, int) or g > 0 else 0)
                    for k in range(KB):
                        mm = three(pe, bank[b][:], xw_h[:, b, k, :], xw_l[:, b, k, :],
                                   an_h[:, k, :], an_l[:, k, :], start=(k == 0), stop=(k == KB - 1))
                    mm.then_inc(s["mix_ps"], 1)

            h_bank = [bank[4], bank[5], bank[7], bank[4]]

            def turn_h(g, slot, b):
                pe.wait_ge(s["h_ready"], g * GB + (b + 1))
                if b == 3:
                    pe.wait_ge(s["hT_l_ready"], g * GB + 1)
                for k in range(KB):
                    mm = pe.transpose(h_bank[b][:, k * P:(k + 1) * P], h[slot][:, b, k * P:(k + 1) * P], ident[:])
                mm.then_inc(s["hT_ps"], 1)

            def project_z(g, i, freed, done):
                for e in range(KB):
                    wait(pe, freed[0], freed[1] + (e + 1))
                    for k in range(KB):
                        mm = three(pe, bank[e][:], wT_h[i][:, k, e * P:(e + 1) * P], wT_l[i][:, k, e * P:(e + 1) * P],
                                   hT_h[:, k, :, :], hT_l[:, k, :, :], start=(k == 0), stop=(k == KB - 1))
                    mm.then_inc(done, 1)

            def inner_products(g, i, done):
                for b in range(GB):
                    for e in range(KB):
                        mm = three(pe, bank[4 + i][:, b * P:(b + 1) * P], z_h[i][:, e, b, :], z_l[i][:, e, b, :],
                                   z_h[i][:, e, b, :], z_l[i][:, e, b, :],
                                   start=(b == 0 and e == 0), stop=(b == GB - 1 and e == KB - 1))
                mm.then_inc(done, 1)

            def values(g, b, last_group):
                if last_group:
                    pe.wait_ge(s["zg_l_ready"], g * GB + (b + 1))
                else:
                    pe.wait_ge(s["mixed"], g * GB + GB + (b + 1))
                for k in range(KB):
                    mm = three(pe, bank[b][:], hT_h[:, k, b, :], hT_l[:, k, b, :],
                               wT_h[2][:, k, :], wT_l[2][:, k, :], start=(k == 0), stop=(k == KB - 1))
                mm.then_inc(s["v_ps"], 1)

            def weighted(g, b):
                pe.wait_ge(s["v_l_ready"], g * GB + (b + 1))
                three(pe, bank[b][:], kT_h[:, b, :], kT_l[:, b, :], v_h[:, b, :], v_l[:, b, :],
                      start=True, stop=True).then_inc(s["out_ps"], 1)

            def body(g, slot, has_next):
                pe.wait_ge(s["hT_l_ready"], g * GB + GB)
                if isinstance(g, int) and g == 0:
                    project_z(g, 0, (s["mixed"], 0), s["zl_ps"])
                else:
                    project_z(g, 0, (s["y2_ready"], g * GB - GB), s["zl_ps"])
                if has_next:
                    project_x(g + 1)
                    project_z(g, 1, (s["xw_l_ready"], g * GB + GB), s["zg_ps"])
                    mix_nodes(g + 1)
                else:
                    project_z(g, 1, (s["zl_l_ready"], g * GB), s["zg_ps"])
                pe.wait_ge(s["zg_l_ready"], g * GB + GB)
                inner_products(g, 1, s["gg_ps"])
                inner_products(g, 0, s["gl_ps"])
                pe.wait_ge(s["w_l_ready"], 5)
                values(g, 0, not has_next)
                pe.wait_ge(s["dg_ready"], g * 2 + 2)
                pe.matmul(bank[5][:], minus_half[:], diag_g, start=False, stop=True,
                          skip_group_check=True).then_inc(s["sq_ps"], 1)
                values(g, 1, not has_next)
                pe.wait_ge(s["dr_ready"], g + 1)
                pe.matmul(bank[7][:], ones[:], diag_r, start=True, stop=True).then_inc(s["rm_ps"], 1)
                values(g, 2, not has_next)
                values(g, 3, not has_next)
                pe.wait_ge(s["k_ready"], g + 1)
                wait(pe, s["kT_l_ready"], g)
                for b in range(GB):
                    mm = pe.transpose(bank[6][:, b * P:(b + 1) * P], k_mix[:, b, :], ident[:])
                mm.then_inc(s["kT_ps"], 1)
                if has_next:
                    for b in range(3):
                        turn_h(g + 1, 1 - slot, b)
                pe.wait_ge(s["kT_l_ready"], g + 1)
                weighted(g, 0)
                if has_next:
                    turn_h(g + 1, 1 - slot, 3)
                weighted(g, 1)
                weighted(g, 2)
                weighted(g, 3)

            pe.wait_ge(s["vo_out"], KB)
            pe.wait_ge(s["adj_l_ready"], 1)
            project_x(0)
            for i in range(KB):
                pe.wait_ge(s["A_ready"], i + 1)
                mm = pe.matmul(bank[7][:], ones[:], A[:, i, :], start=(i == 0), stop=(i == KB - 1))
            mm.then_inc(s["deg_ps"], 1)
            pe.wait_ge(s["an_l_ready"], KB)
            mix_nodes(0)
            for b in range(GB):
                turn_h(0, 0, b)
            body(0, 0, True)
            with pe.Fori(0, NG // 2 - 1) as j:
                for t in (1, 2):
                    body(j * 2 + t, t % 2, True)
            body(NG - 1, (NG - 1) % 2, False)

        @block.scalar
        def _(act):
            def square(c):
                act.wait_ge(x_loaded[c % SLOTS], 16 * (c // SLOTS + 1))
                wait(act, s["ssum_ready"], c)
                act.activation(sq, xc[c % SLOTS], ACT.Square).then_inc(s["sq_ready"], 1)

            def root(c):
                act.wait_ge(s["nrm_in"], c + 1)
                act.activation(nrm, nrm, ACT.Sqrt).then_inc(s["nrm_ready"], 1)

            def high(c, half):
                act.wait_ge(s["xn_ready"], 3 * c + (1, 3)[half])
                act.activation(xn_h[:, c * CL + half * HALF:c * CL + (half + 1) * HALF, :],
                               xc[c % SLOTS][:, half * HALF:(half + 1) * HALF, :],
                               ACT.Copy).then_inc(s["xn_h_ready"], 1)

            square(0)
            root(0)
            for c in range(NC):
                if c + 1 < NC:
                    square(c + 1)
                high(c, 0)
                if c + 1 < NC:
                    root(c + 1)
                high(c, 1)

            def s_out(dst, src):
                act.activation(dst, src, ACT.Copy, scale=S_SCALE).then_inc(s["S_ready"], 1)

            act.wait_ge(s["gram_ps"], 2)
            act.wait_ge(s["xn_l_ready"], 2 * NC)
            s_out(S[:, 0, :], bank[0][:])
            s_out(S[:, 1, P:], bank[1][:, 0:NODES - P])
            act.wait_ge(s["S_turned"], 3)
            for dst, src in ((S[:, 1, 0:P], bank[4][:, 0:P]), (S[:, 2, 0:2 * P], bank[5][:, 0:2 * P]),
                             (S[:, 3, 0:2 * P], bank[6][:, 0:2 * P])):
                act.activation(dst, src, ACT.Copy).then_inc(s["S_ready"], 1)
            act.wait_ge(s["gram_ps"], 3)
            s_out(S[:, 2, 2 * P:], bank[2][:, 0:2 * P])
            act.wait_ge(s["gram_ps"], 4)
            s_out(S[:, 3, 3 * P:], bank[3][:, 0:P])
            act.wait_ge(s["S_turned"], 4)
            act.activation(S[:, 3, 2 * P:3 * P], bank[7][:, 0:P], ACT.Copy).then_inc(s["S_ready"], 1)

            act.wait_ge(s["consts_made"], 4)
            for i in range(4):
                act.wait_ge(s[f"w_in{i}"], 16)
                if i:
                    act.wait_ge(s["magn_ready"], i)
                act.activation(squares, w_raw[i], ACT.Square, accum_out=magn[:, i:i + 1]).then_inc(s["magn_ready"], 1)
            act.wait_ge(s["magn_ready"], 4)
            act.activation(squares[:, 0, 0:P], adj_sb[:], ACT.Square,
                           accum_out=magn[:, 4:5]).then_inc(s["magn_ready"], 1)
            act.wait_ge(s["magn_guarded"], 1)
            act.activation(magn_all[:], magn_all[:], ACT.Sqrt).then_inc(s["magn_root"], 1)

            act.wait_ge(s["scale_ready"], 1)
            act.activation(adj_sb[:], adj_sb[:], ACT.Copy, scale=up[:, 4:5]).then_inc(s["adj_h_ready"], 1)
            act.wait_ge(s["adj_h_ready"], 1)
            act.activation(adj_h[:], adj_sb[:], ACT.Copy).then_inc(s["adj_h_ready"], 1)
            for i, hi in enumerate([wT_h[0], wT_h[1], vo_h[0], vo_h[1]]):
                act.activation(w_raw[i], w_raw[i], ACT.Copy, scale=up[:, i:i + 1]).then_inc(s["w_scaled"], 1)
                act.wait_ge(s["w_scaled"], i + 1)
                act.activation(hi, w_raw[i], ACT.Copy).then_inc(s["w_h_ready"], 1)

            def x_high(g):
                act.wait_ge(s["x_in"], g * 16 + 16)
                wait(act, s["xw_ps"], g * GB)
                act.activation(x_h, xg, ACT.Copy, scale=up[:, 5:6]).then_inc(s["x_h_ready"], 1)

            def xw_high(g):
                for b in range(GB):
                    act.wait_ge(s["xw_ps"], g * GB + (b + 1))
                    act.activation(xw_h[:, b, :, :], bank[b][:], ACT.Copy, scale=XW_DOWN).then_inc(s["xw_h_ready"], 1)

            def add_bias(g):
                for b in range(GB):
                    act.wait_ge(s["mix_ps"], g * GB + (b + 1))
                    wait(act, s["h_ready"], g * GB - GB + (b + 1) if not isinstance(g, int) or g > 0 else 0)
                    act.activation(y[:, b, :], bank[b][:], ACT.Identity, scale=c1(ALPHA_C),
                                   bias=bias_c[:]).then_inc(s["mixed"], 1)

            def log_exp(g, t, ready, logged, done):
                act.wait_ge(ready, g + 1)
                act.activation(t[:, 1, :], t[:, 0, :], ACT.Ln).then_inc(logged, 1)
                act.wait_ge(logged, g + 1)
                act.activation(t[:, 2, :], t[:, 1, :], ACT.Exp, scale=-0.5).then_inc(done, 1)

            x_high(0)
            for d in range(KB):
                act.wait_ge(s["vo_ps"], d + 1)
                act.activation(vo_raw[:, d, :], bank[d][:], ACT.Copy, scale=VO_DOWN).then_inc(s["vo_out"], 1)
            act.wait_ge(s["vo_out"], KB)
            act.activation(vo_squares, vo_raw, ACT.Square, accum_out=vo_magn[:, 0:1]).then_inc(s["vo_magn_ready"], 1)
            xw_high(0)
            act.wait_ge(s["vo_guarded"], 1)
            act.activation(vo_scale[:, 0:1], vo_magn[:, 1:2], ACT.Sqrt).then_inc(s["vo_root"], 1)
            act.wait_ge(s["deg_in"], 1)
            act.activation(deg_t, deg_m, ACT.Sqrt).then_inc(s["deg_root"], 1)
            for i in range(KB):
                act.wait_ge(s["an_f"], i + 1)
                act.activation(an_h[:, i, :], A[:, i, :], ACT.Copy).then_inc(s["an_h_ready"], 1)
            act.preload_act_table_set("natural_log_exp_and_others")
            act.wait_ge(s["small_in"], 64)
            act.activation(c1(T0), gate_c[:], ACT.Exp, scale=-1.0).then_inc(s["col_exp"], 1)
            act.activation(c1(T1), ls_c[:], ACT.Exp, scale=-2.0).then_inc(s["col_exp"], 1)
            act.wait_ge(s["d_ready"], 1)
            add_bias(0)
            log_exp(0, ln1, s["ln1_var"], s["ln1_log"], s["ln1_exp"])

            def hT_high(g, b):
                act.wait_ge(s["hT_ps"], g * GB + (b + 1))
                act.activation(hT_h[:, :, b, :], bank[(4, 5, 7, 4)[b]][:].rearrange("p (k n) -> p k n", k=KB),
                               ACT.Copy, scale=H_UP).then_inc(s["hT_h_ready"], 1)

            def body(g, slot, has_next, has_second, has_previous):
                def z_high(i, ps, done, e):
                    act.wait_ge(ps, g * GB + (e + 1))
                    act.activation(z_h[i][:, e, :, :], bank[e][:].rearrange("p (b n) -> p b n", b=GB), ACT.Copy,
                                   scale=Z_DOWN).then_inc(done, 1)

                for e in range(KB):
                    z_high(0, s["zl_ps"], s["zl_h_ready"], e)
                    if e == 1 and has_previous:
                        log_exp(g - 1, ln2, s["ln2_var"], s["ln2_log"], s["ln2_exp"])
                if has_next:
                    xw_high(g + 1)
                for e in range(KB):
                    z_high(1, s["zg_ps"], s["zg_h_ready"], e)
                if has_next:
                    add_bias(g + 1)
                    log_exp(g + 1, ln1, s["ln1_var"], s["ln1_log"], s["ln1_exp"])
                log_exp(g, nl, s["nl_in"], s["nl_log"], s["nl_exp"])

                def v_high(b):
                    act.wait_ge(s["v_ps"], g * GB + (b + 1))
                    act.activation(v_h[:, b, :], bank[b][:], ACT.Copy, scale=V_DOWN).then_inc(s["v_h_ready"], 1)

                v_high(0)
                act.wait_ge(s["sq_ps"], g + 1)
                act.wait_ge(s["hk_ready"], g + 1)
                wait(act, s["graph_steps"], g * 4)
                for b in range(GB):
                    ex = act.activation(e_g[:, b, :], bank[5][:, b * P:(b + 1) * P], ACT.Exp,
                                        scale=c1(KAPPA), bias=cf[:, 0, b:b + 1])
                ex.then_inc(s["e_ready"], 1)
                for b in range(1, GB):
                    v_high(b)
                act.wait_ge(s["kT_ps"], g + 1)
                act.activation(kT_h, bank[6][:].rearrange("p (b n) -> p b n", b=GB), ACT.Copy,
                               scale=K_UP).then_inc(s["kT_h_ready"], 1)
                if has_next:
                    for b in range(GB):
                        hT_high(g + 1, b)
                if has_second:
                    x_high(g + 2)

            for b in range(GB):
                hT_high(0, b)
            act.wait_ge(s["vo_up"], 1)
            act.activation(vo_raw, vo_raw, ACT.Copy, scale=vo_scale[:, 3:4]).then_inc(s["vo_scaled"], 1)
            act.wait_ge(s["vo_scaled"], 1)
            act.activation(wT_h[2], vo_raw, ACT.Copy).then_inc(s["w_h_ready"], 1)
            x_high(1)
            body(0, 0, True, True, False)
            with act.Fori(0, NG // 2 - 2) as j:
                for t in (1, 2):
                    body(j * 2 + t, t % 2, True, True, True)
            body(NG - 3, (NG - 3) % 2, True, True, True)
            body(NG - 2, (NG - 2) % 2, True, False, True)
            body(NG - 1, (NG - 1) % 2, False, False, True)
            log_exp(NG - 1, ln2, s["ln2_var"], s["ln2_log"], s["ln2_exp"])

        @block.vector
        def _(dve):
            def sum_squares(c):
                dve.wait_ge(s["sq_ready"], c + 1)
                wait(dve, s["nrm_ps"], c)
                dve.tensor_reduce(ssum, sq.rearrange("p l n -> p n l"), AX.X, ALU.add).then_inc(s["ssum_ready"], 1)

            def squared_norms(c):
                dve.wait_ge(s["nrm_ps"], c + 1)
                wait(dve, s["rinv_ready"], c)
                dve.tensor_scalar(nrm, bank[7][:], NORM_EPS * NORM_EPS, 0.0, ALU.max, ALU.max,
                                  accum_out=chunk_max[:, c:c + 1]).then_inc(s["nrm_in"], 1)

            def inverse_norms(c):
                dve.wait_ge(s["nrm_ready"], c + 1)
                wait(dve, s["xn_ready"], 3 * c)
                dve.reciprocal(rinv[:], nrm).then_inc(s["rinv_ready"], 1)

            def normalise(c, first, end):
                dve.wait_ge(s["rinv_ready"], c + 1)
                dve.wait_ge(s["sq_ready"], c + 1)
                t = xc[c % SLOTS][:, first:end, :]
                dve.scalar_tensor_tensor(t, t, X_HAT, rinv[:].unsqueeze(1).broadcast_to([P, end - first, NODES]),
                                         ALU.mult, ALU.mult).then_inc(s["xn_ready"], 1)

            sum_squares(0)
            squared_norms(0)
            inverse_norms(0)
            for c in range(NC):
                normalise(c, 0, HALF)
                if c + 1 < NC:
                    sum_squares(c + 1)
                normalise(c, HALF, HALF + HALF // 2)
                if c + 1 < NC:
                    squared_norms(c + 1)
                normalise(c, HALF + HALF // 2, CL)
                if c + 1 < NC:
                    inverse_norms(c + 1)
            dve.wait_ge(s["nrm_in"], NC)
            dve.tensor_reduce(magn[:, 5:6], chunk_max[:], AX.X, ALU.max).then_inc(s["magn_x"], 1)
            dve.wait_ge(s["xn_l_ready"], 2 * NC)
            dve.memset(work[:, :, NODES:], PAD).then_inc(s["work_ready"], 1)

            def fill_work(r, done):
                dve.wait_ge(s["S_ready"], done)
                dve.tensor_copy(work[:, r, 0:NODES], S[:, r, :]).then_inc(s["work_ready"], 1)
                dve.wait_ge(s["work_ready"], 1 + 2 * r + 1)
                dve.tensor_tensor(work[:, r, r * P:(r + 1) * P], work[:, r, r * P:(r + 1) * P], self_mark[:],
                                  ALU.add).then_inc(s["work_ready"], 1)

            PICKS = 4 * (ROUNDS + 1) + 2

            def pick(pair):
                r0 = 2 * pair
                base = pair * PICKS
                ps = s["pick_steps"]
                dve.wait_ge(s["work_ready"], 1 + 2 * (r0 + 2))
                for i in range(ROUNDS + 1):
                    n = base + 4 * i
                    for t in range(2):
                        wait(dve, ps, n - 1 + t if i > 0 else 0)
                        dve.max(top8[:, r0 + t, :], work[:, r0 + t, :]).then_inc(ps, 1)
                    n += 2
                    if i == ROUNDS:
                        for t in range(2):
                            dve.wait_ge(ps, n - 1 + t)
                            dve.memset(top8[:, r0 + t, LAST:], PAD).then_inc(ps, 1)
                        n += 2
                    for t in range(2):
                        dve.wait_ge(ps, n - 1 + t)
                        dve.match_replace(work[:, r0 + t, :], top8[:, r0 + t, :], work[:, r0 + t, :],
                                          TAKEN).then_inc(ps, 1)
                return base + PICKS

            def keep(pair, picked):
                for t in range(2):
                    r = 2 * pair + t
                    dve.wait_ge(s["pick_steps"], picked)
                    dve.scalar_tensor_tensor(A[:, r, :], work[:, r, 0:NODES], TAKEN, S[:, r, :],
                                             ALU.is_equal, ALU.mult).then_inc(s["A_ready"], 1)

            dve.wait_ge(s["consts_made"], 4)
            fill_work(0, 2)
            fill_work(1, 3)
            picked = pick(0)
            dve.wait_ge(s["magn_all_ready"], 1)
            ss = s["scale_steps"]
            dve.tensor_scalar(magn_all[:], magn_all[:], 1e-30, None, ALU.max).then_inc(s["magn_guarded"], 1)
            keep(0, picked)
            dve.wait_ge(s["magn_root"], 1)
            dve.tensor_scalar(magn_all[:], magn_all[:], 1.0, None, ALU.mult).then_inc(ss, 1)
            dve.wait_ge(ss, 1)
            dve.tensor_scalar(pw[:].bitcast(I32), magn_all[:].bitcast(I32), EXPONENT, None,
                              ALU.bitwise_and).then_inc(ss, 1)
            dve.wait_ge(ss, 2)
            dve.reciprocal(ipw[:], pw[:]).then_inc(ss, 1)
            dve.wait_ge(ss, 3)
            dve.tensor_scalar(up[:, 0:5], ipw[:, 0:5], W_UP, None, ALU.mult).then_inc(ss, 1)
            dve.tensor_scalar(up[:, 5:6], ipw[:, 5:6], X_UP, None, ALU.mult).then_inc(ss, 1)
            dve.wait_ge(ss, 5)
            dve.tensor_scalar(magn_all[:], magn_all[:], 1.0, None, ALU.mult).then_inc(s["scale_ready"], 1)

            fill_work(2, 6)
            fill_work(3, 8)
            picked = pick(1)
            keep(1, picked)

            def x_low(g):
                dve.wait_ge(s["x_h_ready"], g + 1)
                dve.scalar_tensor_tensor(x_l, xg, up[:, 5:6], x_h, ALU.mult,
                                         ALU.subtract).then_inc(s["x_l_ready"], 1)

            def xw_low(g):
                for b in range(GB):
                    dve.wait_ge(s["xw_h_ready"], g * GB + (b + 1))
                    dve.scalar_tensor_tensor(xw_l[:, b, :, :], bank[b][:].rearrange("p (k n) -> p k n", k=KB),
                                             XW_DOWN, xw_h[:, b, :, :], ALU.mult,
                                             ALU.subtract).then_inc(s["xw_l_ready"], 1)

            x_low(0)
            xw_low(0)
            ds_ = s["deg_steps"]
            dve.wait_ge(s["deg_ps"], 1)
            dve.tensor_scalar(deg_m, bank[7][:], 1e-34, None, ALU.max).then_inc(s["deg_in"], 1)
            dve.tensor_scalar(dinv, bank[7][:], 0.0, None, ALU.is_gt).then_inc(ds_, 1)
            vs = s["vo_steps"]
            dve.wait_ge(s["vo_root"], 1)
            dve.tensor_scalar(vo_scale[:, 1:2].bitcast(I32), vo_scale[:, 0:1].bitcast(I32), EXPONENT, None,
                              ALU.bitwise_and).then_inc(vs, 1)
            dve.wait_ge(vs, 1)
            dve.reciprocal(vo_scale[:, 2:3], vo_scale[:, 1:2]).then_inc(vs, 1)
            dve.wait_ge(vs, 2)
            dve.tensor_scalar(vo_scale[:, 3:4], vo_scale[:, 2:3], W_UP, None, ALU.mult).then_inc(s["vo_up"], 1)
            dve.wait_ge(s["deg_root"], 1)
            dve.reciprocal(deg_t, deg_t).then_inc(ds_, 1)
            dve.wait_ge(ds_, 2)
            dve.tensor_tensor(deg_u, deg_m, deg_t, ALU.mult).then_inc(ds_, 1)
            dve.wait_ge(ds_, 3)
            dve.scalar_tensor_tensor(deg_u, deg_u, -0.5, deg_t, ALU.mult, ALU.mult).then_inc(ds_, 1)
            dve.wait_ge(ds_, 4)
            dve.scalar_tensor_tensor(deg_t, deg_u, 1.5, deg_t, ALU.add, ALU.mult).then_inc(ds_, 1)
            dve.wait_ge(ds_, 5)
            dve.tensor_tensor(dinv, dinv, deg_t, ALU.mult).then_inc(ds_, 1)
            dve.wait_ge(ds_, 6)
            dve.tensor_reduce(c1(D_MAX), dinv, AX.X, ALU.max).then_inc(ds_, 1)
            dve.tensor_tensor(deg_u.rearrange("p (k n) -> p k n", k=KB), dinv.rearrange("p (k n) -> p k n", k=KB),
                              ident[:].unsqueeze(1).broadcast_to([P, KB, P]), ALU.mult).then_inc(ds_, 1)
            dve.wait_ge(ds_, 8)
            dve.tensor_reduce(dinv_col[:], deg_u.rearrange("p (k n) -> p k n", k=KB), AX.X,
                              ALU.add).then_inc(ds_, 1)
            dve.tensor_scalar(c1(D_MAX), c1(D_MAX), 1e-30, None, ALU.max).then_inc(ds_, 1)
            dve.wait_ge(ds_, 10)
            dve.tensor_scalar(c1(D_POW).bitcast(I32), c1(D_MAX).bitcast(I32), EXPONENT, None,
                              ALU.bitwise_and).then_inc(ds_, 1)
            dve.wait_ge(ds_, 11)
            dve.reciprocal(c1(D_INV), c1(D_POW)).then_inc(ds_, 1)
            dve.wait_ge(ds_, 12)
            dve.tensor_scalar(dinv, dinv, c1(D_INV), None, ALU.mult).then_inc(ds_, 1)
            dve.tensor_scalar(dinv_col[:], dinv_col[:], c1(D_INV), A_UP, ALU.mult, ALU.mult).then_inc(ds_, 1)
            dve.wait_ge(ds_, 14)
            for i in range(KB):
                dve.scalar_tensor_tensor(A[:, i, :], A[:, i, :], dinv_col[:, i:i + 1], dinv, ALU.mult,
                                         ALU.mult).then_inc(s["an_f"], 1)
            for i in range(KB):
                dve.wait_ge(s["an_h_ready"], i + 1)
                dve.tensor_tensor(an_l[:, i, :], A[:, i, :], an_h[:, i, :], ALU.subtract).then_inc(s["an_l_ready"], 1)
            cs = s["col_steps"]
            dve.scalar_tensor_tensor(c1(ALPHA_C), c1(D_POW), ALPHA, c1(D_POW), ALU.mult, ALU.mult).then_inc(cs, 1)
            dve.wait_ge(cs, 1)
            dve.scalar_tensor_tensor(c1(ALPHA_C), c1(ALPHA_C), pw[:, 4:5], pw[:, 5:6], ALU.mult,
                                     ALU.mult).then_inc(s["d_ready"], 1)
            dve.tensor_scalar(c1(CAP_C), pw[:, 0:1], Z_UNIT / ROW_EPS, None, ALU.mult).then_inc(cs, 1)
            dve.scalar_tensor_tensor(c1(BETA_C), pw[:, 2:3], BETA, pw[:, 3:4], ALU.mult, ALU.mult).then_inc(cs, 1)
            dve.scalar_tensor_tensor(c1(KAPPA), pw[:, 1:2], Z_UNIT * Z_UNIT, pw[:, 1:2], ALU.mult,
                                     ALU.mult).then_inc(cs, 1)
            dve.wait_ge(cs, 4)
            dve.tensor_tensor(c1(BETA_C), c1(BETA_C), vo_scale[:, 1:2], ALU.mult).then_inc(cs, 1)
            dve.wait_ge(s["col_exp"], 2)
            dve.tensor_tensor(c1(KAPPA), c1(KAPPA), c1(T1), ALU.mult).then_inc(cs, 1)
            dve.tensor_scalar(c1(W_G), c1(T0), 1.0, None, ALU.add).then_inc(cs, 1)
            dve.wait_ge(cs, 7)
            dve.tensor_scalar(c1(HK), c1(KAPPA), -0.5, None, ALU.mult).then_inc(cs, 1)
            dve.reciprocal(c1(W_L), c1(W_G)).then_inc(cs, 1)
            dve.wait_ge(cs, 9)
            dve.tensor_scalar(c1(W_G), c1(W_L), -1.0, 1.0, ALU.mult, ALU.add).then_inc(cs, 1)
            dve.wait_ge(cs, 10)

            def newton(g, t, exped, steps, dst, per):
                dve.wait_ge(exped, g + 1)
                dve.scalar_tensor_tensor(t[:, 3, :], t[:, 0, :], -0.5, t[:, 2, :], ALU.mult, ALU.mult).then_inc(steps, 1)
                dve.wait_ge(steps, g * per + 1)
                dve.tensor_tensor(t[:, 4, :], t[:, 3, :], t[:, 2, :], ALU.mult).then_inc(steps, 1)
                dve.wait_ge(steps, g * per + 2)
                return dve.scalar_tensor_tensor(dst, t[:, 4, :], 1.5, t[:, 2, :], ALU.add, ALU.mult)

            def moments(g, st, m, var, ready, ln):
                dve.wait_ge(s["consts_made"], 4)
                dve.wait_ge(ready, g * GB + GB)
                for b in range(GB):
                    ag = dve.bn_aggr(m[:, b, :], st[:, b, :])
                ag.then_inc(s["stats_ready"] if m is mv else s["stats2_ready"], 1)
                dve.wait_ge(s["stats_ready"] if m is mv else s["stats2_ready"], g + 1)
                dve.tensor_scalar(ln[:, 0, :], m[:, :, 1], LN_EPS, None, ALU.add).then_inc(var, 1)

            def norm_rows(g, src, dst, m, ln, exped, steps, per, done):
                newton(g, ln, exped, steps, ln[:, 3, :], per).then_inc(steps, 1)
                dve.wait_ge(steps, g * per + 3)
                for b in range(GB):
                    dve.tensor_scalar(dst[:, b, :], src[:, b, :], m[:, b, 0:1], ln[:, 3, b:b + 1], ALU.subtract,
                                      ALU.mult).then_inc(done, 1)

            def residual(g):
                for b in range(GB):
                    dve.wait_ge(s["mixed"], g * GB + (b + 1))
                    dve.tensor_tensor(y[:, b, :], y[:, b, :], xg[:, b, :], ALU.add).then_inc(s["y_ready"], 1)
                    if b:
                        dve.wait_ge(s["y_ready"], g * GB + b)
                        dve.bn_stats(stats[:, b - 1, :], y[:, b - 1, :]).then_inc(s["stat1_steps"], 1)
                dve.wait_ge(s["y_ready"], g * GB + GB)
                dve.bn_stats(stats[:, GB - 1, :], y[:, GB - 1, :]).then_inc(s["stat1_steps"], 1)
                moments(g, stats, mv, s["ln1_var"], s["stat1_steps"], ln1)

            def first_norm(g, slot):
                norm_rows(g, y, h[slot], mv, ln1, s["ln1_exp"], s["ln1_steps"], 3, s["h_ready"])

            def second_norm(g):
                norm_rows(g, y2, y2, mv2, ln2, s["ln2_exp"], s["ln2_steps"], 3, s["o_ready"])

            def second_residual(g, slot, has_previous):
                if has_previous:
                    dve.wait_ge(s["stored"], g * 16)
                for b in range(GB):
                    dve.wait_ge(s["out_ps"], g * GB + (b + 1))
                    dve.scalar_tensor_tensor(y2[:, b, :], bank[b][:], c1(BETA_C), h[slot][:, b, :], ALU.mult,
                                             ALU.add).then_inc(s["y2_ready"], 1)
                    if b:
                        dve.wait_ge(s["y2_ready"], g * GB + b)
                        dve.bn_stats(stats2[:, b - 1, :], y2[:, b - 1, :]).then_inc(s["stat2_steps"], 1)
                dve.wait_ge(s["y2_ready"], g * GB + GB)
                dve.bn_stats(stats2[:, GB - 1, :], y2[:, GB - 1, :]).then_inc(s["stat2_steps"], 1)
                moments(g, stats2, mv2, s["ln2_var"], s["stat2_steps"], ln2)

            def hT_low(g, b):
                dve.wait_ge(s["hT_h_ready"], g * GB + (b + 1))
                dve.scalar_tensor_tensor(hT_l[:, :, b, :], bank[(4, 5, 7, 4)[b]][:].rearrange("p (k n) -> p k n", k=KB),
                                         H_UP, hT_h[:, :, b, :], ALU.mult,
                                         ALU.subtract).then_inc(s["hT_l_ready"], 1)

            def body(g, slot, has_next, has_second, has_previous):
                def z_low(i, hi, done, e):
                    dve.wait_ge(hi, g * GB + (e + 1))
                    dve.scalar_tensor_tensor(z_l[i][:, e, :, :], bank[e][:].rearrange("p (b n) -> p b n", b=GB),
                                             Z_DOWN, z_h[i][:, e, :, :], ALU.mult,
                                             ALU.subtract).then_inc(done, 1)

                for e in range(KB):
                    z_low(0, s["zl_h_ready"], s["zl_l_ready"], e)
                    if e == 1 and has_previous:
                        second_norm(g - 1)
                if has_next:
                    xw_low(g + 1)
                for e in range(KB):
                    z_low(1, s["zg_h_ready"], s["zg_l_ready"], e)
                if has_next:
                    residual(g + 1)

                gl = bank[4][:].rearrange("p (b n) -> p b n", b=GB)
                gg = bank[5][:].rearrange("p (b n) -> p b n", b=GB)
                gs = s["graph_steps"]
                dve.wait_ge(s["gg_ps"], g + 1)
                dve.tensor_tensor(diag_g, gg, for_items(ident[:]), ALU.mult).then_inc(s["dg_ready"], 1)
                dve.wait_ge(s["dg_ready"], g * 2 + 1)
                dve.tensor_reduce(cf[:, 1, :], diag_g, AX.X, ALU.add).then_inc(s["dg_ready"], 1)
                dve.wait_ge(s["dg_ready"], g * 2 + 2)
                dve.tensor_scalar(cf[:, 0, :], cf[:, 1, :], c1(HK), None, ALU.mult).then_inc(s["hk_ready"], 1)
                if has_next:
                    first_norm(g + 1, 1 - slot)
                dve.wait_ge(s["gl_ps"], g + 1)
                dve.tensor_tensor(diag_l, gl, for_items(ident[:]), ALU.mult).then_inc(s["nl_steps"], 1)
                dve.wait_ge(s["nl_steps"], g * 2 + 1)
                dve.tensor_reduce(nl[:, 5, :], diag_l, AX.X, ALU.add).then_inc(s["nl_steps"], 1)
                dve.wait_ge(s["nl_steps"], g * 2 + 2)
                dve.tensor_scalar(nl[:, 0, :], nl[:, 5, :], 1e-18, None, ALU.max).then_inc(s["nl_in"], 1)
                dve.scalar_tensor_tensor(t_l, gl, 0.0, for_items(mask[:]), ALU.max, ALU.mult).then_inc(gs, 1)
                newton(g, nl, s["nl_exp"], s["nl_steps2"], nl[:, 3, :], 3).then_inc(s["nl_steps2"], 1)
                dve.wait_ge(s["nl_steps2"], g * 3 + 3)
                dve.tensor_scalar(nl[:, 5, :], nl[:, 3, :], c1(CAP_C), None, ALU.min).then_inc(s["r_ready"], 1)

                def v_low(b):
                    dve.wait_ge(s["v_h_ready"], g * GB + (b + 1))
                    dve.scalar_tensor_tensor(v_l[:, b, :], bank[b][:], V_DOWN, v_h[:, b, :], ALU.mult,
                                             ALU.subtract).then_inc(s["v_l_ready"], 1)

                v_low(0)
                fs = s["cf_steps"]
                dve.wait_ge(s["e_ready"], g + 1)
                dve.scalar_tensor_tensor(a_g, e_g, 1.0, for_items(mask[:]), ALU.min, ALU.mult).then_inc(gs, 1)
                dve.wait_ge(gs, g * 4 + 2)
                dve.tensor_reduce(cf[:, 6, :], a_g, AX.X, ALU.add).then_inc(gs, 1)
                dve.wait_ge(gs, g * 4 + 3)
                dve.tensor_scalar(cf[:, 6, :], cf[:, 6, :], ROW_EPS, None, ALU.max).then_inc(fs, 1)
                dve.wait_ge(fs, g * 6 + 1)
                dve.reciprocal(cf[:, 6, :], cf[:, 6, :]).then_inc(fs, 1)
                dve.wait_ge(fs, g * 6 + 2)
                dve.tensor_scalar(cf[:, 7, :], cf[:, 6, :], c1(W_G), None, ALU.mult).then_inc(s["cf_ready"], 1)
                v_low(1)
                dve.wait_ge(s["rm_ps"], g + 1)
                dve.tensor_tensor(a_l, t_l, bank[7][:].rearrange("p (b n) -> p b n", b=GB), ALU.mult).then_inc(gs, 1)
                dve.wait_ge(gs, g * 4 + 4)
                dve.tensor_reduce(cf[:, 2, :], a_l, AX.X, ALU.add).then_inc(fs, 1)
                dve.wait_ge(fs, g * 6 + 3)
                dve.tensor_tensor(cf[:, 4, :], cf[:, 2, :], nl[:, 5, :], ALU.mult).then_inc(fs, 1)
                dve.wait_ge(fs, g * 6 + 4)
                dve.tensor_scalar(cf[:, 4, :], cf[:, 4, :], ROW_EPS, None, ALU.max).then_inc(fs, 1)
                dve.wait_ge(fs, g * 6 + 5)
                dve.reciprocal(cf[:, 5, :], cf[:, 4, :]).then_inc(fs, 1)
                dve.wait_ge(fs, g * 6 + 6)
                dve.scalar_tensor_tensor(cf[:, 3, :], cf[:, 5, :], c1(W_L), nl[:, 5, :], ALU.mult,
                                         ALU.mult).then_inc(s["cl_ready"], 1)
                dve.wait_ge(s["cl_ready"], g + 1)
                dve.wait_ge(s["kg_ready"], g + 1)
                for b in range(GB):
                    last = dve.scalar_tensor_tensor(k_mix[:, b, :], a_l[:, b, :], cf[:, 3, b:b + 1], k_g[:, b, :],
                                                    ALU.mult, ALU.add)
                last.then_inc(s["k_ready"], 1)
                v_low(2)
                v_low(3)
                dve.wait_ge(s["kT_h_ready"], g + 1)
                dve.scalar_tensor_tensor(kT_l, bank[6][:].rearrange("p (b n) -> p b n", b=GB), K_UP, kT_h, ALU.mult,
                                         ALU.subtract).then_inc(s["kT_l_ready"], 1)
                if has_next:
                    for b in range(GB):
                        hT_low(g + 1, b)
                second_residual(g, slot, has_previous)
                if has_second:
                    x_low(g + 2)

            residual(0)
            first_norm(0, 0)
            for b in range(GB):
                hT_low(0, b)
            x_low(1)
            body(0, 0, True, True, False)
            with dve.Fori(0, NG // 2 - 2) as j:
                for t in (1, 2):
                    body(j * 2 + t, t % 2, True, True, True)
            body(NG - 3, (NG - 3) % 2, True, True, True)
            body(NG - 2, (NG - 2) % 2, True, False, True)
            body(NG - 1, (NG - 1) % 2, False, False, True)
            second_norm(NG - 1)


def kernel(**inputs):
    import numpy as np
    import concourse.bacc as bacc
    from concourse.bass_utils import run_bass_kernel_spmd as run

    f = {n: np.asarray(a) for n, a in inputs.items()}
    arrays = {
        "x": np.ascontiguousarray(f["x"]),
        "adj": np.ascontiguousarray(f["adj"]),
        "bias": np.ascontiguousarray(f["L0_gnn_bias"].reshape(-1, 1)),
        "w_lang_t": np.ascontiguousarray(f["L1_gnn_W_lang"].T),
        "w_grav_t": np.ascontiguousarray(f["L1_gnn_W_grav"].T),
        "w_v": np.ascontiguousarray(f["L1_gnn_W_V"]),
        "w_o_t": np.ascontiguousarray(f["L1_gnn_W_O"].T),
        "gate_logit": np.ascontiguousarray(f["L1_gnn_gate_logit"].reshape(1, 1)),
        "log_sigma": np.ascontiguousarray(f["L1_gnn_log_sigma"].reshape(1, 1)),
    }
    nc = bacc.Bacc("TRN2", target_bir_lowering=False, num_devices=1)
    args = [nc.dram_tensor(f"in_{n}", a.shape, mybir.dt.from_np(a.dtype), kind="ExternalInput").ap()
            for n, a in arrays.items()]
    res = nc.dram_tensor("out_dram", arrays["x"].shape, F32, kind="ExternalOutput").ap()
    build(nc, *args, res)
    r = run(nc, [{f"in_{n}": a for n, a in arrays.items()}], core_ids=[0])
    return r.results[0]["out_dram"]
```

```python
from contextlib import ExitStack

import concourse.bass as bass
from concourse import mybir

F32 = mybir.dt.float32
F16 = mybir.dt.float16
BF16 = mybir.dt.bfloat16
I32 = mybir.dt.int32
ALU = mybir.AluOpType
ACT = mybir.ActivationFunctionType
AX = mybir.AxisListType
ABSMAX = bass.bass_isa.ReduceOp.absmax

P = 128
EXPONENT = 0x7F800000


def wait(eng, sem, value):
    if not isinstance(value, int) or value > 0:
        eng.wait_ge(sem, value)


def build(nc, x, adj, bias, wlT, wgT, wv, woT, gate, log_sigma, out):
    B, L, NODES = x.shape
    assert L == P and NODES % P == 0
    KB = NODES // P
    GB = 4
    NG = B // GB
    K_NEAR = max(int(NODES * 0.3), 1)
    ROUNDS = 2
    FIRST_GUESS, STEPS = 0.525, (0.2, 0.1, 0.05, 0.025)
    CB = 4
    NC = B // CB
    LG = P // CB
    CL = L // LG
    SLOTS = 6
    assert NG % 2 == 0 and NG >= 4 and NC % 2 == 0 and NC > SLOTS + 2

    X_HAT = 2.0 ** 12
    S_SCALE = 1.0 / (X_HAT * X_HAT * B)
    X_UP, W_UP, A_UP, H_UP, K_UP = 2.0 ** 13, 2.0 ** 14, 2.0 ** 12, 2.0 ** 8, 2.0 ** 14
    XW_DOWN, Z_DOWN, VO_DOWN, V_DOWN = 2.0 ** -17, 2.0 ** -16, 2.0 ** -22, 2.0 ** -16
    CROSS_DOWN = 2.0 ** -13
    ALPHA = 1.0 / (X_UP * W_UP * XW_DOWN * A_UP)
    Z_UNIT = 1.0 / (H_UP * W_UP * Z_DOWN)
    BETA = 1.0 / (H_UP * W_UP * W_UP * VO_DOWN * W_UP * V_DOWN * K_UP)
    TAKEN, SELF, PAD, ABOVE = -1e30, -2e30, -3e30, 1e20
    NORM_EPS, LN_EPS, ROW_EPS = 1e-12, 1e-5, 1e-8

    x_chunk = x.rearrange("(c b) (g l) n -> c (b g) l n", b=CB, g=LG)
    x_group = x.rearrange("(g b) l n -> g l b n", b=GB)
    out_group = out.rearrange("(g b) l n -> g l b n", b=GB)

    with ExitStack() as ctx:
        def sb(name, shape, dt=F32):
            return ctx.enter_context(nc.sbuf_tensor(name, shape, dt))

        def sem(name):
            return ctx.enter_context(nc.semaphore(name))

        bank = [ctx.enter_context(nc.psum_tensor(f"bank{i}", [P, 512], F32)) for i in range(8)]

        cross_ps = [bank[4][:, 0:P], bank[1][:, 3 * P:4 * P], bank[2][:, 2 * P:3 * P], bank[3][:, P:2 * P]]

        ident = sb("ident", [P, P])
        ones = sb("ones", [P, P])
        ident_b = sb("ident_b", [P, P], BF16)
        ident_up = sb("ident_up", [P, P], F16)
        zero = sb("zero", [P, GB])
        PARTS = 3
        pick_item = sb("pick_item", [GB * PARTS, GB, P], BF16)
        sq_parts = sb("sq_parts", [P, GB, PARTS], BF16)
        sq_rows = sb("sq_rows", [GB * PARTS, P], BF16)
        rn_parts = sb("rn_parts", [P, GB, PARTS], BF16)
        rn_rows = sb("rn_rows", [GB * PARTS, P], BF16)
        part_rest = sb("part_rest", [P, 2, GB])
        item_of = sb("item_of", [P, CB])
        sqn = sb("sqn", [P, KB, CB])
        rinv = sb("rinv", [P, KB, CB])
        rinv_rep = sb("rinv_rep", [P, KB, P])
        self_mark = sb("self_mark", [P, P])
        mask = sb("mask", [P, P])
        adj_sb = sb("adj_sb", [P, P])
        adj_h = sb("adj_h", [P, P], F16)
        adj_l = sb("adj_l", [P, P], F16)
        bias_c = sb("bias_c", [P, 1])
        gate_c = sb("gate_c", [P, 1])
        ls_c = sb("ls_c", [P, 1])
        chunk_max = sb("chunk_max", [P, NC])
        magn = sb("magn", [P, 8])
        magn_all = sb("magn_all", [P, 8])
        pw = sb("pw", [P, 8])
        ipw = sb("ipw", [P, 8])
        vo_scale = sb("vo_scale", [P, 4])
        vo_magn = sb("vo_magn", [P, 2])
        up = sb("up", [P, 8])
        col = sb("col", [P, 16])
        D_MAX, D_POW, D_INV, ALPHA_C, CAP_C, KAPPA, W_L, W_G, BETA_C, T0, T1, HK = range(12)
        c1 = lambda i: col[:, i:i + 1]
        deg_m, deg_t, deg_u, dinv, dinv_col = (sb(n, [P, KB]) for n in ("deg_m", "deg_t", "deg_u", "dinv", "dinv_col"))
        top8 = sb("top8", [P, 2, 8])
        rank = sb("rank", [P, 8 * ROUNDS])
        rank_i = sb("rank_i", [P, 8 * ROUNDS], I32)
        cut = sb("cut", [P, 2, 8 * ROUNDS])
        cut8 = sb("cut8", [P, 2, 8])
        guess = sb("guess", [P, 12, 2])
        row_stats = sb("row_stats", [P, 2, 6])
        row_mv = sb("row_mv", [P, 2, 2])
        most = sb("most", [P, 2])
        extra_f = sb("extra_f", [1, 2])
        extra_i = sb("extra_i", [1, 4], I32)
        stats = sb("stats", [P, GB, 6])
        stats2 = sb("stats2", [P, GB, 6])
        mv = sb("mv", [P, GB, 2])
        mv2 = sb("mv2", [P, GB, 2])
        ln1 = sb("ln1", [P, 5, GB])
        ln2 = sb("ln2", [P, 5, GB])
        nl = sb("nl", [P, 6, GB])
        cf = sb("cf", [P, 8, GB])

        KIB = 1024
        arena = sb("arena", [P, 198 * KIB // 4])

        def at(start, free, dt=F32):
            size = (2 if dt == F16 else 4)
            n = 1
            for d in free:
                n *= d
            flat = arena[:, start // 4:(start + n * size) // 4]
            if dt == F16:
                flat = flat.bitcast(F16)
            if len(free) == 1:
                return flat
            names = "abcd"[:len(free)]
            spec = f"p ({' '.join(names)}) -> p {' '.join(names)}"
            return flat.rearrange(spec, **dict(zip(names, free)))

        TILES = B * L // P
        xn_h = at(0, [TILES, NODES], F16)
        xn_l = at(64 * KIB, [TILES, NODES], F16)
        xc = [at(k * KIB, [CL, NODES]) for k in (128, 136, 144, 152, 176, 184)]
        sq = [at(k * KIB, [CL, NODES]) for k in (160, 168)]
        S = at(176 * KIB, [KB, NODES])
        work = at(184 * KIB, [KB, NODES + 8])
        ssum = [at((193 + 2 * i) * KIB - KIB // 2, [NODES]) for i in range(2)]
        wT_h = [at(k * KIB, [KB, NODES], F16) for k in (144, 152, 136)]
        wT_l = [at(k * KIB, [KB, NODES], F16) for k in (148, 156, 140)]
        an_h = at(128 * KIB, [KB, NODES], F16)
        an_l = at(132 * KIB, [KB, NODES], F16)
        w_raw = [at(k * KIB, [KB, NODES]) for k in (160, 168, 128, 136)]
        A = work[:, :, 0:NODES]
        squares = at(144 * KIB, [KB, NODES])
        vo_h = [at(k * KIB, [KB, NODES], F16) for k in (144, 152)]
        vo_l = [at(k * KIB, [KB, NODES], F16) for k in (148, 156)]
        vo_raw = at(120 * KIB, [KB, NODES])
        vo_squares = at(80 * KIB, [KB, NODES])
        dinv_rep = rinv_rep[:]
        cross = rinv_rep
        tally = at(193 * KIB - KIB // 2, [2, NODES])
        xg = at(0, [GB, NODES])
        x_h = at(8 * KIB, [GB, NODES], F16)
        x_l = at(12 * KIB, [GB, NODES], F16)
        xw_h = at(16 * KIB, [GB, KB, P], F16)
        xw_l = at(20 * KIB, [GB, KB, P], F16)
        y = at(24 * KIB, [GB, NODES])
        h = [at(32 * KIB, [GB, NODES]), at(40 * KIB, [GB, NODES])]
        hT_h = at(48 * KIB, [KB, GB, P], F16)
        hT_l = at(52 * KIB, [KB, GB, P], F16)
        z_h = [at(56 * KIB, [KB, GB, P], F16), at(64 * KIB, [KB, GB, P], F16)]
        z_l = [at(60 * KIB, [KB, GB, P], F16), at(68 * KIB, [KB, GB, P], F16)]
        v_h = at(72 * KIB, [GB, NODES], F16)
        v_l = at(76 * KIB, [GB, NODES], F16)
        y2 = at(80 * KIB, [GB, NODES])
        tile_at = iter(range(88 * KIB, 110 * KIB, 2 * KIB))
        diag_l, diag_g, t_l, a_l, e_g, a_g, k_g, k_mix = (
            at(next(tile_at), [GB, P]) for _ in range(8))
        kT_h = at(108 * KIB, [GB, P], F16)
        kT_l = at(109 * KIB, [GB, P], F16)
        gram_cross = [at(k * KIB, [GB, P], F16) for k in (110, 111)]

        names = """consts_made picks_made const_steps small_in sq_ready ssum_ready nrm_ps nrm_in nrm_ready rinv_made
            rinv_ready spread_ps xn_ready xn_h_ready xn_l_ready gram_ps cross_out gram_full S_ready
            S_turned work_ready work_filled work_23_ready pick_steps need_ready most_ready var_ready
            deviation_ready more_steps0 more_steps1 rank_made A_ready w_in0 w_in1 w_in2 w_in3
            magn_ready magn_x magn_all_ready magn_guarded magn_root scale_steps scale_ready
            adj_h_ready adj_l_ready w_scaled vo_out vo_magn_ready vo_magn_all vo_guarded vo_root
            vo_steps vo_up w_h_ready w_l_ready vo_ps vo_scaled deg_ps deg_steps deg_in deg_root
            dinv_ready dinv_ps d_ready an_h_ready an_l_ready an_f col_exp col_steps x_in x_scaled
            x_h_ready x_l_ready xw_ps xw_h_ready xw_l_ready mix_ps mixed y_ready stats_ready ln1_var
            ln1_log ln1_exp ln1_steps ln1_ready h_ready hT_ps hT_h_ready hT_l_ready zl_ps zl_h_ready
            zl_l_ready zg_ps zg_h_ready zg_l_ready gl_ps gg_ps gl_cross_ps gg_cross_ps gl_cross_out
            gg_cross_out nl_in nl_log nl_exp nl_steps r_ready dg_ready part_steps sq_parted
            rn_parted sq_rows_ps rn_rows_ps sq_rows_ready rn_rows_ready sq_ps rm_ps hk_ready e_ready
            graph_steps cf_steps cf_ready k_ready kg_ready cl_ready v_ps v_h_ready v_l_ready kT_ps
            kT_h_ready kT_l_ready out_ps y2_ready ln2_var ln2_log ln2_exp ln2_steps o_ready stored
            stats2_ready nl_steps2 stat1_steps stat2_steps""".split()
        s = {n: sem(n) for n in names}
        x_loaded = [sem(f"x_loaded{i}") for i in range(SLOTS)]

        def three(pe, dst, ah, al, bh, bl, start, stop):
            pe.matmul(dst, ah, bh, start=start, stop=False)
            pe.matmul(dst, ah, bl, start=False, stop=False)
            return pe.matmul(dst, al, bh, start=False, stop=stop)

        def per_item(c):
            return c.unsqueeze(2).broadcast_to([P, GB, P])

        def for_items(m):
            return m.unsqueeze(1).broadcast_to([P, GB, P])

        block = ctx.enter_context(nc.Block())

        @block.sync
        def _(sp):
            for c in range(SLOTS):
                sp.dma_start(xc[c], x_chunk[c]).then_inc(x_loaded[c], 16)
            sp.dma_start(adj_sb[:], adj).then_inc(s["small_in"], 16)
            sp.dma_start(bias_c[:], bias).then_inc(s["small_in"], 16)
            sp.dma_start(gate_c[:], gate.broadcast_to([P, 1])).then_inc(s["small_in"], 16)
            sp.dma_start(ls_c[:], log_sigma.broadcast_to([P, 1])).then_inc(s["small_in"], 16)
            for c in range(SLOTS, NC):
                sp.wait_ge(s["xn_l_ready"], c - SLOTS + 1)
                sp.dma_start(xc[c % SLOTS], x_chunk[c]).then_inc(x_loaded[c % SLOTS], 16)
            sp.wait_ge(s["ssum_ready"], NC)
            sp.dma_start(w_raw[0], wlT.rearrange("(k p) e -> p k e", p=P)).then_inc(s["w_in0"], 16)
            sp.dma_start(w_raw[1], wgT.rearrange("(k p) e -> p k e", p=P)).then_inc(s["w_in1"], 16)
            sp.wait_ge(s["xn_l_ready"], NC)
            sp.dma_start(w_raw[2], wv.rearrange("(k p) e -> p k e", p=P)).then_inc(s["w_in2"], 16)
            sp.dma_start(w_raw[3], woT.rearrange("(k p) e -> p k e", p=P)).then_inc(s["w_in3"], 16)
            sp.wait_ge(s["gram_ps"], 4)
            sp.dma_start(xg, x_group[0]).then_inc(s["x_in"], 16)

            def load_x(g):
                sp.wait_ge(s["y_ready"], g * GB)
                sp.wait_ge(s["x_h_ready"], g)
                sp.wait_ge(s["x_l_ready"], g)
                sp.dma_start(xg, x_group[g]).then_inc(s["x_in"], 16)

            def store(g):
                sp.wait_ge(s["o_ready"], g * GB + GB)
                sp.dma_start(out_group[g], y2).then_inc(s["stored"], 16)

            load_x(1)
            load_x(2)
            with sp.Fori(0, NG - 3) as g:
                load_x(g + 3)
                store(g)
            store(NG - 3)
            store(NG - 2)
            for b in range(GB):
                sp.wait_ge(s["o_ready"], (NG - 1) * GB + (b + 1))
                sp.dma_start(out_group[NG - 1][:, b, :], y2[:, b, :]).then_inc(s["stored"], 16)
            sp.wait_ge(s["stored"], 16 * (NG - 1 + GB))

        @block.gpsimd
        def _(pool):
            cs = s["const_steps"]
            pool.memset(ident[:], 0.0).then_inc(cs, 1)
            pool.memset(item_of[:], 1.0).then_inc(cs, 1)
            pool.memset(ones[:], 1.0).then_inc(cs, 1)
            pool.memset(zero[:], 0.0).then_inc(cs, 1)
            pool.memset(ident_up[:], 0.0).then_inc(cs, 1)
            pool.memset(pick_item[:], 1.0).then_inc(cs, 1)
            pool.memset(self_mark[:], 0.0).then_inc(cs, 1)
            pool.memset(magn[:], 1.0).then_inc(cs, 1)
            pool.wait_ge(cs, 8)
            pool.affine_select(out=ident[:], in_=ident[:], compare_op=ALU.not_equal, fill=1.0, base=0,
                               pattern=[[-1, P]], channel_multiplier=1).then_inc(s["consts_made"], 1)
            pool.affine_select(out=self_mark[:], in_=self_mark[:], compare_op=ALU.not_equal, fill=SELF, base=0,
                               pattern=[[-1, P]], channel_multiplier=1).then_inc(s["consts_made"], 1)
            pool.iota(rank_i[:], [[1, 8 * ROUNDS]], channel_multiplier=0).then_inc(s["rank_made"], 1)
            pool.wait_ge(s["rank_made"], 1)
            pool.tensor_copy(rank[:], rank_i[:]).then_inc(s["rank_made"], 1)
            pool.affine_select(out=item_of[:], in_=item_of[:], compare_op=ALU.is_ge, fill=0.0, base=0,
                               pattern=[[-LG, CB]], channel_multiplier=1).then_inc(cs, 1)
            pool.wait_ge(cs, 9)
            pool.affine_select(out=item_of[:], in_=item_of[:], compare_op=ALU.is_ge, fill=0.0, base=LG - 1,
                               pattern=[[LG, CB]], channel_multiplier=-1).then_inc(s["consts_made"], 1)
            pool.affine_select(out=ident_up[:], in_=ident_up[:], compare_op=ALU.not_equal, fill=1.0 / CROSS_DOWN,
                               base=0, pattern=[[-1, P]], channel_multiplier=1).then_inc(s["picks_made"], 1)
            pool.affine_select(out=pick_item[:], in_=pick_item[:], compare_op=ALU.is_ge, fill=0.0, base=0,
                               pattern=[[-PARTS, GB], [0, P]], channel_multiplier=1).then_inc(cs, 1)
            pool.wait_ge(cs, 10)
            pool.affine_select(out=pick_item[:], in_=pick_item[:], compare_op=ALU.is_ge, fill=0.0, base=PARTS - 1,
                               pattern=[[PARTS, GB], [0, P]], channel_multiplier=-1).then_inc(s["picks_made"], 1)
            pool.wait_ge(s["consts_made"], 1)
            pool.tensor_copy(ident_b[:], ident[:]).then_inc(s["picks_made"], 1)
            pool.wait_ge(s["small_in"], 64)
            pool.affine_select(out=mask[:], in_=adj_sb[:], compare_op=ALU.not_equal, fill=0.0, base=0,
                               pattern=[[-1, P]], channel_multiplier=1).then_inc(s["consts_made"], 1)

            for c in range(NC):
                pool.wait_ge(s["xn_h_ready"], c + 1)
                o = slice(c * CL, (c + 1) * CL)
                pool.tensor_tensor(xn_l[:, o, :], xc[c % SLOTS], xn_h[:, o, :],
                                   ALU.subtract).then_inc(s["xn_l_ready"], 1)

            def weight_low(i, nth):
                pool.wait_ge(s["w_h_ready"], nth)
                raw, hi, lo = [(w_raw[0], wT_h[0], wT_l[0]), (w_raw[1], wT_h[1], wT_l[1]),
                               (w_raw[2], vo_h[0], vo_l[0]), (w_raw[3], vo_h[1], vo_l[1])][i]
                pool.tensor_tensor(lo, raw, hi, ALU.subtract).then_inc(s["w_l_ready"], 1)

            pool.wait_ge(s["need_ready"], 1)
            pool.partition_all_reduce(most[:], guess[:, 9, :], P, ABSMAX).then_inc(s["most_ready"], 1)
            pool.wait_ge(s["magn_ready"], 5)
            pool.wait_ge(s["magn_x"], 1)
            pool.partition_all_reduce(magn_all[:], magn[:], P, ABSMAX).then_inc(s["magn_all_ready"], 1)
            pool.wait_ge(s["magn_all_ready"], 1)
            pool.tensor_scalar(magn_all[:], magn_all[:], 1e-30, None, ALU.max).then_inc(s["magn_guarded"], 1)
            weight_low(2, 1)
            weight_low(3, 2)
            for i in range(KB // 2, KB):
                pool.wait_ge(s["work_filled"], i - KB // 2 + 1)
                pool.tensor_tensor(work[:, i, i * P:(i + 1) * P], work[:, i, i * P:(i + 1) * P], self_mark[:],
                                   ALU.add).then_inc(s["work_23_ready"], 1)
            pool.wait_ge(s["adj_h_ready"], 2)
            pool.tensor_tensor(adj_l[:], adj_sb[:], adj_h[:], ALU.subtract).then_inc(s["adj_l_ready"], 1)
            pool.wait_ge(s["x_h_ready"], 1)
            pool.tensor_tensor(x_l, y, x_h, ALU.subtract).then_inc(s["x_l_ready"], 1)
            pool.wait_ge(s["vo_magn_ready"], 1)
            pool.partition_all_reduce(vo_magn[:, 1:2], vo_magn[:, 0:1], P, ABSMAX).then_inc(s["vo_magn_all"], 1)
            pool.wait_ge(s["vo_magn_all"], 1)
            pool.tensor_scalar(vo_magn[:, 1:2], vo_magn[:, 1:2], 1e-30, None, ALU.max).then_inc(s["vo_guarded"], 1)
            weight_low(0, 3)
            weight_low(1, 4)
            def residual(g):
                for b in range(GB):
                    pool.wait_ge(s["mixed"], g * GB + (b + 1))
                    pool.tensor_tensor(y[:, b, :], y[:, b, :], xg[:, b, :], ALU.add).then_inc(s["y_ready"], 1)

            residual(0)
            pool.wait_ge(s["w_h_ready"], 5)
            pool.tensor_tensor(wT_l[2], vo_raw, wT_h[2], ALU.subtract).then_inc(s["w_l_ready"], 1)

            def part(g, src, parts, used, steps, done):
                wait(pool, used, g)
                for i, (rest, less) in enumerate([(src, None), (part_rest[:, 0, :], src),
                                                  (part_rest[:, 1, :], part_rest[:, 0, :])]):
                    if i:
                        pool.wait_ge(steps[0], g * 8 + (steps[1] + 2 * i - 1))
                        pool.tensor_tensor(rest, less, parts[:, :, i - 1], ALU.subtract).then_inc(steps[0], 1)
                        pool.wait_ge(steps[0], g * 8 + (steps[1] + 2 * i))
                    pool.tensor_tensor(parts[:, :, i], rest, zero[:], ALU.add).then_inc(done if i == 2 else steps[0], 1)

            def graphs(g):
                pool.wait_ge(s["dg_ready"], g * 2 + 2)
                part(g, cf[:, 1, :], sq_parts, s["sq_rows_ps"], (s["part_steps"], 0), s["sq_parted"])
                pool.wait_ge(s["r_ready"], g + 1)
                pool.wait_ge(s["sq_parted"], g + 1)
                part(g, nl[:, 5, :], rn_parts, s["rn_rows_ps"], (s["part_steps"], 4), s["rn_parted"])
                pool.wait_ge(s["cf_ready"], g + 1)
                wait(pool, s["k_ready"], g)
                pool.tensor_tensor(k_g, a_g, per_item(cf[:, 7, :]), ALU.mult).then_inc(s["kg_ready"], 1)

            residual(1)
            graphs(0)
            with pool.Fori(1, NG - 1) as g:
                residual(g + 1)
                graphs(g)
            graphs(NG - 1)

        @block.tensor
        def _(pe):
            pe.wait_ge(s["consts_made"], 3)
            pe.wait_ge(s["picks_made"], 3)

            def item_sums(c, slot):
                pe.wait_ge(s["ssum_ready"], c + 1)
                wait(pe, s["nrm_in"], c)
                for k in range(KB):
                    mm = pe.matmul(bank[7][:, k * CB:(k + 1) * CB], ssum[slot][:, k * P:(k + 1) * P], item_of[:],
                                   start=True, stop=True)
                mm.then_inc(s["nrm_ps"], 1)

            def spread(c, slot):
                pe.wait_ge(s["rinv_ready"], c + 1)
                wait(pe, s["xn_ready"], c - 1)
                for k in range(KB):
                    mm = pe.transpose(bank[5 + slot][:, k * P:(k + 1) * P],
                                      rinv_rep[:, k, :], ident[:])
                mm.then_inc(s["spread_ps"], 1)

            def cross_product(r, xh, xl, start, stop):
                mine = slice(r * P, (r + 1) * P)
                pe.matmul(cross_ps[r], xh[:, mine], xl[:, mine], start=start, stop=stop, skip_group_check=True)

            def gram(c, rows, first=False, last=False, ts=range(CL)):
                for t in ts:
                    for r in rows:
                        o = bass.ds(c * CL + t, 1) if not isinstance(c, int) else slice(c * CL + t, c * CL + t + 1)
                        xh = xn_h[:, o, :].rearrange("p a n -> p (a n)")
                        xl = xn_l[:, o, :].rearrange("p a n -> p (a n)")
                        begin = first and t == 0
                        end = last and t == CL - 1
                        mine, right = slice(r * P, (r + 1) * P), slice((r + 1) * P, NODES)
                        if not begin or r == 0:
                            cross_product(r, xh, xl, start=(begin and r == 0), stop=(end and r == 0))
                        mm = pe.matmul(bank[r][:, 0:NODES - r * P], xh[:, mine], xh[:, r * P:], start=begin,
                                       stop=(end and r == KB - 1))
                        if begin and r:
                            cross_product(r, xh, xl, start=False, stop=False)
                        if r < KB - 1:
                            pe.matmul(bank[r][:, P:NODES - r * P], xh[:, mine], xl[:, right], start=False, stop=False)
                            mm = pe.matmul(bank[r][:, P:NODES - r * P], xl[:, mine], xh[:, right], start=False,
                                           stop=end)
                        if end:
                            mm.then_inc(s["gram_ps"], 1)

            def finish_diagonal(r):
                pe.wait_ge(s["cross_out"], r + 1)
                pe.matmul(bank[r][:, 0:P], ident[:], cross[:, r, :], start=False, stop=False, skip_group_check=True)
                pe.matmul(bank[r][:, 0:P], cross[:, r, :], ident[:], start=False, stop=True,
                          skip_group_check=True).then_inc(s["gram_full"], 1)

            def turn(dst, i, j):
                return pe.transpose(dst, S[:, i, j * P:(j + 1) * P], ident[:])

            def rows_01(c, slot, first=False, last=False):
                if not isinstance(c, int) or c + 2 < NC:
                    spread(c + 2, slot)
                pe.wait_ge(s["xn_l_ready"], c + 1)
                gram(c, (0, 1), first=first, ts=range(0, CL // 2))
                if not isinstance(c, int) or c + 3 < NC:
                    item_sums(c + 3, 1 - slot)
                gram(c, (0, 1), last=last, ts=range(CL // 2, CL))

            item_sums(0, 0)
            spread(0, 0)
            item_sums(1, 1)
            spread(1, 1)
            item_sums(2, 0)
            rows_01(0, 0, first=True)
            with pe.Fori(0, (NC - 4) // 2) as j:
                for t in (1, 2):
                    rows_01(j * 2 + t, t % 2)
            for c in range(NC - 3, NC):
                rows_01(c, c % 2, last=(c == NC - 1))
            finish_diagonal(0)
            finish_diagonal(1)
            pe.wait_ge(s["S_ready"], 2)
            turn(bank[7][:, 0:P], 0, 1).then_inc(s["S_turned"], 1)
            turn(bank[5][:, 0:P], 0, 2)
            turn(bank[5][:, P:2 * P], 1, 2).then_inc(s["S_turned"], 1)
            turn(bank[6][:, 0:P], 0, 3)
            turn(bank[6][:, P:2 * P], 1, 3).then_inc(s["S_turned"], 1)
            for c in range(NC):
                gram(c, range(2, KB), first=(c == 0), last=(c == NC - 1))
            finish_diagonal(2)
            finish_diagonal(3)
            pe.wait_ge(s["S_ready"], 6)
            turn(bank[7][:, P:2 * P], 2, 3).then_inc(s["S_turned"], 1)

            pe.wait_ge(s["w_l_ready"], 2)
            pe.wait_ge(s["S_ready"], 7)
            for d in range(KB):
                for f in range(KB):
                    mm = three(pe, bank[d][:], vo_h[0][:, f, d * P:(d + 1) * P], vo_l[0][:, f, d * P:(d + 1) * P],
                               vo_h[1][:, f, :], vo_l[1][:, f, :], start=(f == 0), stop=(f == KB - 1))
                mm.then_inc(s["vo_ps"], 1)

            def project_x(g):
                pe.wait_ge(s["x_l_ready"], g + 1)
                for b in range(GB):
                    wait(pe, s["zl_l_ready"], g * GB - GB + (b + 1) if not isinstance(g, int) or g > 0 else 0)
                    for k in range(KB):
                        mm = three(pe, bank[b][:, k * P:(k + 1) * P],
                                   x_h[:, b, k * P:(k + 1) * P], x_l[:, b, k * P:(k + 1) * P],
                                   adj_h[:], adj_l[:], start=True, stop=True)
                    mm.then_inc(s["xw_ps"], 1)

            def mix_nodes(g):
                for b in range(GB):
                    pe.wait_ge(s["xw_l_ready"], g * GB + (b + 1))
                    wait(pe, s["zg_l_ready"], g * GB - GB + (b + 1) if not isinstance(g, int) or g > 0 else 0)
                    for k in range(KB):
                        if isinstance(g, int) and g == 0 and b == 0:
                            pe.wait_ge(s["an_l_ready"], k + 1)
                        mm = three(pe, bank[b][:], xw_h[:, b, k, :], xw_l[:, b, k, :],
                                   an_h[:, k, :], an_l[:, k, :], start=(k == 0), stop=(k == KB - 1))
                    mm.then_inc(s["mix_ps"], 1)

            h_bank = [bank[4], bank[5], bank[7], bank[3]]

            def turn_h(g, slot, b):
                pe.wait_ge(s["h_ready"], g * GB + (b + 1))
                if b == 3 and not (isinstance(g, int) and g == 0):
                    pe.wait_ge(s["v_l_ready"], g * GB)
                for k in range(KB):
                    mm = pe.transpose(h_bank[b][:, k * P:(k + 1) * P], h[slot][:, b, k * P:(k + 1) * P], ident[:])
                mm.then_inc(s["hT_ps"], 1)

            def project_z(g, i, freed, done):
                for e in range(KB):
                    wait(pe, freed[0], freed[1] + (e + 1))
                    for k in range(KB):
                        mm = three(pe, bank[e][:], wT_h[i][:, k, e * P:(e + 1) * P], wT_l[i][:, k, e * P:(e + 1) * P],
                                   hT_h[:, k, :, :], hT_l[:, k, :, :], start=(k == 0), stop=(k == KB - 1))
                    mm.then_inc(done, 1)

            def inner_products(i, cross_bank, done):
                for b in range(GB):
                    for e in range(KB):
                        first, last = (b == 0 and e == 0), (b == GB - 1 and e == KB - 1)
                        pe.matmul(bank[4 + i][:, b * P:(b + 1) * P], z_h[i][:, e, b, :], z_h[i][:, e, b, :],
                                  start=first, stop=False)
                        mm = pe.matmul(cross_bank[:, b * P:(b + 1) * P], z_h[i][:, e, b, :], z_l[i][:, e, b, :],
                                       start=first, stop=last)
                mm.then_inc(done, 1)

            def add_cross(i, done):
                pe.matmul(bank[4 + i][:], ident_up[:], gram_cross[i], start=False, stop=False)
                for b in range(GB):
                    mm = pe.matmul(bank[4 + i][:, b * P:(b + 1) * P], gram_cross[i][:, b, :], ident_up[:],
                                   start=False, stop=(b == GB - 1))
                mm.then_inc(done, 1)

            def values(g, b, last_group, ks=range(KB)):
                if ks[0] == 0:
                    if last_group:
                        pe.wait_ge(s["zg_l_ready"], g * GB + (b + 1))
                    else:
                        pe.wait_ge(s["mixed"], g * GB + GB + (b + 1))
                for k in ks:
                    mm = three(pe, bank[b][:], hT_h[:, k, b, :], hT_l[:, k, b, :],
                               wT_h[2][:, k, :], wT_l[2][:, k, :], start=(k == 0), stop=(k == KB - 1))
                if ks[-1] == KB - 1:
                    mm.then_inc(s["v_ps"], 1)

            def part_rows(first, parts, done):
                pe.matmul(bank[6][0:GB * PARTS, first:first + P], parts[:].rearrange("p b i -> p (b i)"), ident_b[:],
                          start=True, stop=True).then_inc(done, 1)

            def along_rows(dst, rows, start, done):
                for b in range(GB):
                    mm = pe.matmul(dst[:, b * P:(b + 1) * P], pick_item[:, b, :], rows[:], start=(start and b == 0),
                                   stop=(b == GB - 1), skip_group_check=True)
                mm.then_inc(done, 1)

            def weighted(g, b):
                pe.wait_ge(s["v_l_ready"], g * GB + (b + 1))
                three(pe, bank[b][:], kT_h[:, b, :], kT_l[:, b, :], v_h[:, b, :], v_l[:, b, :],
                      start=True, stop=True).then_inc(s["out_ps"], 1)

            def body(g, slot, has_next):
                pe.wait_ge(s["hT_l_ready"], g * GB + GB)
                if isinstance(g, int) and g == 0:
                    project_z(g, 0, (s["mixed"], 0), s["zl_ps"])
                else:
                    project_z(g, 0, (s["y2_ready"], g * GB - GB), s["zl_ps"])
                if has_next:
                    project_x(g + 1)
                    project_z(g, 1, (s["xw_l_ready"], g * GB + GB), s["zg_ps"])
                    mix_nodes(g + 1)
                else:
                    project_z(g, 1, (s["zl_l_ready"], g * GB), s["zg_ps"])
                pe.wait_ge(s["zg_l_ready"], g * GB + GB)
                inner_products(1, bank[7], s["gg_cross_ps"])
                pe.wait_ge(s["w_l_ready"], 5)
                values(g, 0, not has_next, range(0, 1))
                pe.wait_ge(s["gg_cross_out"], g + 1)
                add_cross(1, s["gg_ps"])
                wait(pe, s["kT_l_ready"], g)
                inner_products(0, bank[6], s["gl_cross_ps"])
                values(g, 0, not has_next, range(1, 2))
                pe.wait_ge(s["gl_cross_out"], g + 1)
                add_cross(0, s["gl_ps"])
                values(g, 0, not has_next, range(2, 3))
                pe.wait_ge(s["sq_parted"], g + 1)
                part_rows(0, sq_parts, s["sq_rows_ps"])
                values(g, 0, not has_next, range(3, KB))
                pe.wait_ge(s["sq_rows_ready"], g + 1)
                along_rows(bank[5], sq_rows, False, s["sq_ps"])
                values(g, 1, not has_next)
                values(g, 2, not has_next, range(0, 1))
                pe.wait_ge(s["rn_parted"], g + 1)
                part_rows(P, rn_parts, s["rn_rows_ps"])
                values(g, 2, not has_next, range(1, 2))
                pe.wait_ge(s["rn_rows_ready"], g + 1)
                along_rows(bank[7], rn_rows, True, s["rm_ps"])
                values(g, 2, not has_next, range(2, KB))
                values(g, 3, not has_next)
                if has_next:
                    turn_h(g + 1, 1 - slot, 0)
                    turn_h(g + 1, 1 - slot, 1)
                pe.wait_ge(s["k_ready"], g + 1)
                for b in range(GB):
                    mm = pe.transpose(bank[6][:, b * P:(b + 1) * P], k_mix[:, b, :], ident[:])
                mm.then_inc(s["kT_ps"], 1)
                if has_next:
                    turn_h(g + 1, 1 - slot, 2)
                    turn_h(g + 1, 1 - slot, 3)
                pe.wait_ge(s["kT_l_ready"], g + 1)
                for b in range(GB):
                    if b == GB - 1 and has_next:
                        pe.wait_ge(s["hT_l_ready"], g * GB + 2 * GB)
                    weighted(g, b)

            pe.wait_ge(s["vo_out"], KB)
            pe.wait_ge(s["adj_l_ready"], 1)
            project_x(0)
            pe.wait_ge(s["need_ready"], 2)
            for t in range(2):
                mm = pe.transpose(bank[6][0:1, t * P:(t + 1) * P], guess[:, 9, t:t + 1], ident[:])
            mm.then_inc(s["most_ready"], 1)
            for i in range(KB):
                pe.wait_ge(s["A_ready"], i + 1)
                for k in range(KB):
                    mm = pe.matmul(bank[7][:, k:k + 1], A[:, i, k * P:(k + 1) * P], ones[:, 0:1],
                                   start=(i == 0 and k == 0), stop=(i == KB - 1 and k == KB - 1),
                                   skip_group_check=True)
            mm.then_inc(s["deg_ps"], 1)
            pe.wait_ge(s["dinv_ready"], 1)
            for k in range(KB):
                mm = pe.transpose(bank[6][:, k * P:(k + 1) * P], dinv_rep[:, k, :], ident[:])
            mm.then_inc(s["dinv_ps"], 1)
            mix_nodes(0)
            pe.wait_ge(s["w_l_ready"], 4)
            for b in range(GB):
                turn_h(0, 0, b)
            body(0, 0, True)
            with pe.Fori(0, NG // 2 - 1) as j:
                for t in (1, 2):
                    body(j * 2 + t, t % 2, True)
            body(NG - 1, (NG - 1) % 2, False)

        @block.scalar
        def _(act):
            def square(c):
                act.wait_ge(x_loaded[c % SLOTS], 16 * (c // SLOTS + 1))
                wait(act, s["ssum_ready"], c - 1)
                act.activation(sq[c % 2], xc[c % SLOTS], ACT.Square).then_inc(s["sq_ready"], 1)

            def root(c):
                act.wait_ge(s["nrm_in"], c + 1)
                act.activation(sqn[:], sqn[:], ACT.Sqrt).then_inc(s["nrm_ready"], 1)

            def repeat(c):
                act.wait_ge(s["rinv_made"], c + 1)
                wait(act, s["spread_ps"], c)
                act.activation(rinv_rep[:].rearrange("p k (b g) -> p (k b) g", b=CB),
                               rinv[:].rearrange("p k b -> p (k b)").unsqueeze(2).broadcast_to([P, KB * CB, LG]),
                               ACT.Copy).then_inc(s["rinv_ready"], 1)

            def high(c):
                act.wait_ge(s["xn_ready"], c + 1)
                act.activation(xn_h[:, c * CL:(c + 1) * CL, :], xc[c % SLOTS], ACT.Copy).then_inc(s["xn_h_ready"], 1)

            square(0)
            square(1)
            root(0)
            repeat(0)
            square(2)
            for c in range(NC):
                if c + 1 < NC:
                    root(c + 1)
                    repeat(c + 1)
                high(c)
                if c + 3 < NC:
                    square(c + 3)

            def s_out(dst, src):
                act.activation(dst, src, ACT.Copy, scale=S_SCALE).then_inc(s["S_ready"], 1)

            def cross_out(r):
                act.wait_ge(s["gram_ps"], r + 1)
                act.wait_ge(s["spread_ps"], NC)
                act.activation(cross[:, r, :], cross_ps[r], ACT.Copy).then_inc(s["cross_out"], 1)

            cross_out(0)
            cross_out(1)
            act.wait_ge(s["xn_l_ready"], NC)
            act.wait_ge(s["gram_full"], 2)
            s_out(S[:, 0, :], bank[0][:])
            s_out(S[:, 1, P:], bank[1][:, 0:NODES - P])
            def deviation(pair):
                act.wait_ge(s["var_ready"], pair + 1)
                act.activation(guess[:, 3, :], guess[:, 3, :], ACT.Sqrt).then_inc(s["deviation_ready"], 1)

            act.wait_ge(s["S_turned"], 3)
            for dst, src in ((S[:, 1, 0:P], bank[7][:, 0:P]), (S[:, 2, 0:2 * P], bank[5][:, 0:2 * P]),
                             (S[:, 3, 0:2 * P], bank[6][:, 0:2 * P])):
                act.activation(dst, src, ACT.Copy).then_inc(s["S_ready"], 1)
            deviation(0)
            act.wait_ge(s["consts_made"], 4)
            for i in range(4):
                act.wait_ge(s[f"w_in{i}"], 16)
                if i:
                    act.wait_ge(s["magn_ready"], i)
                act.activation(squares, w_raw[i], ACT.Square, accum_out=magn[:, i:i + 1]).then_inc(s["magn_ready"], 1)
            act.wait_ge(s["magn_ready"], 4)
            act.activation(squares[:, 0, 0:P], adj_sb[:], ACT.Square,
                           accum_out=magn[:, 4:5]).then_inc(s["magn_ready"], 1)
            act.wait_ge(s["magn_guarded"], 1)
            act.activation(magn_all[:], magn_all[:], ACT.Sqrt).then_inc(s["magn_root"], 1)

            def weight_high(i, nth):
                hi = [wT_h[0], wT_h[1], vo_h[0], vo_h[1]][i]
                act.activation(w_raw[i], w_raw[i], ACT.Copy, scale=up[:, i:i + 1]).then_inc(s["w_scaled"], 1)
                act.wait_ge(s["w_scaled"], nth)
                act.activation(hi, w_raw[i], ACT.Copy).then_inc(s["w_h_ready"], 1)

            act.wait_ge(s["scale_ready"], 2)
            weight_high(2, 1)
            weight_high(3, 2)
            cross_out(2)
            cross_out(3)
            act.wait_ge(s["gram_full"], 3)
            s_out(S[:, 2, 2 * P:], bank[2][:, 0:2 * P])
            act.wait_ge(s["gram_full"], 4)
            s_out(S[:, 3, 3 * P:], bank[3][:, 0:P])
            act.wait_ge(s["S_turned"], 4)
            act.activation(S[:, 3, 2 * P:3 * P], bank[7][:, P:2 * P], ACT.Copy).then_inc(s["S_ready"], 1)
            act.wait_ge(s["S_ready"], 8)
            for i in range(KB // 2, KB):
                act.activation(work[:, i, 0:NODES], S[:, i, :], ACT.Copy).then_inc(s["work_filled"], 1)
            act.activation(adj_sb[:], adj_sb[:], ACT.Copy, scale=up[:, 4:5]).then_inc(s["adj_h_ready"], 1)
            act.wait_ge(s["adj_h_ready"], 1)
            act.activation(adj_h[:], adj_sb[:], ACT.Copy).then_inc(s["adj_h_ready"], 1)
            deviation(1)
            act.wait_ge(s["x_in"], 16)
            act.activation(y, xg, ACT.Copy, scale=up[:, 5:6]).then_inc(s["x_scaled"], 1)
            act.wait_ge(s["x_scaled"], 1)
            act.activation(x_h, y, ACT.Copy).then_inc(s["x_h_ready"], 1)

            def x_high(g):
                act.wait_ge(s["x_in"], g * 16 + 16)
                wait(act, s["xw_ps"], g * GB)
                act.activation(x_h, xg, ACT.Copy, scale=up[:, 5:6]).then_inc(s["x_h_ready"], 1)

            def xw_high(g):
                for b in range(GB):
                    act.wait_ge(s["xw_ps"], g * GB + (b + 1))
                    act.activation(xw_h[:, b, :, :], bank[b][:], ACT.Copy, scale=XW_DOWN).then_inc(s["xw_h_ready"], 1)

            def add_bias(g):
                for b in range(GB):
                    act.wait_ge(s["mix_ps"], g * GB + (b + 1))
                    wait(act, s["h_ready"], g * GB - GB + (b + 1) if not isinstance(g, int) or g > 0 else 0)
                    act.activation(y[:, b, :], bank[b][:], ACT.Identity, scale=c1(ALPHA_C),
                                   bias=bias_c[:]).then_inc(s["mixed"], 1)

            def log_exp(g, t, ready, logged, done):
                act.wait_ge(ready, g + 1)
                act.activation(t[:, 1, :], t[:, 0, :], ACT.Ln).then_inc(logged, 1)
                act.wait_ge(logged, g + 1)
                act.activation(t[:, 2, :], t[:, 1, :], ACT.Exp, scale=-0.5).then_inc(done, 1)

            for d in range(KB):
                act.wait_ge(s["vo_ps"], d + 1)
                act.activation(vo_raw[:, d, :], bank[d][:], ACT.Copy, scale=VO_DOWN).then_inc(s["vo_out"], 1)
            act.wait_ge(s["vo_out"], KB)
            act.activation(vo_squares, vo_raw, ACT.Square, accum_out=vo_magn[:, 0:1]).then_inc(s["vo_magn_ready"], 1)
            xw_high(0)
            act.wait_ge(s["vo_ps"], KB)
            weight_high(0, 3)
            weight_high(1, 4)
            act.wait_ge(s["vo_guarded"], 1)
            act.activation(vo_scale[:, 0:1], vo_magn[:, 1:2], ACT.Sqrt).then_inc(s["vo_root"], 1)
            act.wait_ge(s["deg_in"], 1)
            act.activation(deg_t[:], deg_m[:], ACT.Sqrt).then_inc(s["deg_root"], 1)
            for i in range(KB):
                act.wait_ge(s["an_f"], i + 1)
                act.activation(an_h[:, i, :], A[:, i, :], ACT.Copy).then_inc(s["an_h_ready"], 1)
            act.preload_act_table_set("natural_log_exp_and_others")
            act.wait_ge(s["small_in"], 64)
            act.activation(c1(T0), gate_c[:], ACT.Exp, scale=-1.0).then_inc(s["col_exp"], 1)
            act.activation(c1(T1), ls_c[:], ACT.Exp, scale=-2.0).then_inc(s["col_exp"], 1)
            act.wait_ge(s["d_ready"], 1)
            add_bias(0)
            log_exp(0, ln1, s["ln1_var"], s["ln1_log"], s["ln1_exp"])

            def first_norm(g, slot, items):
                act.wait_ge(s["ln1_ready"], g + 1)
                for b in items:
                    act.activation(h[slot][:, b, :], y[:, b, :], ACT.Identity, scale=ln1[:, 3, b:b + 1],
                                   bias=ln1[:, 4, b:b + 1]).then_inc(s["h_ready"], 1)

            def hT_high(g, b):
                act.wait_ge(s["hT_ps"], g * GB + (b + 1))
                act.activation(hT_h[:, :, b, :], bank[(4, 5, 7, 3)[b]][:].rearrange("p (k n) -> p k n", k=KB),
                               ACT.Copy, scale=H_UP).then_inc(s["hT_h_ready"], 1)

            def body(g, slot, has_next, has_second, has_previous):
                def z_high(i, ps, done, e):
                    act.wait_ge(ps, g * GB + (e + 1))
                    act.activation(z_h[i][:, e, :, :], bank[e][:].rearrange("p (b n) -> p b n", b=GB), ACT.Copy,
                                   scale=Z_DOWN).then_inc(done, 1)

                for e in range(KB):
                    z_high(0, s["zl_ps"], s["zl_h_ready"], e)
                    if e == 1 and has_previous:
                        log_exp(g - 1, ln2, s["ln2_var"], s["ln2_log"], s["ln2_exp"])
                if has_next:
                    xw_high(g + 1)
                for e in range(KB):
                    z_high(1, s["zg_ps"], s["zg_h_ready"], e)
                if has_next:
                    add_bias(g + 1)
                def cross_out(i, ps, cross_bank, done):
                    act.wait_ge(ps, g + 1)
                    act.activation(gram_cross[i], cross_bank[:].rearrange("p (b n) -> p b n", b=GB), ACT.Copy,
                                   scale=CROSS_DOWN).then_inc(done, 1)

                cross_out(1, s["gg_cross_ps"], bank[7], s["gg_cross_out"])
                if has_next:
                    log_exp(g + 1, ln1, s["ln1_var"], s["ln1_log"], s["ln1_exp"])
                cross_out(0, s["gl_cross_ps"], bank[6], s["gl_cross_out"])
                act.wait_ge(s["sq_rows_ps"], g + 1)
                wait(act, s["sq_ps"], g)
                act.activation(sq_rows[:], bank[6][0:GB * PARTS, 0:P], ACT.Copy,
                               scale=-0.5).then_inc(s["sq_rows_ready"], 1)
                log_exp(g, nl, s["nl_in"], s["nl_log"], s["nl_exp"])

                def v_high(b):
                    act.wait_ge(s["v_ps"], g * GB + (b + 1))
                    act.activation(v_h[:, b, :], bank[b][:], ACT.Copy, scale=V_DOWN).then_inc(s["v_h_ready"], 1)

                act.wait_ge(s["sq_ps"], g + 1)
                act.wait_ge(s["hk_ready"], g + 1)
                wait(act, s["graph_steps"], g * 4)
                for b in range(GB):
                    ex = act.activation(e_g[:, b, :], bank[5][:, b * P:(b + 1) * P], ACT.Exp,
                                        scale=c1(KAPPA), bias=cf[:, 0, b:b + 1])
                ex.then_inc(s["e_ready"], 1)
                v_high(0)
                if has_next:
                    first_norm(g + 1, 1 - slot, range(0, 1))
                act.wait_ge(s["rn_rows_ps"], g + 1)
                wait(act, s["rm_ps"], g)
                act.activation(rn_rows[:], bank[6][0:GB * PARTS, P:2 * P], ACT.Copy).then_inc(s["rn_rows_ready"], 1)
                v_high(1)
                if has_next:
                    first_norm(g + 1, 1 - slot, range(1, GB))
                v_high(2)
                v_high(3)
                if has_next:
                    hT_high(g + 1, 0)
                    hT_high(g + 1, 1)
                act.wait_ge(s["kT_ps"], g + 1)
                act.activation(kT_h, bank[6][:].rearrange("p (b n) -> p b n", b=GB), ACT.Copy,
                               scale=K_UP).then_inc(s["kT_h_ready"], 1)
                if has_next:
                    hT_high(g + 1, 2)
                    hT_high(g + 1, 3)
                if has_second:
                    x_high(g + 2)

            first_norm(0, 0, range(GB))
            for b in range(GB):
                hT_high(0, b)
            act.wait_ge(s["vo_up"], 1)
            act.activation(vo_raw, vo_raw, ACT.Copy, scale=vo_scale[:, 3:4]).then_inc(s["vo_scaled"], 1)
            act.wait_ge(s["vo_scaled"], 1)
            act.activation(wT_h[2], vo_raw, ACT.Copy).then_inc(s["w_h_ready"], 1)
            x_high(1)
            body(0, 0, True, True, False)
            with act.Fori(0, NG // 2 - 2) as j:
                for t in (1, 2):
                    body(j * 2 + t, t % 2, True, True, True)
            body(NG - 3, (NG - 3) % 2, True, True, True)
            body(NG - 2, (NG - 2) % 2, True, False, True)
            body(NG - 1, (NG - 1) % 2, False, False, True)
            log_exp(NG - 1, ln2, s["ln2_var"], s["ln2_log"], s["ln2_exp"])

        @block.vector
        def _(dve):
            def sum_squares(c):
                dve.wait_ge(s["sq_ready"], c + 1)
                wait(dve, s["nrm_ps"], c - 1)
                dve.tensor_reduce(ssum[c % 2], sq[c % 2].rearrange("p l n -> p n l"), AX.X,
                                  ALU.add).then_inc(s["ssum_ready"], 1)

            def squared_norms(c):
                dve.wait_ge(s["nrm_ps"], c + 1)
                wait(dve, s["rinv_made"], c)
                dve.tensor_scalar(sqn[:].rearrange("p k b -> p (k b)"), bank[7][:, 0:KB * CB], NORM_EPS * NORM_EPS,
                                  0.0, ALU.max, ALU.max, accum_out=chunk_max[:, c:c + 1]).then_inc(s["nrm_in"], 1)

            def inverse_norms(c):
                dve.wait_ge(s["nrm_ready"], c + 1)
                wait(dve, s["rinv_ready"], c)
                dve.reciprocal(rinv[:], sqn[:]).then_inc(s["rinv_made"], 1)

            def normalise(c):
                dve.wait_ge(s["spread_ps"], c + 1)
                dve.wait_ge(s["sq_ready"], c + 1)
                dve.scalar_tensor_tensor(xc[c % SLOTS], xc[c % SLOTS], X_HAT,
                                         bank[5 + c % 2][:].unsqueeze(1).broadcast_to([P, CL, NODES]),
                                         ALU.mult, ALU.mult).then_inc(s["xn_ready"], 1)

            sum_squares(0)
            squared_norms(0)
            sum_squares(1)
            inverse_norms(0)
            normalise(0)
            squared_norms(1)
            for c in range(1, NC):
                inverse_norms(c)
                if c + 1 < NC:
                    sum_squares(c + 1)
                normalise(c)
                if c + 1 < NC:
                    squared_norms(c + 1)
            dve.wait_ge(s["nrm_in"], NC)
            dve.tensor_reduce(magn[:, 5:6], chunk_max[:], AX.X, ALU.max).then_inc(s["magn_x"], 1)
            dve.wait_ge(s["xn_l_ready"], NC)
            dve.memset(work[:, :, NODES:], PAD).then_inc(s["work_ready"], 1)

            def fill_work(r, done):
                dve.wait_ge(s["S_ready"], done)
                dve.tensor_copy(work[:, r, 0:NODES], S[:, r, :]).then_inc(s["work_ready"], 1)
                dve.wait_ge(s["work_ready"], 1 + 2 * r + 1)
                dve.tensor_tensor(work[:, r, r * P:(r + 1) * P], work[:, r, r * P:(r + 1) * P], self_mark[:],
                                  ALU.add).then_inc(s["work_ready"], 1)

            def x_low(g):
                dve.wait_ge(s["x_h_ready"], g + 1)
                dve.scalar_tensor_tensor(x_l, xg, up[:, 5:6], x_h, ALU.mult,
                                         ALU.subtract).then_inc(s["x_l_ready"], 1)

            def xw_low(g):
                for b in range(GB):
                    dve.wait_ge(s["xw_h_ready"], g * GB + (b + 1))
                    dve.scalar_tensor_tensor(xw_l[:, b, :, :], bank[b][:].rearrange("p (k n) -> p k n", k=KB),
                                             XW_DOWN, xw_h[:, b, :, :], ALU.mult,
                                             ALU.subtract).then_inc(s["xw_l_ready"], 1)

            MEAN, D, VAR, DEV, T, HIGH, COUNT, U, V, NEED, LEFT = range(11)

            def pick(pair, n, between=lambda: None):
                r0 = 2 * pair
                ps = s["pick_steps"]
                w = [work[:, r0 + t, :] for t in range(2)]
                g = lambda i: guess[:, i, :]
                if pair == 0:
                    dve.wait_ge(s["work_ready"], 5)
                else:
                    dve.wait_ge(s["work_23_ready"], 2)
                    dve.wait_ge(s["most_ready"], 1)
                for t in range(2):
                    dve.bn_stats(row_stats[:, t, :], S[:, r0 + t, :]).then_inc(ps, 1)
                n += 2
                dve.wait_ge(ps, n)
                for t in range(2):
                    dve.bn_aggr(row_mv[:, t, :], row_stats[:, t, :]).then_inc(ps, 1)
                n += 2
                dve.wait_ge(ps, n)
                others = NODES - 1.0
                dve.tensor_scalar(g(MEAN), row_mv[:, :, 0], NODES / others, -1.0 / others, ALU.mult,
                                  ALU.add).then_inc(ps, 1)
                dve.tensor_scalar(g(VAR), row_mv[:, :, 1], NODES / others, None, ALU.mult).then_inc(ps, 1)
                n += 2
                dve.wait_ge(ps, n)
                dve.tensor_scalar(g(D), g(MEAN), -1.0, 1.0, ALU.mult, ALU.add).then_inc(ps, 1)
                n += 1
                dve.wait_ge(ps, n)
                dve.tensor_tensor(g(D), g(D), g(D), ALU.mult).then_inc(ps, 1)
                n += 1
                dve.wait_ge(ps, n)
                dve.scalar_tensor_tensor(g(DEV), g(D), -1.0 / NODES, g(VAR), ALU.mult, ALU.add).then_inc(ps, 1)
                n += 1
                dve.wait_ge(ps, n)
                dve.tensor_scalar(g(DEV), g(DEV), 1e-20, None, ALU.max).then_inc(s["var_ready"], 1)
                dve.memset(g(HIGH), ABOVE).then_inc(ps, 1)
                n += 1
                dve.wait_ge(s["deviation_ready"], pair + 1)
                dve.scalar_tensor_tensor(g(T), g(DEV), FIRST_GUESS, g(MEAN), ALU.mult, ALU.add).then_inc(ps, 1)
                n += 1
                for i in range(len(STEPS) + 1):
                    dve.wait_ge(ps, n)
                    for t in range(2):
                        dve.tensor_scalar(tally[:, t, :], w[t][:, 0:NODES], g(T)[:, t:t + 1], 0.0, ALU.is_gt, ALU.add,
                                          accum_out=g(COUNT)[:, t:t + 1]).then_inc(ps, 1)
                    n += 2
                    dve.wait_ge(ps, n)
                    dve.tensor_scalar(g(U), g(COUNT), float(K_NEAR), ABOVE, ALU.is_gt, ALU.mult).then_inc(ps, 1)
                    n += 1
                    if i < len(STEPS):
                        dve.tensor_scalar(g(V), g(COUNT), float(K_NEAR), 2 * STEPS[i], ALU.is_gt,
                                          ALU.mult).then_inc(ps, 1)
                        n += 1
                        dve.wait_ge(ps, n)
                        dve.tensor_tensor(g(U), g(U), g(T), ALU.add).then_inc(ps, 1)
                        dve.scalar_tensor_tensor(g(V), g(V), -STEPS[i], g(DEV), ALU.add, ALU.mult).then_inc(ps, 1)
                        n += 2
                        dve.wait_ge(ps, n)
                        dve.tensor_tensor(g(HIGH), g(HIGH), g(U), ALU.min).then_inc(ps, 1)
                        dve.tensor_tensor(g(T), g(T), g(V), ALU.add).then_inc(ps, 1)
                        n += 2
                    else:
                        dve.wait_ge(ps, n)
                        dve.tensor_tensor(g(U), g(U), g(T), ALU.add).then_inc(ps, 1)
                        n += 1
                        dve.wait_ge(ps, n)
                        dve.tensor_tensor(g(HIGH), g(HIGH), g(U), ALU.min).then_inc(ps, 1)
                        n += 1
                dve.wait_ge(ps, n)
                for t in range(2):
                    dve.tensor_scalar(tally[:, t, :], w[t][:, 0:NODES], g(HIGH)[:, t:t + 1], 0.0, ALU.is_gt, ALU.add,
                                      accum_out=g(COUNT)[:, t:t + 1]).then_inc(ps, 1)
                n += 2
                dve.wait_ge(ps, n)
                dve.tensor_scalar(g(NEED), g(COUNT), -1.0, float(K_NEAR), ALU.mult, ALU.add).then_inc(s["need_ready"], 1)
                for t in range(2):
                    dve.scalar_tensor_tensor(w[t][:, 0:NODES], tally[:, t, :], TAKEN, w[t][:, 0:NODES], ALU.mult,
                                             ALU.add).then_inc(ps, 1)
                n += 2
                dve.wait_ge(s["need_ready"], pair + 1)
                dve.wait_ge(s["rank_made"], 2)
                for t in range(2):
                    dve.tensor_scalar(cut[:, t, :], rank[:], g(NEED)[:, t:t + 1], PAD, ALU.is_ge,
                                      ALU.mult).then_inc(ps, 1)
                n += 2
                dve.tensor_scalar(g(LEFT), g(NEED), -8.0 * ROUNDS, None, ALU.add).then_inc(ps, 1)
                n += 1
                between()
                for i in range(ROUNDS):
                    dve.wait_ge(ps, n)
                    for t in range(2):
                        dve.max(top8[:, t, :], w[t]).then_inc(ps, 1)
                    n += 2
                    dve.wait_ge(ps, n)
                    dve.tensor_tensor(top8[:], top8[:], cut[:, :, 8 * i:8 * (i + 1)], ALU.add).then_inc(ps, 1)
                    dve.memset(work[:, r0:r0 + 2, NODES:], PAD).then_inc(ps, 1)
                    n += 2
                    dve.wait_ge(ps, n)
                    for t in range(2):
                        dve.match_replace(w[t], top8[:, t, :], w[t], TAKEN).then_inc(ps, 1)
                    n += 2
                dve.wait_ge(s["most_ready"], pair + 1)
                needs = most[0:1, :] if pair == 0 else bank[6][0:1, 0:2 * P]
                dve.tensor_reduce(extra_f[0:1, pair:pair + 1], needs, AX.X, ALU.max).then_inc(ps, 1)
                n += 1
                dve.wait_ge(ps, n)
                dve.tensor_scalar(extra_i[0:1, 2 * pair:2 * pair + 1], extra_f[0:1, pair:pair + 1], 7.0 - 8 * ROUNDS, 8.0, ALU.add,
                                  ALU.max).then_inc(ps, 1)
                n += 1
                dve.wait_ge(ps, n)
                dve.tensor_scalar(extra_i[0:1, 2 * pair + 1:2 * pair + 2], extra_i[0:1, 2 * pair:2 * pair + 1], 0xF8, None,
                                  ALU.bitwise_and).then_inc(ps, 1)
                n += 1
                dve.wait_ge(ps, n)
                extra = dve.value_load(extra_i[0:1, 2 * pair + 1:2 * pair + 2], min_val=8, max_val=K_NEAR)
                ms = s[f"more_steps{pair}"]
                dve.memset(cut8[:], 0.0).then_inc(ms, 8)
                with dve.Fori(0, extra, 8) as i:
                    dve.wait_ge(ms, i * 6 + 8)
                    for t in range(2):
                        dve.tensor_scalar(cut8[:, t, :], rank[:, 0:8], g(LEFT)[:, t:t + 1], PAD, ALU.is_ge, ALU.mult)
                    dve.memset(work[:, r0:r0 + 2, NODES:], PAD).then_inc(ms, 8)
                    dve.wait_ge(ms, i * 6 + 16)
                    dve.tensor_scalar(g(LEFT), g(LEFT), -8.0, None, ALU.add).then_inc(ms, 8)
                    dve.max(top8[:, 0, :], w[0])
                    dve.max(top8[:, 1, :], w[1]).then_inc(ms, 8)
                    dve.wait_ge(ms, i * 6 + 32)
                    dve.tensor_tensor(top8[:], top8[:], cut8[:], ALU.add).then_inc(ms, 8)
                    dve.wait_ge(ms, i * 6 + 40)
                    dve.memset(g(U), 0.0)
                    dve.match_replace(w[0], top8[:, 0, :], w[0], TAKEN).then_inc(ms, 8)
                    dve.match_replace(w[1], top8[:, 1, :], w[1], TAKEN).then_inc(ms, 8)
                dve.wait_ge(ms, extra * 6 + 8)
                return n

            def keep(pair, picked):
                for t in range(2):
                    r = 2 * pair + t
                    dve.wait_ge(s["pick_steps"], picked)
                    dve.scalar_tensor_tensor(A[:, r, :], work[:, r, 0:NODES], TAKEN, S[:, r, :],
                                             ALU.is_equal, ALU.mult).then_inc(s["A_ready"], 1)

            dve.wait_ge(s["consts_made"], 4)
            fill_work(0, 2)
            fill_work(1, 3)
            ss = s["scale_steps"]

            def scales():
                dve.wait_ge(s["magn_root"], 1)
                dve.tensor_scalar(pw[:].bitcast(I32), magn_all[:].bitcast(I32), EXPONENT, None,
                                  ALU.bitwise_and).then_inc(ss, 1)
                dve.wait_ge(ss, 1)
                dve.reciprocal(ipw[:], pw[:]).then_inc(ss, 1)
                dve.wait_ge(ss, 2)
                dve.tensor_scalar(up[:, 0:5], ipw[:, 0:5], W_UP, None, ALU.mult).then_inc(s["scale_ready"], 1)
                dve.tensor_scalar(up[:, 5:6], ipw[:, 5:6], X_UP, None, ALU.mult).then_inc(s["scale_ready"], 1)

            picked = pick(0, 0, scales)
            keep(0, picked)
            picked = pick(1, picked)
            keep(1, picked)
            xw_low(0)

            ds_ = s["deg_steps"]
            dve.wait_ge(s["deg_ps"], 1)
            dve.tensor_scalar(deg_m[:], bank[7][:, 0:KB], 1e-34, None, ALU.max).then_inc(s["deg_in"], 1)
            dve.tensor_scalar(dinv[:], bank[7][:, 0:KB], 0.0, None, ALU.is_gt).then_inc(ds_, 1)
            vs = s["vo_steps"]
            dve.wait_ge(s["vo_root"], 1)
            dve.tensor_scalar(vo_scale[:, 1:2].bitcast(I32), vo_scale[:, 0:1].bitcast(I32), EXPONENT, None,
                              ALU.bitwise_and).then_inc(vs, 1)
            dve.wait_ge(vs, 1)
            dve.reciprocal(vo_scale[:, 2:3], vo_scale[:, 1:2]).then_inc(vs, 1)
            dve.wait_ge(vs, 2)
            dve.tensor_scalar(vo_scale[:, 3:4], vo_scale[:, 2:3], W_UP, None, ALU.mult).then_inc(s["vo_up"], 1)
            dve.wait_ge(s["deg_root"], 1)
            dve.reciprocal(deg_t[:], deg_t[:]).then_inc(ds_, 1)
            dve.wait_ge(ds_, 2)
            dve.tensor_tensor(deg_u[:], deg_m[:], deg_t[:], ALU.mult).then_inc(ds_, 1)
            dve.wait_ge(ds_, 3)
            dve.scalar_tensor_tensor(deg_u[:], deg_u[:], -0.5, deg_t[:], ALU.mult, ALU.mult).then_inc(ds_, 1)
            dve.wait_ge(ds_, 4)
            dve.scalar_tensor_tensor(deg_t[:], deg_u[:], 1.5, deg_t[:], ALU.add, ALU.mult).then_inc(ds_, 1)
            dve.wait_ge(ds_, 5)
            dve.tensor_tensor(dinv[:], dinv[:], deg_t[:], ALU.mult).then_inc(ds_, 1)
            dve.wait_ge(ds_, 6)
            dve.tensor_copy(dinv_rep, dinv[:].unsqueeze(2).broadcast_to([P, KB, P])).then_inc(s["dinv_ready"], 1)
            dve.wait_ge(s["dinv_ps"], 1)
            dve.tensor_reduce(c1(D_MAX), bank[6][:], AX.X, ALU.max).then_inc(ds_, 1)
            dve.wait_ge(ds_, 7)
            dve.tensor_scalar(c1(D_MAX), c1(D_MAX), 1e-30, None, ALU.max).then_inc(ds_, 1)
            dve.wait_ge(ds_, 8)
            dve.tensor_scalar(c1(D_POW).bitcast(I32), c1(D_MAX).bitcast(I32), EXPONENT, None,
                              ALU.bitwise_and).then_inc(ds_, 1)
            dve.wait_ge(ds_, 9)
            dve.reciprocal(c1(D_INV), c1(D_POW)).then_inc(ds_, 1)
            dve.wait_ge(ds_, 10)
            dve.tensor_scalar(dinv_col[:], dinv[:], c1(D_INV), A_UP, ALU.mult, ALU.mult).then_inc(ds_, 1)
            dve.wait_ge(ds_, 11)
            dve.tensor_scalar(dinv_col[:], dinv_col[:], c1(D_INV), None, ALU.mult).then_inc(ds_, 1)
            dve.wait_ge(ds_, 12)
            for i in range(KB):
                dve.scalar_tensor_tensor(A[:, i, :], A[:, i, :], dinv_col[:, i:i + 1], bank[6][:], ALU.mult,
                                         ALU.mult).then_inc(s["an_f"], 1)
                if i:
                    dve.wait_ge(s["an_h_ready"], i)
                    dve.tensor_tensor(an_l[:, i - 1, :], A[:, i - 1, :], an_h[:, i - 1, :],
                                      ALU.subtract).then_inc(s["an_l_ready"], 1)
            dve.wait_ge(s["an_h_ready"], KB)
            dve.tensor_tensor(an_l[:, KB - 1, :], A[:, KB - 1, :], an_h[:, KB - 1, :],
                              ALU.subtract).then_inc(s["an_l_ready"], 1)
            cs = s["col_steps"]
            dve.scalar_tensor_tensor(c1(ALPHA_C), c1(D_POW), ALPHA, c1(D_POW), ALU.mult, ALU.mult).then_inc(cs, 1)
            dve.wait_ge(cs, 1)
            dve.scalar_tensor_tensor(c1(ALPHA_C), c1(ALPHA_C), pw[:, 4:5], pw[:, 5:6], ALU.mult,
                                     ALU.mult).then_inc(s["d_ready"], 1)
            dve.tensor_scalar(c1(CAP_C), pw[:, 0:1], Z_UNIT / ROW_EPS, None, ALU.mult).then_inc(cs, 1)
            dve.scalar_tensor_tensor(c1(BETA_C), pw[:, 2:3], BETA, pw[:, 3:4], ALU.mult, ALU.mult).then_inc(cs, 1)
            dve.scalar_tensor_tensor(c1(KAPPA), pw[:, 1:2], Z_UNIT * Z_UNIT, pw[:, 1:2], ALU.mult,
                                     ALU.mult).then_inc(cs, 1)
            dve.wait_ge(cs, 4)
            dve.tensor_tensor(c1(BETA_C), c1(BETA_C), vo_scale[:, 1:2], ALU.mult).then_inc(cs, 1)
            dve.wait_ge(s["col_exp"], 2)
            dve.tensor_tensor(c1(KAPPA), c1(KAPPA), c1(T1), ALU.mult).then_inc(cs, 1)
            dve.tensor_scalar(c1(W_G), c1(T0), 1.0, None, ALU.add).then_inc(cs, 1)
            dve.wait_ge(cs, 7)
            dve.tensor_scalar(c1(HK), c1(KAPPA), -0.5, None, ALU.mult).then_inc(cs, 1)
            dve.reciprocal(c1(W_L), c1(W_G)).then_inc(cs, 1)
            dve.wait_ge(cs, 9)
            dve.tensor_scalar(c1(W_G), c1(W_L), -1.0, 1.0, ALU.mult, ALU.add).then_inc(cs, 1)
            dve.wait_ge(cs, 10)

            def newton(g, t, exped, steps, dst, per):
                dve.wait_ge(exped, g + 1)
                dve.scalar_tensor_tensor(t[:, 3, :], t[:, 0, :], -0.5, t[:, 2, :], ALU.mult, ALU.mult).then_inc(steps, 1)
                dve.wait_ge(steps, g * per + 1)
                dve.tensor_tensor(t[:, 4, :], t[:, 3, :], t[:, 2, :], ALU.mult).then_inc(steps, 1)
                dve.wait_ge(steps, g * per + 2)
                return dve.scalar_tensor_tensor(dst, t[:, 4, :], 1.5, t[:, 2, :], ALU.add, ALU.mult)

            def moments(g, st, m, var, ready, ln):
                dve.wait_ge(s["consts_made"], 4)
                dve.wait_ge(ready, g * GB + GB)
                for b in range(GB):
                    ag = dve.bn_aggr(m[:, b, :], st[:, b, :])
                ag.then_inc(s["stats_ready"] if m is mv else s["stats2_ready"], 1)
                dve.wait_ge(s["stats_ready"] if m is mv else s["stats2_ready"], g + 1)
                dve.tensor_scalar(ln[:, 0, :], m[:, :, 1], LN_EPS, None, ALU.add).then_inc(var, 1)

            def row_stats_1(g):
                for b in range(GB):
                    dve.wait_ge(s["y_ready"], g * GB + (b + 1))
                    dve.bn_stats(stats[:, b, :], y[:, b, :]).then_inc(s["stat1_steps"], 1)
                moments(g, stats, mv, s["ln1_var"], s["stat1_steps"], ln1)

            def first_factors(g):
                newton(g, ln1, s["ln1_exp"], s["ln1_steps"], ln1[:, 3, :], 3).then_inc(s["ln1_steps"], 1)
                dve.wait_ge(s["ln1_steps"], g * 3 + 3)
                dve.scalar_tensor_tensor(ln1[:, 4, :], mv[:, :, 0], -1.0, ln1[:, 3, :], ALU.mult,
                                         ALU.mult).then_inc(s["ln1_ready"], 1)

            def second_norm(g):
                newton(g, ln2, s["ln2_exp"], s["ln2_steps"], ln2[:, 3, :], 3).then_inc(s["ln2_steps"], 1)
                dve.wait_ge(s["ln2_steps"], g * 3 + 3)
                for b in range(GB):
                    dve.tensor_scalar(y2[:, b, :], y2[:, b, :], mv2[:, b, 0:1], ln2[:, 3, b:b + 1], ALU.subtract,
                                      ALU.mult).then_inc(s["o_ready"], 1)

            def second_residual(g, slot, has_previous):
                if has_previous:
                    dve.wait_ge(s["stored"], g * 16)
                for b in range(GB):
                    dve.wait_ge(s["out_ps"], g * GB + (b + 1))
                    dve.scalar_tensor_tensor(y2[:, b, :], bank[b][:], c1(BETA_C), h[slot][:, b, :], ALU.mult,
                                             ALU.add).then_inc(s["y2_ready"], 1)
                    if b:
                        dve.wait_ge(s["y2_ready"], g * GB + b)
                        dve.bn_stats(stats2[:, b - 1, :], y2[:, b - 1, :]).then_inc(s["stat2_steps"], 1)
                dve.wait_ge(s["y2_ready"], g * GB + GB)
                dve.bn_stats(stats2[:, GB - 1, :], y2[:, GB - 1, :]).then_inc(s["stat2_steps"], 1)
                moments(g, stats2, mv2, s["ln2_var"], s["stat2_steps"], ln2)

            def hT_low(g, b):
                dve.wait_ge(s["hT_h_ready"], g * GB + (b + 1))
                dve.scalar_tensor_tensor(hT_l[:, :, b, :], bank[(4, 5, 7, 3)[b]][:].rearrange("p (k n) -> p k n", k=KB),
                                         H_UP, hT_h[:, :, b, :], ALU.mult,
                                         ALU.subtract).then_inc(s["hT_l_ready"], 1)

            def body(g, slot, has_next, has_second, has_previous):
                def z_low(i, hi, done, e):
                    dve.wait_ge(hi, g * GB + (e + 1))
                    dve.scalar_tensor_tensor(z_l[i][:, e, :, :], bank[e][:].rearrange("p (b n) -> p b n", b=GB),
                                             Z_DOWN, z_h[i][:, e, :, :], ALU.mult,
                                             ALU.subtract).then_inc(done, 1)

                for e in range(KB):
                    z_low(0, s["zl_h_ready"], s["zl_l_ready"], e)
                    if e == 1 and has_previous:
                        second_norm(g - 1)
                if has_next:
                    xw_low(g + 1)
                for e in range(KB):
                    z_low(1, s["zg_h_ready"], s["zg_l_ready"], e)
                if has_next:
                    row_stats_1(g + 1)

                gl = bank[4][:].rearrange("p (b n) -> p b n", b=GB)
                gg = bank[5][:].rearrange("p (b n) -> p b n", b=GB)
                gs = s["graph_steps"]
                dve.wait_ge(s["gg_ps"], g + 1)
                dve.tensor_tensor(diag_g, gg, for_items(ident[:]), ALU.mult).then_inc(s["dg_ready"], 1)
                dve.wait_ge(s["dg_ready"], g * 2 + 1)
                dve.tensor_reduce(cf[:, 1, :], diag_g, AX.X, ALU.add).then_inc(s["dg_ready"], 1)
                dve.wait_ge(s["dg_ready"], g * 2 + 2)
                dve.tensor_scalar(cf[:, 0, :], cf[:, 1, :], c1(HK), None, ALU.mult).then_inc(s["hk_ready"], 1)
                if has_next:
                    first_factors(g + 1)
                dve.wait_ge(s["gl_ps"], g + 1)
                dve.tensor_tensor(diag_l, gl, for_items(ident[:]), ALU.mult).then_inc(s["nl_steps"], 1)
                dve.wait_ge(s["nl_steps"], g * 2 + 1)
                dve.tensor_reduce(nl[:, 5, :], diag_l, AX.X, ALU.add).then_inc(s["nl_steps"], 1)
                dve.wait_ge(s["nl_steps"], g * 2 + 2)
                dve.tensor_scalar(nl[:, 0, :], nl[:, 5, :], 1e-18, None, ALU.max).then_inc(s["nl_in"], 1)
                dve.scalar_tensor_tensor(t_l, gl, 0.0, for_items(mask[:]), ALU.max, ALU.mult).then_inc(gs, 1)
                newton(g, nl, s["nl_exp"], s["nl_steps2"], nl[:, 3, :], 3).then_inc(s["nl_steps2"], 1)
                dve.wait_ge(s["nl_steps2"], g * 3 + 3)
                dve.tensor_scalar(nl[:, 5, :], nl[:, 3, :], c1(CAP_C), None, ALU.min).then_inc(s["r_ready"], 1)

                def v_low(b):
                    dve.wait_ge(s["v_h_ready"], g * GB + (b + 1))
                    dve.scalar_tensor_tensor(v_l[:, b, :], bank[b][:], V_DOWN, v_h[:, b, :], ALU.mult,
                                             ALU.subtract).then_inc(s["v_l_ready"], 1)

                fs = s["cf_steps"]
                dve.wait_ge(s["e_ready"], g + 1)
                dve.scalar_tensor_tensor(a_g, e_g, 1.0, for_items(mask[:]), ALU.min, ALU.mult).then_inc(gs, 1)
                v_low(0)
                dve.wait_ge(gs, g * 4 + 2)
                dve.tensor_reduce(cf[:, 6, :], a_g, AX.X, ALU.add).then_inc(gs, 1)
                dve.wait_ge(s["rm_ps"], g + 1)
                dve.tensor_tensor(a_l, t_l, bank[7][:].rearrange("p (b n) -> p b n", b=GB), ALU.mult).then_inc(gs, 1)
                dve.wait_ge(gs, g * 4 + 3)
                dve.tensor_scalar(cf[:, 6, :], cf[:, 6, :], ROW_EPS, None, ALU.max).then_inc(fs, 1)
                dve.wait_ge(gs, g * 4 + 4)
                dve.tensor_reduce(cf[:, 2, :], a_l, AX.X, ALU.add).then_inc(fs, 1)
                dve.wait_ge(fs, g * 6 + 1)
                dve.reciprocal(cf[:, 6, :], cf[:, 6, :]).then_inc(fs, 1)
                dve.wait_ge(fs, g * 6 + 2)
                dve.tensor_tensor(cf[:, 4, :], cf[:, 2, :], nl[:, 5, :], ALU.mult).then_inc(fs, 1)
                dve.wait_ge(fs, g * 6 + 3)
                dve.tensor_scalar(cf[:, 7, :], cf[:, 6, :], c1(W_G), None, ALU.mult).then_inc(s["cf_ready"], 1)
                dve.wait_ge(fs, g * 6 + 4)
                dve.tensor_scalar(cf[:, 4, :], cf[:, 4, :], ROW_EPS, None, ALU.max).then_inc(fs, 1)
                dve.wait_ge(fs, g * 6 + 5)
                dve.reciprocal(cf[:, 5, :], cf[:, 4, :]).then_inc(fs, 1)
                dve.wait_ge(fs, g * 6 + 6)
                dve.scalar_tensor_tensor(cf[:, 3, :], cf[:, 5, :], c1(W_L), nl[:, 5, :], ALU.mult,
                                         ALU.mult).then_inc(s["cl_ready"], 1)
                v_low(1)
                dve.wait_ge(s["cl_ready"], g + 1)
                dve.wait_ge(s["kg_ready"], g + 1)
                for b in range(GB):
                    last = dve.scalar_tensor_tensor(k_mix[:, b, :], a_l[:, b, :], cf[:, 3, b:b + 1], k_g[:, b, :],
                                                    ALU.mult, ALU.add)
                last.then_inc(s["k_ready"], 1)
                v_low(2)
                v_low(3)
                if has_next:
                    hT_low(g + 1, 0)
                dve.wait_ge(s["kT_h_ready"], g + 1)
                dve.scalar_tensor_tensor(kT_l, bank[6][:].rearrange("p (b n) -> p b n", b=GB), K_UP, kT_h, ALU.mult,
                                         ALU.subtract).then_inc(s["kT_l_ready"], 1)
                if has_next:
                    for b in range(1, GB):
                        hT_low(g + 1, b)
                second_residual(g, slot, has_previous)
                if has_second:
                    x_low(g + 2)

            row_stats_1(0)
            first_factors(0)
            for b in range(GB):
                hT_low(0, b)
            x_low(1)
            body(0, 0, True, True, False)
            with dve.Fori(0, NG // 2 - 2) as j:
                for t in (1, 2):
                    body(j * 2 + t, t % 2, True, True, True)
            body(NG - 3, (NG - 3) % 2, True, True, True)
            body(NG - 2, (NG - 2) % 2, True, False, True)
            body(NG - 1, (NG - 1) % 2, False, False, True)
            second_norm(NG - 1)


def kernel(**inputs):
    import numpy as np
    import concourse.bacc as bacc
    from concourse.bass_utils import run_bass_kernel_spmd as run

    f = {n: np.asarray(a) for n, a in inputs.items()}
    arrays = {
        "x": np.ascontiguousarray(f["x"]),
        "adj": np.ascontiguousarray(f["adj"]),
        "bias": np.ascontiguousarray(f["L0_gnn_bias"].reshape(-1, 1)),
        "w_lang_t": np.ascontiguousarray(f["L1_gnn_W_lang"].T),
        "w_grav_t": np.ascontiguousarray(f["L1_gnn_W_grav"].T),
        "w_v": np.ascontiguousarray(f["L1_gnn_W_V"]),
        "w_o_t": np.ascontiguousarray(f["L1_gnn_W_O"].T),
        "gate_logit": np.ascontiguousarray(f["L1_gnn_gate_logit"].reshape(1, 1)),
        "log_sigma": np.ascontiguousarray(f["L1_gnn_log_sigma"].reshape(1, 1)),
    }
    nc = bacc.Bacc("TRN2", target_bir_lowering=False, num_devices=1)
    args = [nc.dram_tensor(f"in_{n}", a.shape, mybir.dt.from_np(a.dtype), kind="ExternalInput").ap()
            for n, a in arrays.items()]
    res = nc.dram_tensor("out_dram", arrays["x"].shape, F32, kind="ExternalOutput").ap()
    build(nc, *args, res)
    r = run(nc, [{f"in_{n}": a for n, a in arrays.items()}], core_ids=[0])
    return r.results[0]["out_dram"]
```
